# Optimizing a Trainium2 kernel written in Bass

```python
import numpy as np
import jax
import jax.numpy as jnp

def _softmax(x, axis=-1):
    return jax.nn.softmax(x, axis=axis)

def _gelu(x):
    return jax.nn.gelu(x, approximate=True)

def _silu(x):
    return jax.nn.silu(x)

def _sigmoid(x):
    return jax.nn.sigmoid(x)

def _layernorm(x, axis=-1, eps=1e-05):
    m = jnp.mean(x, axis=axis, keepdims=True)
    v = jnp.var(x, axis=axis, keepdims=True)
    return (x - m) / jnp.sqrt(v + eps)

def _scatter_add(tgt, idx, src, axis=0):
    return tgt.at[idx].add(src)

def _segment_sum(src, seg, n):
    return jax.ops.segment_sum(src, seg, n)
kernel_name = 'mk_vit_tower_d1_tok_img1024_r4_73d1cf'

def setup_inputs(seed: int=0):
    np.random.seed(seed)
    _w = jnp.asarray

    def _rec_inputs():
        import jax
        import jax.numpy as jnp
        _rk = jax.random.key(seed)
        x = jax.random.uniform(jax.random.fold_in(_rk, 1), (16, 3, 256, 256), jnp.float32, 0.0, 1)
        return x
    x = _rec_inputs()

    def _L0_tok_setup():
        import jax, jax.numpy as jnp
        import numpy as np
        _GRAY_W = (0.2989, 0.587, 0.114)
        key = jax.random.key(seed)
        x = jax.random.uniform(key, (32, 3, 256, 256), dtype=jnp.float32)
        sx = jnp.array([[-3.0, 0.0, 3.0], [-10.0, 0.0, 10.0], [-3.0, 0.0, 3.0]], dtype=jnp.float32)
        scharr = jnp.stack([sx, sx.T])[:, None, :, :]
        return {'x': x, 'scharr': scharr}
    _L0_tok_all = _L0_tok_setup()
    _L0_tok_in = {k: v for k, v in _L0_tok_all.items() if k in ('scharr',)}
    del _L0_tok_all

    def _L0_attn_setup():
        import math
        import jax, jax.numpy as jnp
        import numpy as np
        EPS = 1e-06
        NEG = -1000000000.0

        def rms_norm(x):
            return x * jax.lax.rsqrt(jnp.mean(x * x, axis=-1, keepdims=True) + EPS)

        def apply_rope(x, cos, sin):
            d2 = x.shape[-1] // 2
            x1, x2 = (x[..., :d2], x[..., d2:])
            c = cos[None, None, :, :]
            s = sin[None, None, :, :]
            return jnp.concatenate([x1 * c - x2 * s, x2 * c + x1 * s], axis=-1)
        key = jax.random.key(seed)
        k1, k2, k3 = jax.random.split(key, 3)
        B, T, C = (2, 512, 256)
        H, D = (16, 64)
        dim_inner = H * D
        x = jax.random.normal(k1, (B, T, C), dtype=jnp.float32)
        w_qkv = jax.random.normal(k2, (3 * dim_inner, C), dtype=jnp.float32) * (1.0 / math.sqrt(C))
        w_out = jax.random.normal(k3, (C, dim_inner), dtype=jnp.float32) * (1.0 / math.sqrt(dim_inner))
        return {'x': x, 'w_qkv': w_qkv, 'w_out': w_out}
    _L0_attn_all = _L0_attn_setup()
    _L0_attn_in = {k: v for k, v in _L0_attn_all.items() if k in ('w_qkv', 'w_out')}
    del _L0_attn_all

    def _L0_ffn_setup():
        import jax, jax.numpy as jnp
        import numpy as np
        B, T, C, H, E, MIN_E = (4, 512, 256, 128, 16, 2)
        IS_CAUSAL = False

        def _forward(hidden_states, sim_matrix, gates, q_proj, k_proj, v_proj, o_proj):
            b, t, c = hidden_states.shape
            n = b * t
            x = hidden_states.reshape(n, c)
            xn = x / jnp.maximum(jnp.linalg.norm(x, axis=-1, keepdims=True), 1e-12)
            sn = sim_matrix / jnp.maximum(jnp.linalg.norm(sim_matrix, axis=0, keepdims=True), 1e-12)
            logits = xn @ sn - jax.nn.sigmoid(gates)
            gated = jax.nn.relu(logits)
            hard = (gated > 0).astype(gated.dtype)
            mask = gated + jax.lax.stop_gradient(hard - gated)
            inactive = jnp.sum(hard, axis=1) == 0
            _, fb_idx = jax.lax.top_k(logits, MIN_E)
            fb = jnp.zeros((n, logits.shape[1]), gated.dtype).at[jnp.arange(n)[:, None], fb_idx].set(1.0)
            put = jax.lax.stop_gradient(inactive[:, None].astype(gated.dtype) * fb)
            mask = mask * (1.0 - put) + put
            masked = jnp.where(mask > 0, gated, -jnp.inf)
            w = jax.nn.softmax(masked, axis=-1)

            def moe_proj(p):
                y = jnp.einsum('nc,ech->neh', x, p)
                return jnp.einsum('ne,neh->nh', w, y)
            q = moe_proj(q_proj).reshape(b, t, -1)
            k = moe_proj(k_proj).reshape(b, t, -1)
            v = moe_proj(v_proj).reshape(b, t, -1)
            h = q.shape[-1]
            scores = jnp.einsum('bth,bsh->bts', q, k) / jnp.sqrt(jnp.asarray(h, q.dtype))
            if IS_CAUSAL and t > 1:
                causal = jnp.tril(jnp.ones((t, t), bool))
                scores = jnp.where(causal[None], scores, -jnp.inf)
            attn = jax.nn.softmax(scores, axis=-1)
            o = jnp.einsum('bts,bsh->bth', attn, v).reshape(n, h)
            z = jnp.einsum('ne,nh->enh', w, o)
            out = jnp.einsum('enh,ehc->nc', z, o_proj)
            return out.reshape(b, t, c)
        key = jax.random.key(seed)
        ks = jax.random.split(key, 6)
        lim_qkv = float(np.sqrt(6.0 / (C + H)))
        inp = {'hidden_states': jax.random.normal(ks[0], (B, T, C), jnp.float32), 'sim_matrix': jax.random.normal(ks[1], (C, E), jnp.float32), 'gates': jnp.zeros((E,), jnp.float32), 'q_proj': jax.random.uniform(ks[2], (E, C, H), jnp.float32, -lim_qkv, lim_qkv), 'k_proj': jax.random.uniform(ks[3], (E, C, H), jnp.float32, -lim_qkv, lim_qkv), 'v_proj': jax.random.uniform(ks[4], (E, C, H), jnp.float32, -lim_qkv, lim_qkv), 'o_proj': jax.random.uniform(ks[5], (E, H, C), jnp.float32, -lim_qkv, lim_qkv)}
        return inp
    _L0_ffn_all = _L0_ffn_setup()
    _L0_ffn_in = {k: v for k, v in _L0_ffn_all.items() if k in ('sim_matrix', 'gates', 'q_proj', 'k_proj', 'v_proj', 'o_proj')}
    del _L0_ffn_all
    return {'x': x, 'L0_tok_scharr': _L0_tok_in['scharr'], 'L0_attn_w_qkv': _L0_attn_in['w_qkv'], 'L0_attn_w_out': _L0_attn_in['w_out'], 'L0_ffn_sim_matrix': _L0_ffn_in['sim_matrix'], 'L0_ffn_gates': _L0_ffn_in['gates'], 'L0_ffn_q_proj': _L0_ffn_in['q_proj'], 'L0_ffn_k_proj': _L0_ffn_in['k_proj'], 'L0_ffn_v_proj': _L0_ffn_in['v_proj'], 'L0_ffn_o_proj': _L0_ffn_in['o_proj']}

def reference(x, L0_tok_scharr, L0_attn_w_qkv, L0_attn_w_out, L0_ffn_sim_matrix, L0_ffn_gates, L0_ffn_q_proj, L0_ffn_k_proj, L0_ffn_v_proj, L0_ffn_o_proj):
    import jax
    import jax.numpy as jnp

    def _L0_tok_ref(x, scharr):
        import jax, jax.numpy as jnp
        import numpy as np
        _GRAY_W = (0.2989, 0.587, 0.114)
        w = jnp.asarray(_GRAY_W, dtype=x.dtype)
        gray = jnp.einsum('bchw,c->bhw', x, w)[:, None]
        edges = jax.lax.conv_general_dilated(gray, scharr, window_strides=(1, 1), padding='SAME', dimension_numbers=('NCHW', 'OIHW', 'NCHW'))
        abs_edges = jnp.sqrt(jnp.square(edges))
        edge = abs_edges.sum(axis=1) / 2
        return edge

    def _L0_attn_ref(x, w_qkv, w_out):
        import math
        import jax, jax.numpy as jnp
        import numpy as np
        EPS = 1e-06
        NEG = -1000000000.0

        def rms_norm(x):
            return x * jax.lax.rsqrt(jnp.mean(x * x, axis=-1, keepdims=True) + EPS)

        def apply_rope(x, cos, sin):
            d2 = x.shape[-1] // 2
            x1, x2 = (x[..., :d2], x[..., d2:])
            c = cos[None, None, :, :]
            s = sin[None, None, :, :]
            return jnp.concatenate([x1 * c - x2 * s, x2 * c + x1 * s], axis=-1)
        H, D, window_size = (16, 64, 64)
        B, T, C = x.shape
        xn = rms_norm(x)
        qkv = xn @ w_qkv.T
        q, k, v = jnp.split(qkv, 3, axis=-1)
        q = q.reshape(B, T, H, D).transpose(0, 2, 1, 3)
        k = k.reshape(B, T, H, D).transpose(0, 2, 1, 3)
        v = v.reshape(B, T, H, D).transpose(0, 2, 1, 3)
        inv_freq = 1.0 / 10000.0 ** (jnp.arange(0, D, 2, dtype=jnp.float32) / D)
        freqs = jnp.outer(jnp.arange(T, dtype=jnp.float32), inv_freq)
        cos, sin = (jnp.cos(freqs), jnp.sin(freqs))
        q = apply_rope(q, cos, sin)
        k = apply_rope(k, cos, sin)
        scale = 1.0 / math.sqrt(D)
        attn = jnp.einsum('bhqd,bhkd->bhqk', q, k) * scale
        q_pos = jnp.arange(T)[:, None]
        k_pos = jnp.arange(T)[None, :]
        mask = (q_pos >= k_pos) & (q_pos - k_pos <= window_size)
        attn = jnp.where(mask[None, None], attn, NEG)
        attn = jax.nn.softmax(attn.astype(jnp.float32), axis=-1).astype(q.dtype)
        out = jnp.einsum('bhqk,bhkd->bhqd', attn, v)
        out = out.transpose(0, 2, 1, 3).reshape(B, T, H * D)
        return out @ w_out.T

    def _L0_ffn_ref(hidden_states, sim_matrix, gates, q_proj, k_proj, v_proj, o_proj):
        import jax, jax.numpy as jnp
        import numpy as np
        B, T, C, H, E, MIN_E = (4, 512, 256, 128, 16, 2)
        IS_CAUSAL = False

        def _forward(hidden_states, sim_matrix, gates, q_proj, k_proj, v_proj, o_proj):
            b, t, c = hidden_states.shape
            n = b * t
            x = hidden_states.reshape(n, c)
            xn = x / jnp.maximum(jnp.linalg.norm(x, axis=-1, keepdims=True), 1e-12)
            sn = sim_matrix / jnp.maximum(jnp.linalg.norm(sim_matrix, axis=0, keepdims=True), 1e-12)
            logits = xn @ sn - jax.nn.sigmoid(gates)
            gated = jax.nn.relu(logits)
            hard = (gated > 0).astype(gated.dtype)
            mask = gated + jax.lax.stop_gradient(hard - gated)
            inactive = jnp.sum(hard, axis=1) == 0
            _, fb_idx = jax.lax.top_k(logits, MIN_E)
            fb = jnp.zeros((n, logits.shape[1]), gated.dtype).at[jnp.arange(n)[:, None], fb_idx].set(1.0)
            put = jax.lax.stop_gradient(inactive[:, None].astype(gated.dtype) * fb)
            mask = mask * (1.0 - put) + put
            masked = jnp.where(mask > 0, gated, -jnp.inf)
            w = jax.nn.softmax(masked, axis=-1)

            def moe_proj(p):
                y = jnp.einsum('nc,ech->neh', x, p)
                return jnp.einsum('ne,neh->nh', w, y)
            q = moe_proj(q_proj).reshape(b, t, -1)
            k = moe_proj(k_proj).reshape(b, t, -1)
            v = moe_proj(v_proj).reshape(b, t, -1)
            h = q.shape[-1]
            scores = jnp.einsum('bth,bsh->bts', q, k) / jnp.sqrt(jnp.asarray(h, q.dtype))
            if IS_CAUSAL and t > 1:
                causal = jnp.tril(jnp.ones((t, t), bool))
                scores = jnp.where(causal[None], scores, -jnp.inf)
            attn = jax.nn.softmax(scores, axis=-1)
            o = jnp.einsum('bts,bsh->bth', attn, v).reshape(n, h)
            z = jnp.einsum('ne,nh->enh', w, o)
            out = jnp.einsum('enh,ehc->nc', z, o_proj)
            return out.reshape(b, t, c)
        return _forward(hidden_states, sim_matrix, gates, q_proj, k_proj, v_proj, o_proj)
    h = _L0_tok_ref(x, L0_tok_scharr)
    h = h + _L0_attn_ref(_layernorm(h, axis=-1), L0_attn_w_qkv, L0_attn_w_out)
    h = h + _L0_ffn_ref(_layernorm(h, axis=-1), L0_ffn_sim_matrix, L0_ffn_gates, L0_ffn_q_proj, L0_ffn_k_proj, L0_ffn_v_proj, L0_ffn_o_proj)
    return h

_drawn_inputs = setup_inputs


def setup_inputs(seed=0):
    import zlib

    import numpy as np

    out = dict(_drawn_inputs(seed))
    spreads = {'L0_ffn_gates': (0.0, 0.399)}
    factors = {'L0_ffn_q_proj': 6.684, 'L0_ffn_k_proj': 6.697}
    for name, (base, spread) in spreads.items():
        noise = np.random.default_rng([zlib.crc32(name.encode()), seed]).standard_normal(out[name].shape)
        drawn = base * np.exp(spread * noise) if base else spread * noise
        out[name] = jnp.asarray(drawn.astype(out[name].dtype))
    for name, factor in factors.items():
        out[name] = (out[name] * factor).astype(out[name].dtype)
    return out
```

```python
from contextlib import ExitStack

import numpy as np

import concourse.bass as bass
from concourse import mybir

F32 = mybir.dt.float32
F32R = mybir.dt.float32r
U32 = mybir.dt.uint32
ALU = mybir.AluOpType
ACT = mybir.ActivationFunctionType
AX_X = mybir.AxisListType.X

P = 128
IMAGES, CHANNELS, ROWS, COLS = 16, 3, 256, 256
TT = ROWS // P
CT = COLS // P
HEADS, HEAD_DIM, WINDOW = 16, 64, 64
HALF = HEAD_DIM // 2
PAIRS = HEADS // 2
GROUPS = HEADS // 4
BLOCKS = ROWS // WINDOW
KEYS = 2 * WINDOW
GROUP_COLS = 3 * 4 * HEAD_DIM
MOVES = 8
GRAY = (0.2989, 0.587, 0.114)
LN_EPS, RMS_EPS = 1e-5, 1e-6
MASKED = -1e9
EXCLUDED = 1e29
EXPERTS, EXPERT_DIM = 16, 128
EXPERT_COLS = 3 * EXPERT_DIM
SCORE_SCALE = float(EXPERT_DIM) ** -0.5


def positive(eng, sem, count):
    if isinstance(count, int) and count <= 0:
        return
    eng.wait_ge(sem, count)


def shape_constants():
    freq = 1.0 / np.float32(10000.0) ** (np.arange(0, HEAD_DIM, 2, dtype=np.float32) / np.float32(HEAD_DIM))
    angle = np.outer(np.arange(ROWS, dtype=np.float32), freq.astype(np.float32)).astype(np.float32)
    cos, sin = np.cos(angle).T, np.sin(angle).T
    cos, sin = np.tile(cos, (4, 1)), np.tile(sin, (4, 1))
    rope_k = np.stack([cos, -sin, sin], 1).astype(np.float32)
    rope_q = (rope_k * np.float32(HEAD_DIM ** -0.5)).astype(np.float32)
    mask = np.full((P, BLOCKS, KEYS), MASKED, np.float32)
    for b in range(BLOCKS):
        for c in range(KEYS):
            key = key_of(b, c)
            for r in range(WINDOW):
                q = WINDOW * b + r
                if q >= key and q - key <= WINDOW:
                    mask[r, b, c] = mask[WINDOW + r, b, c] = 0.0
    row = np.zeros((P, 3, P), np.float32)
    for dy in range(3):
        for m in range(P):
            k = m + dy - 1
            if 0 <= k < P:
                row[k, dy, m] = 1.0
    edge = np.zeros((6, P), np.float32)
    edge[0:3, P - 1] = 1.0
    edge[3:6, 0] = 1.0
    return {"rope": np.stack([rope_q, rope_k], 1).reshape(P, 2, 3, ROWS), "mask": mask, "row": row,
            "edge": edge, "identity": np.eye(P, dtype=np.float32),
            "numbers": np.tile(np.arange(EXPERTS, dtype=np.float32), (P, 1))}


def key_of(block, column):
    if block == 0:
        return column
    if block % 2:
        return WINDOW * (block - 1) + column
    return WINDOW * block + column if column < WINDOW else WINDOW * (block - 1) + column - WINDOW


def reversed_halves(ap):
    (part, (step, two), inner) = ap.ap
    return bass.AP(tensor=ap.tensor, offset=ap.offset + step, ap=[list(part), [-step, two], list(inner)])


def build(nc, x, scharr, scharr_last, w_qkv, w_out, sim, gates, w_moe, w_moe_out, rope, mask, row, edge, identity, numbers, out,
          stop_after_a=False):
    with ExitStack() as ctx:
        def sem(name):
            return ctx.enter_context(nc.semaphore(name))

        def sb(name, shape, dt=F32, scope=ctx):
            return scope.enter_context(nc.sbuf_tensor(name, shape, dt))

        bank = [ctx.enter_context(nc.psum_tensor(f"bank{i}", [P, 512], F32)) for i in range(8)]

        h_all = sb("h_all", [P, IMAGES * TT, COLS])
        ident = sb("ident", [P, P])
        minus_half = sb("minus_half", [P, TT])
        carrier = sb("carrier", [P, 1])

        a_scope = ctx.enter_context(ExitStack())
        a = lambda name, shape, dt=F32: sb(name, shape, dt, a_scope)
        w_hi = a("w_hi", [P, CT, GROUPS, GROUP_COLS], F32R)
        w_lo = a("w_lo", [P, CT, GROUPS, GROUP_COLS], F32R)
        wo_hi = a("wo_hi", [P, PAIRS, COLS], F32R)
        wo_lo = a("wo_lo", [P, PAIRS, COLS], F32R)
        rope_t = a("rope_t", [P, 2, 3, ROWS])
        mask_t = a("mask_t", [P, BLOCKS, KEYS])
        row_t = a("row_t", [P, 3, P])
        edge_t = a("edge_t", [6, P])
        taps = a("taps", [P, 2, 3, 3])
        edge_taps = a("edge_taps", [6, 2])
        band = a("band", [P, 2, 3, P])
        edge_band = a("edge_band", [6, 2, P])
        x_in = a("x_in", [P, CHANNELS, TT, COLS])
        gray = a("gray", [P, TT, COLS + 2])
        halo = a("halo", [6, TT, COLS])
        abs_e = a("abs_e", [P, 2, TT, COLS])
        stats = a("stats", [P, TT, 6])
        moments = a("moments", [P, TT, 2])
        spread = a("spread", [P, TT])
        rstd = a("rstd", [P, TT])
        xn = a("xn", [P, TT, COLS])
        x_hi = a("x_hi", [P, CT, ROWS], F32R)
        x_lo = a("x_lo", [P, CT, ROWS], F32R)
        own_part = a("own_part", [P, 2, 2, ROWS])
        other_part = a("other_part", [P, 2, 2, ROWS])
        rotated = a("rotated", [P, 2, 2, 2, ROWS])
        qk = a("qk", [P, PAIRS, 2, ROWS])
        v = a("v", [P, GROUPS, TT, 4 * HEAD_DIM])
        v_cross = a("v_cross", [P, GROUPS, 4 * HEAD_DIM])
        masked = a("masked", [P, 2, BLOCKS, KEYS])
        neg_max = a("neg_max", [P, 2, BLOCKS])
        prob = a("prob", [P, 2, BLOCKS, KEYS])
        total = a("total", [P, 2, BLOCKS])
        inv_total = a("inv_total", [P, 2, BLOCKS])
        prob_t = a("prob_t", [P, 2, BLOCKS, P])
        o_hi = a("o_hi", [P, 2, ROWS], F32R)
        o_lo = a("o_lo", [P, 2, ROWS], F32R)

        scores_bank = bank[0:2]
        q_bank, k_bank = bank[2], bank[3]
        v_bank, o_bank, out_bank, misc_bank = bank[4], bank[5], bank[6], bank[7]

        const_loaded = sem("const_loaded")
        minus_half_set = sem("minus_half_set")
        borders_zero = sem("borders_zero")
        band_part = sem("band_part")
        band_ready = sem("band_ready")
        raw_loaded = [sem(f"raw_loaded{i}") for i in range(2)]
        w_hi_ready = sem("w_hi_ready")
        w_lo_ready = sem("w_lo_ready")
        x_loaded = sem("x_loaded")
        gray_first = sem("gray_first")
        gray_second = sem("gray_second")
        gray_done = sem("gray_done")
        halo_loaded = sem("halo_loaded")
        conv_done = sem("conv_done")
        abs_done = sem("abs_done")
        h_done = sem("h_done")
        stats_done = sem("stats_done")
        moments_done = sem("moments_done")
        spread_done = sem("spread_done")
        rstd_done = sem("rstd_done")
        xn_done = sem("xn_done")
        xt_done = sem("xt_done")
        x_hi_done = sem("x_hi_done")
        x_lo_done = sem("x_lo_done")
        qk_done = sem("qk_done")
        rope_mul = sem("rope_mul")
        rope_add = sem("rope_add")
        moved = [sem(f"moved{g}") for g in range(GROUPS)]
        v_done = sem("v_done")
        v_evac = sem("v_evac")
        v_crossed = [sem(f"v_crossed{g}") for g in range(GROUPS)]
        s_done = sem("s_done")
        masked_done = sem("masked_done")
        max_done = sem("max_done")
        exp_done = sem("exp_done")
        recip_done = sem("recip_done")
        norm_done = sem("norm_done")
        t_done = sem("t_done")
        pt_evac = sem("pt_evac")
        o_done = sem("o_done")
        o_hi_done = sem("o_hi_done")
        o_lo_done = sem("o_lo_done")
        out_done = sem("out_done")
        resid_done = sem("resid_done")
        stored = sem("stored")

        CONSTS = 8

        CHUNKS = CT * GROUPS + PAIRS // 2
        raw_slot = [rotated[:, i, :, :, :].rearrange("p a b c -> p (a b c)") for i in range(2)]

        def raw_chunk(n):
            slot = raw_slot[n % 2]
            if n < CT * GROUPS:
                g, ct = n // CT, n % CT
                return (w_qkv[ct * P:(ct + 1) * P, g, :], slot[:, 0:GROUP_COLS], w_hi[:, ct, g, :], w_lo[:, ct, g, :])
            pair = 2 * (n - CT * GROUPS)
            return (w_out[pair * P:(pair + 2) * P, :].rearrange("(a p) c -> p a c", p=P),
                    slot[:, 0:2 * COLS].rearrange("p (a c) -> p a c", a=2),
                    wo_hi[:, pair:pair + 2, :], wo_lo[:, pair:pair + 2, :])

        def tiles(image):
            return bass.ds(image * TT, TT)

        def bodies(eng, body):
            body(0, True, True)
            with eng.Fori(1, IMAGES - 2) as n:
                body(n, True, True)
            body(IMAGES - 2, True, False)
            body(IMAGES - 1, False, False)

        block = ctx.enter_context(nc.Block())

        @block.sync
        def _(sp):
            def load_halo(f):
                sp.wait_ge(gray_done, f + 1)
                positive(sp, conv_done, 2 * f)
                for k, (p, t) in enumerate(((0, 1), (P - 1, 0))):
                    src = gray[p:p + 1, t, 0:COLS]
                    shifted = bass.AP(tensor=src.tensor, offset=src.offset, ap=[list(src.ap[0]), [1, 3], [1, COLS]])
                    sp.dma_start(halo[3 * k:3 * k + 3, k, :], shifted).then_inc(halo_loaded, 16)

            def move_rotated(m, g):
                sp.wait_ge(rope_add, 2 * (GROUPS * m + g) + 2)
                for j in range(4):
                    for half in range(2):
                        to = HEAD_DIM * (j % 2) + HALF * half
                        sp.dma_start(qk[to:to + HALF, 2 * g + j // 2, :, :],
                                     rotated[HALF * j:HALF * (j + 1), g % 2, :, half, :]).then_inc(moved[g], 16)

            def move_values(m, g):
                sp.wait_ge(v_evac, GROUPS * m + g + 1)
                sp.dma_start(v_cross[0:WINDOW, g, :], v[0:WINDOW, g, 1, :]).then_inc(v_crossed[g], 16)
                sp.dma_start(v_cross[WINDOW:P, g, :], v[WINDOW:P, g, 0, :]).then_inc(v_crossed[g], 16)

            sp.dma_start(x_in[:, :, :, :], x[0].rearrange("c (t p) w -> p c t w", p=P)).then_inc(x_loaded, 16)
            sp.dma_start(taps[:, :, :, :].rearrange("p a b c -> p (a b c)"),
                         scharr.rearrange("a o b c -> (a o b c)").partition_broadcast(P)).then_inc(const_loaded, 16)
            sp.dma_start(row_t[:, :, :], row).then_inc(const_loaded, 16)
            sp.dma_start(edge_t[:, :], edge).then_inc(const_loaded, 16)
            for k, dy in enumerate((2, 0)):
                sp.dma_start(edge_taps[3 * k:3 * k + 3, :],
                             scharr_last[dy, :, :]).then_inc(const_loaded, 16)
            sp.dma_start(ident[:, :], identity).then_inc(const_loaded, 16)
            sp.dma_start(rope_t[:, :, :, :], rope).then_inc(const_loaded, 16)
            sp.dma_start(mask_t[:, :, :], mask).then_inc(const_loaded, 16)
            for n in range(CHUNKS):
                if n >= 2:
                    sp.wait_ge(w_hi_ready, n - 1)
                    sp.wait_ge(w_lo_ready, n - 1)
                src, slot, _, _ = raw_chunk(n)
                sp.dma_start(slot, src).then_inc(raw_loaded[n % 2], 16)
                if n == 3:
                    load_halo(0)
            for g in range(GROUPS):
                move_rotated(0, g)
                move_values(0, g)
            load_halo(1)

            def body(n, project, edges):
                for g in range(GROUPS):
                    if edges and g == 2:
                        load_halo(n + 2)
                    if project:
                        move_rotated(n + 1, g)
                        move_values(n + 1, g)
            bodies(sp, body)
            if stop_after_a:
                sp.wait_ge(resid_done, IMAGES)
                sp.dma_start(out.rearrange("b (t p) c -> p (b t) c", p=P), h_all[:, :, :]).then_inc(stored, 16)
                sp.wait_ge(stored, 16)

        @block.gpsimd
        def _(pool):
            nc.gpsimd.memset(minus_half[:, :], -0.5).then_inc(minus_half_set, 1)
            pool.wait_ge(minus_half_set, 1)

            def add_edges(f):
                pool.wait_ge(abs_done, 2 * f + 2)
                nc.gpsimd.tensor_tensor(h_all[:, tiles(f), :], abs_e[:, 0, :, :], abs_e[:, 1, :, :],
                                        ALU.add).then_inc(h_done, 1)

            def inverse_root(f):
                pool.wait_ge(spread_done, f + 1)
                nc.gpsimd.tensor_tensor(rstd[:, :], spread[:, :], minus_half[:, :], ALU.pow).then_inc(rstd_done, 1)

            def rotate(m, g, which):
                pool.wait_ge(rope_mul, 2 * (GROUPS * m + g) + which + 1)
                if which == 0:
                    if g >= 2:
                        pool.wait_ge(moved[g - 2], 16 * MOVES * (m + 1))
                    else:
                        positive(pool, moved[g + 2], 16 * MOVES * m)
                nc.gpsimd.tensor_tensor(rotated[:, g % 2, which, :, :], own_part[:, which, :, :],
                                        other_part[:, which, :, :], ALU.add).then_inc(rope_add, 1)

            def normalise(n, p):
                pool.wait_ge(recip_done, PAIRS * n + p + 1)
                nc.gpsimd.tensor_tensor(prob[:, p % 2, :, :], prob[:, p % 2, :, :],
                                        inv_total[:, p % 2, :].unsqueeze(2).to_broadcast([P, BLOCKS, KEYS]),
                                        ALU.mult).then_inc(norm_done, 1)

            add_edges(0)
            inverse_root(0)
            pool.wait_ge(w_hi_ready, CHUNKS)
            pool.wait_ge(w_lo_ready, CHUNKS)
            for g in range(GROUPS):
                rotate(0, g, 0)
                rotate(0, g, 1)
            add_edges(1)
            inverse_root(1)

            def body(n, project, edges):
                for g in range(GROUPS):
                    normalise(n, 2 * g)
                    if project:
                        rotate(n + 1, g, 0)
                    normalise(n, 2 * g + 1)
                    if project:
                        rotate(n + 1, g, 1)
                    if edges and g == 2:
                        add_edges(n + 2)
                    if edges and g == 3:
                        inverse_root(n + 2)
            bodies(pool, body)

        @block.scalar
        def _(act):
            def load_image(f):
                positive(act, gray_done, f)
                act.dma_start(x_in[:, :, :, :], x[f].rearrange("c (t p) w -> p c t w", p=P)).then_inc(x_loaded, 16)

            def gray_red(f):
                act.wait_ge(x_loaded, 16 * (f + 1))
                positive(act, conv_done, 2 * f)
                positive(act, halo_loaded, 32 * f)
                nc.scalar.activation(gray[:, :, 1:COLS + 1], x_in[:, 0, :, :], ACT.Copy,
                                     scale=GRAY[0]).then_inc(gray_first, 1)

            def edge_size(f, which):
                act.wait_ge(conv_done, 2 * f + which + 1)
                if which == 0:
                    positive(act, h_done, f)
                src = (misc_bank, v_bank)[which]
                nc.scalar.activation(abs_e[:, which, :, :], src[:, :].rearrange("p (t c) -> p t c", t=TT),
                                     ACT.Abs, scale=0.5).then_inc(abs_done, 1)

            def split_x(f):
                act.wait_ge(xt_done, f + 1)
                positive(act, v_done, GROUPS * f)
                nc.scalar.activation(x_hi[:, :, :], misc_bank[:, :].rearrange("p (t c) -> p t c", t=CT),
                                     ACT.Copy).then_inc(x_hi_done, 1)

            def values(m, g):
                act.wait_ge(v_done, GROUPS * m + g + 1)
                positive(act, o_done, GROUPS * (m - 1) + g + 1)
                nc.scalar.activation(v[:, g, :, :], v_bank[:, :].rearrange("p (t c) -> p t c", t=TT),
                                     ACT.Copy).then_inc(v_evac, 1)

            def exponent(n, p):
                act.wait_ge(max_done, PAIRS * n + p + 1)
                positive(act, t_done, PAIRS * n + p - 1)
                for b in range(BLOCKS):
                    last = nc.scalar.activation(prob[:, p % 2, b, :], masked[:, p % 2, b, :], ACT.Exp,
                                                bias=neg_max[:, p % 2, b:b + 1],
                                                accum_out=total[:, p % 2, b:b + 1])
                last.then_inc(exp_done, 1)

            def transposed(n, p):
                act.wait_ge(t_done, PAIRS * n + p + 1)
                positive(act, o_done, GROUPS * n + p // 2)
                nc.scalar.activation(prob_t[:, p % 2, :, :],
                                     scores_bank[p % 2][:, :].rearrange("p (b c) -> p b c", b=BLOCKS),
                                     ACT.Copy).then_inc(pt_evac, 1)

            def split_o(n, g):
                act.wait_ge(o_done, GROUPS * n + g + 1)
                nc.scalar.activation(o_hi[:, :, :], o_bank[:, :].rearrange("p (a c) -> p a c", a=2),
                                     ACT.Copy).then_inc(o_hi_done, 1)

            gray_red(0)
            load_image(1)
            for n in range(CHUNKS):
                act.wait_ge(raw_loaded[n % 2], 16 * (n // 2 + 1))
                _, slot, hi, _ = raw_chunk(n)
                nc.scalar.activation(hi, slot, ACT.Copy).then_inc(w_hi_ready, 1)
                if n == 7:
                    edge_size(0, 0)
                    edge_size(0, 1)
            split_x(0)
            gray_red(1)
            for g in range(GROUPS):
                values(0, g)
            edge_size(1, 0)
            edge_size(1, 1)
            split_x(1)

            def body(n, project, edges):
                if edges:
                    load_image(n + 2)
                for g in range(GROUPS):
                    exponent(n, 2 * g)
                    exponent(n, 2 * g + 1)
                    if edges and g == 1:
                        gray_red(n + 2)
                    if edges and g == 2:
                        edge_size(n + 2, 0)
                        edge_size(n + 2, 1)
                    transposed(n, 2 * g)
                    transposed(n, 2 * g + 1)
                    if project:
                        values(n + 1, g)
                    split_o(n, g)
                if edges:
                    split_x(n + 2)
            bodies(act, body)

        @block.vector
        def _(dve):
            def gray_rest(f):
                dve.wait_ge(gray_first, f + 1)
                nc.vector.scalar_tensor_tensor(out=gray[:, :, 1:COLS + 1], in0=x_in[:, 1, :, :], scalar=GRAY[1],
                                               in1=gray[:, :, 1:COLS + 1], op0=ALU.mult,
                                               op1=ALU.add).then_inc(gray_second, 1)
                dve.wait_ge(gray_second, f + 1)
                nc.vector.scalar_tensor_tensor(out=gray[:, :, 1:COLS + 1], in0=x_in[:, 2, :, :], scalar=GRAY[2],
                                               in1=gray[:, :, 1:COLS + 1], op0=ALU.mult,
                                               op1=ALU.add).then_inc(gray_done, 1)

            def layer_stats(f):
                dve.wait_ge(h_done, f + 1)
                for t in range(TT):
                    last = nc.vector.bn_stats(stats[:, t, :], h_all[:, bass.ds(f * TT + t, 1), :])
                last.then_inc(stats_done, 1)
                dve.wait_ge(stats_done, f + 1)
                nc.vector.memset(carrier[:, :], 0.0)
                for t in range(TT):
                    last = nc.vector.bn_aggr(moments[:, t, :], stats[:, t, :])
                last.then_inc(moments_done, 1)
                dve.wait_ge(moments_done, f + 1)
                nc.vector.tensor_scalar(spread[:, :], moments[:, :, 1], 1.0 + RMS_EPS, LN_EPS * RMS_EPS,
                                        ALU.mult, ALU.add).then_inc(spread_done, 1)

            def layer_norm(f):
                dve.wait_ge(rstd_done, f + 1)
                positive(dve, xt_done, f)
                for t in range(TT):
                    last = nc.vector.tensor_scalar(xn[:, t:t + 1, :], h_all[:, bass.ds(f * TT + t, 1), :],
                                                   moments[:, t, 0:1], rstd[:, t:t + 1],
                                                   ALU.subtract, ALU.mult)
                last.then_inc(xn_done, 1)

            def split_x(f):
                dve.wait_ge(x_hi_done, f + 1)
                nc.vector.tensor_tensor(x_lo[:, :, :], misc_bank[:, :].rearrange("p (t c) -> p t c", t=CT),
                                        x_hi[:, :, :].bitcast(F32), ALU.subtract).then_inc(x_lo_done, 1)

            def rotate(m, g, which):
                src = (q_bank, k_bank)[which][:, :].rearrange("p (a c) -> p a c", a=2)
                done = 2 * (GROUPS * m + g) + which
                dve.wait_ge(qk_done, done + 1)
                positive(dve, rope_add, done - 1)
                nc.vector.tensor_tensor(own_part[:, which, :, :], src,
                                        rope_t[:, which, 0:1, :].to_broadcast([P, 2, ROWS]), ALU.mult)
                nc.vector.tensor_tensor(other_part[:, which, :, :], reversed_halves(src),
                                        rope_t[:, which, 1:3, :], ALU.mult).then_inc(rope_mul, 1)

            def row_max(n, p):
                done = PAIRS * n + p
                dve.wait_ge(s_done, done + 1)
                positive(dve, exp_done, done - 1)
                nc.vector.tensor_tensor(masked[:, p % 2, :, :],
                                        scores_bank[p % 2][:, :].rearrange("p (b c) -> p b c", b=BLOCKS),
                                        mask_t[:, :, :], ALU.add).then_inc(masked_done, 1)
                dve.wait_ge(masked_done, done + 1)
                nc.vector.tensor_reduce(neg_max[:, p % 2, :], masked[:, p % 2, :, :], AX_X, ALU.max,
                                        negate=True).then_inc(max_done, 1)

            def inverse_total(n, p):
                dve.wait_ge(exp_done, PAIRS * n + p + 1)
                positive(dve, norm_done, PAIRS * n + p - 1)
                nc.vector.reciprocal(inv_total[:, p % 2, :], total[:, p % 2, :]).then_inc(recip_done, 1)

            def split_o(n, g):
                dve.wait_ge(o_hi_done, GROUPS * n + g + 1)
                nc.vector.tensor_tensor(o_lo[:, :, :], o_bank[:, :].rearrange("p (a c) -> p a c", a=2),
                                        o_hi[:, :, :].bitcast(F32), ALU.subtract).then_inc(o_lo_done, 1)

            def residual(n):
                dve.wait_ge(out_done, n + 1)
                nc.vector.tensor_tensor(h_all[:, tiles(n), :], out_bank[:, :].rearrange("p (t c) -> p t c", t=TT),
                                        h_all[:, tiles(n), :], ALU.add).then_inc(resid_done, 1)

            nc.vector.memset(gray[:, :, 0:1], 0.0)
            nc.vector.memset(gray[:, :, COLS + 1:COLS + 2], 0.0)
            nc.vector.memset(halo[:, :, :], 0.0).then_inc(borders_zero, 1)
            gray_rest(0)
            dve.wait_ge(const_loaded, 16 * CONSTS)
            for f in range(2):
                nc.vector.tensor_scalar(edge_band[:, f, :], edge_t[:, :], edge_taps[:, f:f + 1], None, ALU.mult)
            for dy in range(3):
                if dy:
                    dve.wait_ge(band_part, dy)
                for f in range(2):
                    for dx in range(3):
                        tap = taps[:, f, dy, dx:dx + 1]
                        if dy == 0:
                            last = nc.vector.tensor_scalar(band[:, f, dx, :], row_t[:, 0, :], tap, None, ALU.mult)
                        else:
                            last = nc.vector.scalar_tensor_tensor(
                                out=band[:, f, dx, :], in0=row_t[:, dy, :], scalar=tap, in1=band[:, f, dx, :],
                                op0=ALU.mult, op1=ALU.add)
                last.then_inc(band_part if dy < 2 else band_ready, 1)
            for n in range(CHUNKS):
                dve.wait_ge(w_hi_ready, n + 1)
                _, slot, hi, lo = raw_chunk(n)
                nc.vector.tensor_tensor(lo, slot, hi.bitcast(F32), ALU.subtract).then_inc(w_lo_ready, 1)
                if n == CHUNKS - 3:
                    layer_stats(0)
            layer_norm(0)
            split_x(0)
            gray_rest(1)
            for g in range(GROUPS):
                rotate(0, g, 0)
                rotate(0, g, 1)
            layer_stats(1)
            layer_norm(1)
            split_x(1)

            def body(n, project, edges):
                for g in range(GROUPS):
                    row_max(n, 2 * g)
                    row_max(n, 2 * g + 1)
                    if project:
                        rotate(n + 1, g, 0)
                    inverse_total(n, 2 * g)
                    inverse_total(n, 2 * g + 1)
                    if project:
                        rotate(n + 1, g, 1)
                    if edges and g == 1:
                        gray_rest(n + 2)
                    if edges and g == 3:
                        layer_stats(n + 2)
                    split_o(n, g)
                if edges:
                    layer_norm(n + 2)
                    split_x(n + 2)
                residual(n)
            bodies(dve, body)

        @block.tensor
        def _(pe):
            def convolve(f, values_before):
                pe.wait_ge(gray_done, f + 1)
                positive(pe, x_lo_done, f)
                for which in range(2):
                    dst = (misc_bank, v_bank)[which]
                    if which == 1:
                        positive(pe, v_evac, values_before)
                    for dx in range(3):
                        nc.tensor.matmul(dst[:, :], band[:, which, dx, :], gray[:, :, dx:dx + COLS],
                                         start=(dx == 0), stop=False)
                    if which == 0:
                        pe.wait_ge(halo_loaded, 32 * (f + 1))
                    nc.tensor.matmul(dst[:, :], edge_band[:, which, :], halo[:, :, :],
                                     start=False, stop=True).then_inc(conv_done, 1)

            def transpose_x(f):
                pe.wait_ge(xn_done, f + 1)
                for ct in range(CT):
                    for t in range(TT):
                        last = nc.tensor.transpose(misc_bank[:, ct * ROWS + t * P:ct * ROWS + (t + 1) * P],
                                                   xn[:, t, ct * P:(ct + 1) * P], ident[:, :])
                last.then_inc(xt_done, 1)

            def three_passes(dst, stationary, moving, terms, **flags):
                passes = [(s, m) for k in range(terms) for s, m in ((0, 0), (0, 1), (1, 0))]
                for i, (s, m) in enumerate(passes):
                    k = i // 3
                    last = nc.tensor.matmul(dst, stationary[s](k), moving[m](k),
                                            start=(i == 0), stop=(i == len(passes) - 1), **flags)
                return last

            def project_qk(m, g):
                if g == 0:
                    pe.wait_ge(x_lo_done, m + 1)
                for which in range(2):
                    dst = (q_bank, k_bank)[which]
                    positive(pe, rope_mul, 2 * (GROUPS * m + g) + which - 1)
                    for half in range(2):
                        at = (2 * which + half) * P
                        last = three_passes(
                            dst[:, half * ROWS:(half + 1) * ROWS],
                            [lambda k, w=w: w[:, k, g, at:at + P] for w in (w_hi, w_lo)],
                            [lambda k, t=t: t[:, k, :] for t in (x_hi, x_lo)], CT)
                    last.then_inc(qk_done, 1)

            def project_v(m, g, edges):
                positive(pe, v_evac, GROUPS * m + g)
                if edges:
                    pe.wait_ge(abs_done, 2 * (m + 1) + 2)
                at = 4 * P
                for t in range(TT):
                    last = three_passes(
                        v_bank[:, t * COLS:(t + 1) * COLS],
                        [lambda k, s=s: s[:, k, t * P:(t + 1) * P] for s in (x_hi, x_lo)],
                        [lambda k, w=w: w[:, k, g, at:at + 4 * HEAD_DIM] for w in (w_hi, w_lo)], CT)
                last.then_inc(v_done, 1)

            def scores(n, p):
                for b in range(BLOCKS):
                    for head in range(2):
                        rows = slice(HEAD_DIM * head, HEAD_DIM * (head + 1))
                        if b % 2 or b == 0:
                            first = key_of(b, 0)
                            keys = qk[rows, p, 1, first:first + KEYS]
                        else:
                            own = qk[rows, p, 1, WINDOW * b:WINDOW * (b + 1)]
                            keys = bass.AP(tensor=own.tensor, offset=own.offset,
                                           ap=[list(own.ap[0]), [-WINDOW, 2], [1, WINDOW]])
                        last = nc.tensor.matmul(scores_bank[p % 2][rows, b * KEYS:(b + 1) * KEYS],
                                                qk[rows, p, 0, WINDOW * b:WINDOW * (b + 1)], keys,
                                                start=True, stop=True)
                last.then_inc(s_done, 1)

            def in_place(n, g):
                pe.wait_ge(moved[g], 16 * MOVES * (n + 1))

            def transpose_p(n, p):
                pe.wait_ge(norm_done, PAIRS * n + p + 1)
                for b in range(BLOCKS):
                    last = nc.tensor.transpose(scores_bank[p % 2][:, b * P:(b + 1) * P], prob[:, p % 2, b, :],
                                               ident[:, :])
                last.then_inc(t_done, 1)

            def attend(n, g):
                pe.wait_ge(v_evac, GROUPS * n + g + 1)
                pe.wait_ge(v_crossed[g], 32 * (n + 1))
                positive(pe, o_lo_done, GROUPS * n + g)
                for p in (2 * g, 2 * g + 1):
                    pe.wait_ge(pt_evac, PAIRS * n + p + 1)
                    for b in range(BLOCKS):
                        for head in range(2):
                            at = HEAD_DIM * (2 * (p % 2) + head)
                            vals = v_cross[:, g, at:at + HEAD_DIM] if b == 2 else v[:, g, b // 2, at:at + HEAD_DIM]
                            to = (p % 2) * ROWS + WINDOW * b
                            last = nc.tensor.matmul(
                                o_bank[HEAD_DIM * head:HEAD_DIM * (head + 1), to:to + WINDOW], vals,
                                prob_t[:, p % 2, b, HEAD_DIM * head:HEAD_DIM * (head + 1)], start=True, stop=True)
                last.then_inc(o_done, 1)

            def project_out(n, g):
                pe.wait_ge(o_lo_done, GROUPS * n + g + 1)
                if g == 0:
                    positive(pe, resid_done, n)
                for t in range(TT):
                    for k in range(2):
                        for s, w in ((o_hi, wo_hi), (o_hi, wo_lo), (o_lo, wo_hi)):
                            first = g == 0 and t == 0 and k == 0 and w is wo_hi and s is o_hi
                            last = nc.tensor.matmul(out_bank[:, t * COLS:(t + 1) * COLS],
                                                    s[:, k, t * P:(t + 1) * P], w[:, 2 * g + k, :],
                                                    start=first, stop=(g == GROUPS - 1), skip_group_check=True)
                if g == GROUPS - 1:
                    last.then_inc(out_done, 1)

            pe.wait_ge(const_loaded, 16 * CONSTS)
            pe.wait_ge(borders_zero, 1)
            pe.wait_ge(band_ready, 1)
            convolve(0, 0)
            transpose_x(0)
            pe.wait_ge(w_lo_ready, CHUNKS)
            for g in range(GROUPS):
                project_qk(0, g)
                project_v(0, g, False)
            convolve(1, GROUPS)
            in_place(0, 0)
            transpose_x(1)

            def body(n, project, edges):
                for g in range(GROUPS):
                    scores(n, 2 * g)
                    scores(n, 2 * g + 1)
                    if project:
                        project_qk(n + 1, g)
                    if edges and g == 2:
                        convolve(n + 2, GROUPS * (n + 1) + g)
                    if g:
                        project_out(n, g - 1)
                    if g < GROUPS - 1:
                        in_place(n, g + 1)
                    transpose_p(n, 2 * g)
                    transpose_p(n, 2 * g + 1)
                    if project:
                        project_v(n + 1, g, edges and g == 2)
                    attend(n, g)
                if project:
                    in_place(n + 1, 0)
                if edges:
                    transpose_x(n + 2)
                project_out(n, GROUPS - 1)
            bodies(pe, body)


        a_scope.close()
        b_ = lambda name, shape, dt=F32: sb(name, shape, dt)
        me_hi = b_("me_hi", [P, EXPERTS, CT, EXPERT_COLS], F32R)
        me_lo = b_("me_lo", [P, EXPERTS, CT, EXPERT_COLS], F32R)
        mo_hi = b_("mo_hi", [P, EXPERTS, COLS], F32R)
        mo_lo = b_("mo_lo", [P, EXPERTS, COLS], F32R)
        raw = b_("raw", [P, 2, 4 * COLS])
        sim_t = b_("sim_t", [P, CT, EXPERTS])
        sim_sq = b_("sim_sq", [P, CT, EXPERTS])
        ones = b_("ones", [P, P])
        expert_no = b_("expert_no", [P, EXPERTS])
        gate_t = b_("gate_t", [P, EXPERTS])
        m_stats = b_("m_stats", [P, TT, 6])
        m_moments = b_("m_moments", [P, TT, 2])
        m_spread = b_("m_spread", [P, TT])
        m_rstd = b_("m_rstd", [P, TT])
        m_square = b_("m_square", [P, TT])
        m_rnorm = b_("m_rnorm", [P, TT])
        m_xn = b_("m_xn", [P, TT, COLS])
        m_x = b_("m_x", [P, CT, ROWS])
        mx_hi = b_("mx_hi", [P, CT, ROWS], F32R)
        mx_lo = b_("mx_lo", [P, CT, ROWS], F32R)
        logit = b_("logit", [P, TT, EXPERTS])
        gated = b_("gated", [P, TT, EXPERTS])
        active = b_("active", [P, TT, EXPERTS])
        fallback = b_("fallback", [P, TT, EXPERTS])
        idle = b_("idle", [P, TT])
        top = b_("top", [P, TT, 8])
        top_at = b_("top_at", [P, TT, 8], U32)
        top_no = b_("top_no", [P, TT, 2])
        row_stat = b_("row_stat", [P, TT])
        share = b_("share", [P, 3, TT, EXPERTS])
        share_n = b_("share_n", [P, TT, EXPERTS])
        part = b_("part", [P, TT, EXPERT_COLS])
        qkv = b_("qkv", [P, TT, EXPERT_COLS])
        qkt = b_("qkt", [P, 2, ROWS])
        m_bias = b_("m_bias", [P, 2, TT])
        m_prob = b_("m_prob", [P, TT, ROWS])
        m_total = b_("m_total", [P, TT])
        m_inv = b_("m_inv", [P, TT])
        m_prob_t = b_("m_prob_t", [P, TT, ROWS])
        mo_t_hi = b_("mo_t_hi", [P, ROWS], F32R)
        mo_t_lo = b_("mo_t_lo", [P, ROWS], F32R)
        out_part = b_("out_part", [P, TT, COLS])
        result = b_("result", [P, TT, COLS])

        chunk_bank = bank[0:4]
        down_bank = bank[4:6]
        turn_bank, attn_bank = bank[6], bank[7]
        logit_ps = turn_bank[:, 0:TT * EXPERTS].rearrange("p (t e) -> p t e", t=TT)

        STEPS = EXPERTS * TT
        DOWNS = EXPERTS // 2 * TT
        M_CHUNKS = EXPERTS + EXPERTS // 4
        
        m_const_loaded = sem("m_const_loaded")
        m_raw_loaded = [sem(f"m_raw_loaded{i}") for i in range(2)]
        ones_set = sem("ones_set")
        m_hi_ready = sem("m_hi_ready")
        m_lo_ready = sem("m_lo_ready")
        gate_exp = sem("gate_exp")
        setup_step = sem("setup_step")
        sim_squared = sem("sim_squared")
        sim_summed_ps = sem("sim_summed_ps")
        sim_summed = sem("sim_summed")
        sim_root = sem("sim_root")
        sim_ready = sem("sim_ready")
        norm_step = sem("norm_step")
        m_spread_done = sem("m_spread_done")
        m_rstd_done = sem("m_rstd_done")
        m_square_done = sem("m_square_done")
        m_rnorm_done = sem("m_rnorm_done")
        m_xn_done = sem("m_xn_done")
        m_xt_done = sem("m_xt_done")
        m_x_done = sem("m_x_done")
        mx_hi_done = sem("mx_hi_done")
        mx_lo_done = sem("mx_lo_done")
        logits_done = sem("logits_done")
        logits_read = sem("logits_read")
        router_step = sem("router_step")
        share_step = sem("share_step")
        router_in = sem("router_in")
        router_exp = sem("router_exp")
        shifted = sem("shifted")
        step_done = sem("step_done")
        combined = sem("combined")
        qk_turned = sem("qk_turned")
        qkt_done = sem("qkt_done")
        m_scores = sem("m_scores")
        m_max = sem("m_max")
        m_bias_done = sem("m_bias_done")
        m_exp = sem("m_exp")
        m_inv_done = sem("m_inv_done")
        share_n_done = sem("share_n_done")
        m_turned = sem("m_turned")
        m_prob_t_done = sem("m_prob_t_done")
        mixed = sem("mixed")
        mo_hi_done = sem("mo_hi_done")
        mo_lo_done = sem("mo_lo_done")
        down_done = sem("down_done")
        down_step = sem("down_step")

        def m_chunk(n):
            slot = raw[:, n % 2, :]
            if n < EXPERTS:
                view = slot[:, 0:CT * EXPERT_COLS].rearrange("p (a c) -> p a c", a=CT)
                return w_moe[:, n, :, :], view, me_hi[:, n, :, :], me_lo[:, n, :, :]
            e = 4 * (n - EXPERTS)
            return (w_moe_out[:, e:e + 4, :], slot.rearrange("p (a c) -> p a c", a=4),
                    mo_hi[:, e:e + 4, :], mo_lo[:, e:e + 4, :])


        @block.sync
        def _(sp):
            sp.wait_ge(resid_done, IMAGES)
            sp.dma_start(sim_t[:, :, :], sim.rearrange("(a p) e -> p a e", p=P)).then_inc(m_const_loaded, 16)
            sp.dma_start(gate_t[:, :], gates.partition_broadcast(P)).then_inc(m_const_loaded, 16)
            sp.dma_start(expert_no[:, :], numbers).then_inc(m_const_loaded, 16)
            for n in range(M_CHUNKS):
                if n >= 2:
                    sp.wait_ge(m_hi_ready, n - 1)
                    sp.wait_ge(m_lo_ready, n - 1)
                src, slot, _, _ = m_chunk(n)
                sp.dma_start(slot, src).then_inc(m_raw_loaded[n % 2], 16)

        @block.gpsimd
        def _(pool):
            pool.wait_ge(resid_done, IMAGES)
            nc.gpsimd.memset(ones[:, :], 1.0).then_inc(ones_set, 1)

            def roots(f):
                pool.wait_ge(m_spread_done, f + 1)
                nc.gpsimd.tensor_tensor(m_rstd[:, :], m_spread[:, :], minus_half[:, :], ALU.pow).then_inc(m_rstd_done, 1)
                pool.wait_ge(m_square_done, f + 1)
                nc.gpsimd.tensor_tensor(m_rnorm[:, :], m_square[:, :], minus_half[:, :], ALU.pow).then_inc(m_rnorm_done, 1)

            roots(0)
            pool.wait_ge(sim_summed, 1)
            nc.gpsimd.tensor_tensor(sim_sq[:, 0, :], sim_sq[:, 1, :],
                                    minus_half[:, 0:1].to_broadcast([P, EXPERTS]), ALU.pow).then_inc(sim_root, 1)
            roots(1)

            def body(b, project, front):
                if front:
                    roots(b + 2)
                pool.wait_ge(down_step, 2 * DOWNS * (b + 1))
                pool.dma_start(out[b].rearrange("(t p) c -> p t c", p=P), result[:, :, :]).then_inc(stored, 16)
            bodies(pool, body)
            pool.wait_ge(stored, 16 * IMAGES)

        @block.scalar
        def _(act):
            def evacuate_x(f):
                act.wait_ge(m_xt_done, f + 1)
                positive(act, logits_done, f)
                positive(act, mx_lo_done, f)
                nc.scalar.activation(m_x[:, :, :], turn_bank[:, :].rearrange("p (a c) -> p a c", a=CT),
                                     ACT.Copy).then_inc(m_x_done, 1)

            def split_x(f):
                positive(act, step_done, STEPS * f)
                act.wait_ge(m_x_done, f + 1)
                nc.scalar.activation(mx_hi[:, :, :], m_x[:, :, :], ACT.Copy).then_inc(mx_hi_done, 1)

            def router_exponent(f):
                act.wait_ge(router_in, f + 1)
                nc.scalar.activation(active[:, :, :], gated[:, :, :], ACT.Exp).then_inc(router_exp, 1)

            act.wait_ge(resid_done, IMAGES)
            act.wait_ge(m_const_loaded, 48)
            nc.scalar.activation(gate_t[:, :], gate_t[:, :], ACT.Exp, scale=-1.0).then_inc(gate_exp, 1)
            for n in range(M_CHUNKS):
                act.wait_ge(m_raw_loaded[n % 2], 16 * (n // 2 + 1))
                _, slot, hi, _ = m_chunk(n)
                nc.scalar.activation(hi, slot, ACT.Copy).then_inc(m_hi_ready, 1)
                if n == 2:
                    evacuate_x(0)
                    split_x(0)
                if n == 4:
                    router_exponent(0)
            evacuate_x(1)
            router_exponent(1)
            split_x(1)

            def body(b, project, front):
                act.wait_ge(qk_turned, b + 1)
                positive(act, m_scores, b)
                nc.scalar.activation(qkt[:, :, :], turn_bank[:, :].rearrange("p (a c) -> p a c", a=2),
                                     ACT.Copy).then_inc(qkt_done, 1)
                act.wait_ge(m_bias_done, b + 1)
                positive(act, m_turned, b)
                for t in range(TT):
                    last = nc.scalar.activation(m_prob[:, t, :], attn_bank[:, t * ROWS:(t + 1) * ROWS], ACT.Exp,
                                                bias=m_bias[:, 1, t:t + 1], scale=SCORE_SCALE,
                                                accum_out=m_total[:, t:t + 1])
                last.then_inc(m_exp, 1)
                act.wait_ge(m_turned, b + 1)
                nc.scalar.activation(m_prob_t[:, :, :], attn_bank[:, :].rearrange("p (a c) -> p a c", a=TT),
                                     ACT.Copy).then_inc(m_prob_t_done, 1)
                act.wait_ge(mixed, b + 1)
                positive(act, down_done, DOWNS * b)
                nc.scalar.activation(mo_t_hi[:, :], attn_bank[:, 0:ROWS], ACT.Copy).then_inc(mo_hi_done, 1)
                if front:
                    evacuate_x(b + 2)
                    router_exponent(b + 2)
                    split_x(b + 2)
            bodies(act, body)

        @block.vector
        def _(dve):
            def statistics(f):
                for t in range(TT):
                    last = nc.vector.bn_stats(m_stats[:, t, :], h_all[:, bass.ds(f * TT + t, 1), :])
                last.then_inc(norm_step, 1)
                dve.wait_ge(norm_step, 4 * f + 1)
                positive(dve, m_rnorm_done, f)
                nc.vector.memset(carrier[:, :], 0.0)
                for t in range(TT):
                    last = nc.vector.bn_aggr(m_moments[:, t, :], m_stats[:, t, :])
                last.then_inc(norm_step, 1)
                dve.wait_ge(norm_step, 4 * f + 2)
                nc.vector.tensor_scalar(m_spread[:, :], m_moments[:, :, 1], LN_EPS, None, ALU.add)\
                    .then_inc(m_spread_done, 1)

            def layer_norm(f):
                dve.wait_ge(m_rstd_done, f + 1)
                nc.vector.tensor_tensor(m_square[:, :], m_rstd[:, :], m_rstd[:, :], ALU.mult).then_inc(norm_step, 1)
                positive(dve, m_xt_done, f)
                for t in range(TT):
                    last = nc.vector.tensor_scalar(m_xn[:, t:t + 1, :], h_all[:, bass.ds(f * TT + t, 1), :],
                                                   m_moments[:, t, 0:1], m_rstd[:, t:t + 1],
                                                   ALU.subtract, ALU.mult)
                last.then_inc(m_xn_done, 1)
                dve.wait_ge(norm_step, 4 * f + 3)
                nc.vector.tensor_tensor(m_square[:, :], m_square[:, :], m_moments[:, :, 1], ALU.mult)\
                    .then_inc(norm_step, 1)
                dve.wait_ge(norm_step, 4 * f + 4)
                nc.vector.tensor_scalar(m_square[:, :], m_square[:, :], float(COLS), 1e-24, ALU.mult, ALU.max)\
                    .then_inc(m_square_done, 1)

            def split_x(f):
                dve.wait_ge(mx_hi_done, f + 1)
                nc.vector.tensor_tensor(mx_lo[:, :, :], m_x[:, :, :], mx_hi[:, :, :].bitcast(F32), ALU.subtract)\
                    .then_inc(mx_lo_done, 1)

            ROUTER_STEPS = 12

            def router(f, section):
                base = ROUTER_STEPS * f

                def after(step):
                    dve.wait_ge(router_step, base + step)

                if section == 0:
                    dve.wait_ge(logits_done, f + 1)
                    dve.wait_ge(m_rnorm_done, f + 1)
                    for t in range(TT):
                        last = nc.vector.scalar_tensor_tensor(
                            out=logit[:, t, :], in0=logit_ps[:, t, :], scalar=m_rnorm[:, t:t + 1],
                            in1=gate_t[:, :], op0=ALU.mult, op1=ALU.subtract)
                    last.then_inc(logits_read, 1)
                    dve.wait_ge(logits_read, f + 1)
                    nc.vector.tensor_scalar(active[:, :, :], logit[:, :, :], 0.0, None, ALU.is_gt)\
                        .then_inc(router_step, 1)
                    for t in range(TT):
                        last = nc.vector.max(top[:, t, :], logit[:, t, :])
                    last.then_inc(router_step, 1)
                    after(2)
                    nc.vector.tensor_reduce(row_stat[:, :], active[:, :, :], AX_X, ALU.max)\
                        .then_inc(router_step, 1)
                    for t in range(TT):
                        last = nc.vector.max_index(top_at[:, t, :], top[:, t, :], logit[:, t, :])
                    last.then_inc(router_step, 1)
                    after(4)
                    nc.vector.tensor_copy(top_no[:, :, :], top_at[:, :, 0:2]).then_inc(router_step, 1)
                    nc.vector.tensor_scalar(idle[:, :], row_stat[:, :], 0.0, None, ALU.is_equal)\
                        .then_inc(router_step, 1)
                    after(5)
                    for t in range(TT):
                        last = nc.vector.tensor_scalar(fallback[:, t, :], expert_no[:, :], top_no[:, t, 0:1], None,
                                                       ALU.is_equal)
                    last.then_inc(router_step, 1)
                    after(7)
                    for t in range(TT):
                        last = nc.vector.scalar_tensor_tensor(
                            out=fallback[:, t, :], in0=expert_no[:, :], scalar=top_no[:, t, 1:2],
                            in1=fallback[:, t, :], op0=ALU.is_equal, op1=ALU.max)
                    last.then_inc(router_step, 1)
                    nc.vector.tensor_scalar(gated[:, :, :], logit[:, :, :], 0.0, None, ALU.max)
                    after(8)
                    for t in range(TT):
                        last = nc.vector.scalar_tensor_tensor(
                            out=active[:, t, :], in0=fallback[:, t, :], scalar=idle[:, t:t + 1],
                            in1=active[:, t, :], op0=ALU.mult, op1=ALU.max)
                    last.then_inc(router_step, 1)
                    after(9)
                    nc.vector.tensor_scalar(fallback[:, :, :], active[:, :, :], 1.0, EXCLUDED, ALU.subtract,
                                            ALU.mult).then_inc(router_step, 1)
                    after(10)
                    nc.vector.tensor_tensor(gated[:, :, :], gated[:, :, :], fallback[:, :, :], ALU.add)\
                        .then_inc(router_step, 1)
                    after(11)
                    nc.vector.tensor_reduce(row_stat[:, :], gated[:, :, :], AX_X, ALU.max)\
                        .then_inc(router_step, 1)
                    after(12)
                    nc.vector.tensor_tensor(gated[:, :, :], gated[:, :, :],
                                            row_stat[:, :].unsqueeze(2).to_broadcast([P, TT, EXPERTS]),
                                            ALU.subtract).then_inc(router_in, 1)
                else:
                    dve.wait_ge(router_exp, f + 1)
                    nc.vector.tensor_reduce(row_stat[:, :], active[:, :, :], AX_X, ALU.add).then_inc(share_step, 1)
                    dve.wait_ge(share_step, 3 * f + 1)
                    nc.vector.reciprocal(idle[:, :], row_stat[:, :]).then_inc(share_step, 1)
                    dve.wait_ge(share_step, 3 * f + 2)
                    nc.vector.tensor_tensor(share[:, 2, :, :], active[:, :, :],
                                            idle[:, :].unsqueeze(2).to_broadcast([P, TT, EXPERTS]),
                                            ALU.mult).then_inc(share_step, 1)

            def shift_shares(f):
                dve.wait_ge(share_step, 3 * f + 3)
                positive(dve, combined, STEPS * f)
                if not (isinstance(f, int) and f == 0):
                    nc.vector.tensor_copy(share[:, 0, :, :], share[:, 1, :, :]).then_inc(shifted, 1)
                    dve.wait_ge(shifted, 2 * f)
                    nc.vector.tensor_copy(share[:, 1, :, :], share[:, 2, :, :]).then_inc(shifted, 1)
                else:
                    nc.vector.tensor_copy(share[:, 1, :, :], share[:, 2, :, :]).then_inc(shifted, 1)
                dve.wait_ge(shifted, 2 * f + 1)

            def combine(m, k):
                e, t = k // TT, k % TT
                done = STEPS * m + k
                dve.wait_ge(step_done, done + 1)
                src = chunk_bank[k % 4][:, 0:EXPERT_COLS]
                by = share[:, 1, t, e:e + 1]
                if e == 0:
                    nc.vector.tensor_scalar(part[:, t, :], src, by, None, ALU.mult).then_inc(combined, 1)
                    return
                dve.wait_ge(combined, done - 1)
                if e == EXPERTS - 1:
                    positive(dve, mixed, m)
                nc.vector.scalar_tensor_tensor(out=(qkv if e == EXPERTS - 1 else part)[:, t, :], in0=src, scalar=by,
                                               in1=part[:, t, :], op0=ALU.mult, op1=ALU.add).then_inc(combined, 1)

            def attention_max(b):
                dve.wait_ge(m_scores, b + 1)
                nc.vector.tensor_reduce(m_bias[:, 0, :], attn_bank[:, :].rearrange("p (t c) -> p t c", t=TT), AX_X,
                                        ALU.max, negate=True).then_inc(m_max, 1)
                dve.wait_ge(m_max, b + 1)
                nc.vector.tensor_scalar(m_bias[:, 1, :], m_bias[:, 0, :], SCORE_SCALE, None, ALU.mult)\
                    .then_inc(m_bias_done, 1)

            def normalise_shares(b):
                dve.wait_ge(m_exp, b + 1)
                nc.vector.reciprocal(m_inv[:, :], m_total[:, :]).then_inc(m_inv_done, 1)
                dve.wait_ge(m_inv_done, b + 1)
                nc.vector.tensor_tensor(share_n[:, :, :], share[:, 0, :, :],
                                        m_inv[:, :].unsqueeze(2).to_broadcast([P, TT, EXPERTS]),
                                        ALU.mult).then_inc(share_n_done, 1)

            def split_mixed(b):
                dve.wait_ge(mo_hi_done, b + 1)
                nc.vector.tensor_tensor(mo_t_lo[:, :], attn_bank[:, 0:ROWS], mo_t_hi[:, :].bitcast(F32),
                                        ALU.subtract).then_inc(mo_lo_done, 1)

            def add_down(b, j):
                t = j % TT
                dve.wait_ge(down_done, DOWNS * b + j + 1)
                if j == 0:
                    dve.wait_ge(share_n_done, b + 1)
                for i in range(2):
                    e = 2 * (j // TT) + i
                    at = 2 * DOWNS * b + 2 * j + i
                    if e == 0:
                        before = h_all[:, bass.ds(b * TT + t, 1), :]
                    else:
                        before = out_part[:, t:t + 1, :]
                        dve.wait_ge(down_step, at if i else at - 2)
                    last_e = e == EXPERTS - 1
                    if last_e and t == 0:
                        positive(dve, stored, 16 * b)
                    ins = nc.vector.scalar_tensor_tensor(
                        out=(result if last_e else out_part)[:, t:t + 1, :],
                        in0=down_bank[j % 2][:, i * COLS:(i + 1) * COLS].unsqueeze(1),
                        scalar=share_n[:, t, e:e + 1], in1=before, op0=ALU.mult, op1=ALU.add)
                    ins.then_inc(down_step, 1)

            statistics(0)
            layer_norm(0)
            dve.wait_ge(gate_exp, 1)
            nc.vector.tensor_scalar(gate_t[:, :], gate_t[:, :], 1.0, None, ALU.add).then_inc(setup_step, 1)
            dve.wait_ge(setup_step, 1)
            nc.vector.reciprocal(gate_t[:, :], gate_t[:, :]).then_inc(setup_step, 1)
            nc.vector.tensor_tensor(sim_sq[:, :, :], sim_t[:, :, :], sim_t[:, :, :], ALU.mult).then_inc(sim_squared, 1)
            dve.wait_ge(sim_summed_ps, 1)
            nc.vector.tensor_scalar(sim_sq[:, 1, :], attn_bank[:, 0:EXPERTS], 1e-24, None, ALU.max)\
                .then_inc(sim_summed, 1)
            dve.wait_ge(sim_root, 1)
            nc.vector.tensor_tensor(sim_t[:, :, :], sim_t[:, :, :],
                                    sim_sq[:, 0:1, :].to_broadcast([P, CT, EXPERTS]), ALU.mult).then_inc(sim_ready, 1)
            dve.wait_ge(setup_step, 2)
            for n in range(EXPERTS):
                dve.wait_ge(m_hi_ready, n + 1)
                _, slot, hi, lo = m_chunk(n)
                nc.vector.tensor_tensor(lo, slot, hi.bitcast(F32), ALU.subtract).then_inc(m_lo_ready, 1)
                if n == 2:
                    split_x(0)
                    router(0, 0)
                if n == 4:
                    router(0, 1)
                    shift_shares(0)
                if n >= 5:
                    for k in range(TT * (n - 5), TT * (n - 4)):
                        combine(0, k)
            for k in range(TT * (EXPERTS - 5), STEPS):
                combine(0, k)
            for n in range(EXPERTS, M_CHUNKS):
                dve.wait_ge(m_hi_ready, n + 1)
                _, slot, hi, lo = m_chunk(n)
                nc.vector.tensor_tensor(lo, slot, hi.bitcast(F32), ALU.subtract).then_inc(m_lo_ready, 1)
            statistics(1)
            layer_norm(1)
            router(1, 0)
            router(1, 1)
            shift_shares(1)
            split_x(1)

            def body(b, project, front):
                for k in range(STEPS):
                    if project:
                        combine(b + 1, k)
                    if k == 3:
                        attention_max(b)
                    if k == 6:
                        normalise_shares(b)
                    if k == 11:
                        split_mixed(b)
                    if front and k == 8:
                        statistics(b + 2)
                    if front and k == 12:
                        layer_norm(b + 2)
                    if front and k == 21:
                        router(b + 2, 0)
                    if front and k == 26:
                        router(b + 2, 1)
                    if 13 <= k < 27:
                        add_down(b, k - 13)
                if front:
                    shift_shares(b + 2)
                    split_x(b + 2)
                elif project:
                    nc.vector.tensor_copy(share[:, 0, :, :], share[:, 1, :, :]).then_inc(shifted, 1)
                    dve.wait_ge(shifted, 2 * (b + 2))
                for j in range(DOWNS - 2, DOWNS):
                    add_down(b, j)
            bodies(dve, body)

        @block.tensor
        def _(pe):
            def transpose_x(f):
                pe.wait_ge(m_xn_done, f + 1)
                positive(pe, qkt_done, f - 1)
                for ct in range(CT):
                    for t in range(TT):
                        last = nc.tensor.transpose(turn_bank[:, ct * ROWS + t * P:ct * ROWS + (t + 1) * P],
                                                   m_xn[:, t, ct * P:(ct + 1) * P], ident[:, :])
                last.then_inc(m_xt_done, 1)

            def logits(f):
                pe.wait_ge(m_x_done, f + 1)
                if isinstance(f, int) and f == 0:
                    pe.wait_ge(sim_ready, 1)
                for t in range(TT):
                    for ct in range(CT):
                        last = nc.tensor.matmul(logit_ps[:, t, :], m_x[:, ct, t * P:(t + 1) * P], sim_t[:, ct, :],
                                                start=(ct == 0), stop=(ct == CT - 1))
                last.then_inc(logits_done, 1)

            def expert_step(m, k):
                e, t = k // TT, k % TT
                if k == 0:
                    pe.wait_ge(mx_lo_done, m + 1)
                positive(pe, combined, STEPS * m + k - 3)
                if isinstance(m, int) and m == 0 and t == 0:
                    pe.wait_ge(m_lo_ready, e + 1)
                dst = chunk_bank[k % 4][:, 0:EXPERT_COLS]
                n = 0
                for ct in range(CT):
                    for s, w in ((mx_hi, me_hi), (mx_hi, me_lo), (mx_lo, me_hi)):
                        last = nc.tensor.matmul(dst, s[:, ct, t * P:(t + 1) * P], w[:, e, ct, :],
                                                start=(n == 0), stop=(n == 3 * CT - 1))
                        n += 1
                last.then_inc(step_done, 1)

            def transpose_qk(b):
                pe.wait_ge(combined, STEPS * (b + 1))
                positive(pe, logits_read, b + 2 if not isinstance(b, int) else min(b + 2, IMAGES))
                for which in range(2):
                    for t in range(TT):
                        last = nc.tensor.transpose(turn_bank[:, which * ROWS + t * P:which * ROWS + (t + 1) * P],
                                                   qkv[:, t, which * P:(which + 1) * P], ident[:, :])
                last.then_inc(qk_turned, 1)

            def token_scores(b):
                pe.wait_ge(qkt_done, b + 1)
                positive(pe, mo_lo_done, b)
                for t in range(TT):
                    last = nc.tensor.matmul(attn_bank[:, t * ROWS:(t + 1) * ROWS], qkt[:, 0, t * P:(t + 1) * P],
                                            qkt[:, 1, :], start=True, stop=True)
                last.then_inc(m_scores, 1)

            def transpose_prob(b):
                pe.wait_ge(m_exp, b + 1)
                for kt in range(TT):
                    for t in range(TT):
                        last = nc.tensor.transpose(attn_bank[:, kt * ROWS + t * P:kt * ROWS + (t + 1) * P],
                                                   m_prob[:, t, kt * P:(kt + 1) * P], ident[:, :])
                last.then_inc(m_turned, 1)

            def mix_values(b):
                pe.wait_ge(m_prob_t_done, b + 1)
                for kt in range(TT):
                    last = nc.tensor.matmul(attn_bank[:, 0:ROWS], qkv[:, kt, 2 * EXPERT_DIM:EXPERT_COLS],
                                            m_prob_t[:, kt, :], start=(kt == 0), stop=(kt == TT - 1))
                last.then_inc(mixed, 1)

            def down_step_pair(b, j):
                e, t = 2 * (j // TT), j % TT
                if j == 0:
                    pe.wait_ge(mo_lo_done, b + 1)
                    if isinstance(b, int) and b == 0:
                        pe.wait_ge(m_lo_ready, M_CHUNKS)
                positive(pe, down_step, 2 * DOWNS * b + 2 * j - 2)
                for i, (s, w) in enumerate(((mo_t_hi, mo_hi), (mo_t_hi, mo_lo), (mo_t_lo, mo_hi))):
                    last = nc.tensor.matmul(down_bank[j % 2][:, :], s[:, t * P:(t + 1) * P], w[:, e:e + 2, :],
                                            start=(i == 0), stop=(i == 2))
                last.then_inc(down_done, 1)

            pe.wait_ge(sim_squared, 1)
            pe.wait_ge(ones_set, 1)
            for ct in range(CT):
                last = nc.tensor.matmul(attn_bank[:, 0:EXPERTS], ones[:, :], sim_sq[:, ct, :],
                                        start=(ct == 0), stop=(ct == CT - 1))
            last.then_inc(sim_summed_ps, 1)
            transpose_x(0)
            logits(0)
            for k in range(STEPS):
                expert_step(0, k)
            transpose_x(1)
            logits(1)

            def body(b, project, front):
                for k in range(STEPS):
                    if project:
                        expert_step(b + 1, k)
                    if k == 1:
                        transpose_qk(b)
                    if k == 3:
                        token_scores(b)
                    if k == 7:
                        transpose_prob(b)
                    if k == 10:
                        mix_values(b)
                    if front and k == 14:
                        transpose_x(b + 2)
                    if front and k == 19:
                        logits(b + 2)
                    if 12 <= k < 26:
                        down_step_pair(b, k - 12)
                for j in range(DOWNS - 2, DOWNS):
                    down_step_pair(b, j)
            bodies(pe, body)


def layouts(x, scharr, w_qkv, w_out, sim, gates, q_proj, k_proj, v_proj, o_proj):
    inner = HEADS * HEAD_DIM
    halves = [w_qkv[k * inner:(k + 1) * inner].reshape(GROUPS, 4, 2, HALF, COLS).transpose(4, 0, 2, 1, 3)
              .reshape(COLS, GROUPS, 4 * HEAD_DIM) for k in range(2)]
    values = w_qkv[2 * inner:].reshape(GROUPS, 4 * HEAD_DIM, COLS).transpose(2, 0, 1)
    experts = np.concatenate([q_proj, k_proj, v_proj], axis=2)
    return {
        "x": x,
        "scharr": scharr,
        "scharr_last": np.ascontiguousarray(scharr[:, 0].transpose(1, 2, 0)),
        "w_qkv": np.ascontiguousarray(np.concatenate(halves + [values], axis=2)),
        "w_out": np.ascontiguousarray(w_out.T),
        "sim": sim,
        "gates": gates,
        "w_moe": np.ascontiguousarray(experts.reshape(EXPERTS, CT, P, EXPERT_COLS).transpose(2, 0, 1, 3)),
        "w_moe_out": np.ascontiguousarray(o_proj.transpose(1, 0, 2)),
    }


def kernel(x, L0_tok_scharr, L0_attn_w_qkv, L0_attn_w_out, L0_ffn_sim_matrix, L0_ffn_gates, L0_ffn_q_proj,
           L0_ffn_k_proj, L0_ffn_v_proj, L0_ffn_o_proj):
    import concourse.bacc as bacc
    from concourse.bass_utils import run_bass_kernel_spmd

    given = [np.asarray(a) for a in (x, L0_tok_scharr, L0_attn_w_qkv, L0_attn_w_out, L0_ffn_sim_matrix, L0_ffn_gates,
                                     L0_ffn_q_proj, L0_ffn_k_proj, L0_ffn_v_proj, L0_ffn_o_proj)]
    arrays = {**layouts(*given), **shape_constants()}
    nc = bacc.Bacc("TRN2", target_bir_lowering=False, num_devices=1)
    args = {name: nc.dram_tensor(f"in_{name}", a.shape, mybir.dt.from_np(a.dtype), kind="ExternalInput").ap()
            for name, a in arrays.items()}
    out = nc.dram_tensor("out", (IMAGES, ROWS, COLS), F32, kind="ExternalOutput").ap()
    build(nc, **args, out=out)
    ran = run_bass_kernel_spmd(nc, [{f"in_{name}": np.ascontiguousarray(a) for name, a in arrays.items()}],
                               core_ids=[0])
    return ran.results[0]["out"]
```

```python
from contextlib import ExitStack

import numpy as np

import concourse.bass as bass
from concourse import mybir

F32 = mybir.dt.float32
F32R = mybir.dt.float32r
U32 = mybir.dt.uint32
ALU = mybir.AluOpType
ACT = mybir.ActivationFunctionType
AX_X = mybir.AxisListType.X

P = 128
IMAGES, CHANNELS, ROWS, COLS = 16, 3, 256, 256
TT = ROWS // P
CT = COLS // P
HEADS, HEAD_DIM, WINDOW = 16, 64, 64
HALF = HEAD_DIM // 2
PAIRS = HEADS // 2
GROUPS = HEADS // 4
BLOCKS = ROWS // WINDOW
KEYS = 2 * WINDOW
GROUP_COLS = 3 * 4 * HEAD_DIM
RAW_SLOTS = 5
MOVES = 8
GRAY = (0.2989, 0.587, 0.114)
LN_EPS, RMS_EPS = 1e-5, 1e-6
MASKED = -1e9
EXCLUDED = 1e29
EXPERTS, EXPERT_DIM = 16, 128
EXPERT_COLS = 3 * EXPERT_DIM
SCORE_SCALE = float(EXPERT_DIM) ** -0.5


def positive(eng, sem, count):
    if isinstance(count, int) and count <= 0:
        return
    eng.wait_ge(sem, count)


def shape_constants():
    freq = 1.0 / np.float32(10000.0) ** (np.arange(0, HEAD_DIM, 2, dtype=np.float32) / np.float32(HEAD_DIM))
    angle = np.outer(np.arange(ROWS, dtype=np.float32), freq.astype(np.float32)).astype(np.float32)
    cos, sin = np.cos(angle).T, np.sin(angle).T
    cos, sin = np.tile(cos, (4, 1)), np.tile(sin, (4, 1))
    rope_k = np.stack([cos, -sin, sin], 1).astype(np.float32)
    rope_q = (rope_k * np.float32(HEAD_DIM ** -0.5)).astype(np.float32)
    mask = np.full((P, BLOCKS, KEYS), MASKED, np.float32)
    for b in range(BLOCKS):
        for c in range(KEYS):
            key = key_of(b, c)
            for r in range(WINDOW):
                q = WINDOW * b + r
                if q >= key and q - key <= WINDOW:
                    mask[r, b, c] = mask[WINDOW + r, b, c] = 0.0
    row = np.zeros((P, 3, P), np.float32)
    for dy in range(3):
        for m in range(P):
            k = m + dy - 1
            if 0 <= k < P:
                row[k, dy, m] = 1.0
    edge = np.zeros((6, P), np.float32)
    edge[0:3, P - 1] = 1.0
    edge[3:6, 0] = 1.0
    return {"rope": np.stack([rope_q, rope_k], 1).reshape(P, 2, 3, ROWS), "mask": mask, "row": row,
            "edge": edge, "identity": np.eye(P, dtype=np.float32),
            "numbers": np.tile(np.arange(EXPERTS, dtype=np.float32), (P, 1))}


def key_of(block, column):
    if block == 0:
        return column
    if block % 2:
        return WINDOW * (block - 1) + column
    return WINDOW * block + column if column < WINDOW else WINDOW * (block - 1) + column - WINDOW


def reversed_halves(ap):
    (part, (step, two), inner) = ap.ap
    return bass.AP(tensor=ap.tensor, offset=ap.offset + step, ap=[list(part), [-step, two], list(inner)])


def build(nc, x, scharr, scharr_last, w_qkv, w_out, sim, gates, w_moe, w_moe_out, rope, mask, row, edge, identity, numbers, out,
          stop_after_a=False):
    with ExitStack() as ctx:
        def sem(name):
            return ctx.enter_context(nc.semaphore(name))

        def sb(name, shape, dt=F32, scope=ctx):
            return scope.enter_context(nc.sbuf_tensor(name, shape, dt))

        bank = [ctx.enter_context(nc.psum_tensor(f"bank{i}", [P, 512], F32)) for i in range(8)]

        h_all = sb("h_all", [P, IMAGES * TT, COLS])
        ident = sb("ident", [P, P])
        minus_half = sb("minus_half", [P, TT])
        carrier = sb("carrier", [P, 1])

        a_scope = ctx.enter_context(ExitStack())
        a = lambda name, shape, dt=F32: sb(name, shape, dt, a_scope)
        w_hi = a("w_hi", [P, CT, GROUPS, GROUP_COLS], F32R)
        w_lo = a("w_lo", [P, CT, GROUPS, GROUP_COLS], F32R)
        wo_hi = a("wo_hi", [P, PAIRS, COLS], F32R)
        wo_lo = a("wo_lo", [P, PAIRS, COLS], F32R)
        rope_t = a("rope_t", [P, 2, 3, ROWS])
        mask_t = a("mask_t", [P, BLOCKS, KEYS])
        row_t = a("row_t", [P, 3, P])
        edge_t = a("edge_t", [6, P])
        taps = a("taps", [P, 2, 3, 3])
        edge_taps = a("edge_taps", [6, 2])
        band = a("band", [P, 2, 3, P])
        edge_band = a("edge_band", [6, 2, P])
        x_in = a("x_in", [P, CHANNELS, TT, COLS])
        gray = a("gray", [P, TT, COLS + 2])
        halo = a("halo", [6, TT, COLS])
        abs_e = a("abs_e", [P, 2, TT, COLS])
        stats = a("stats", [P, TT, 6])
        moments = a("moments", [P, TT, 2])
        spread = a("spread", [P, TT])
        rstd = a("rstd", [P, TT])
        xn = a("xn", [P, TT, COLS])
        x_hi = a("x_hi", [P, CT, ROWS], F32R)
        x_lo = a("x_lo", [P, CT, ROWS], F32R)
        own_part = a("own_part", [P, 2, 2, ROWS])
        other_part = a("other_part", [P, 2, 2, ROWS])
        rotated = a("rotated", [P, 2, 2, 2, ROWS])
        qk = a("qk", [P, PAIRS, 2, ROWS])
        v = a("v", [P, GROUPS, TT, 4 * HEAD_DIM])
        v_cross = a("v_cross", [P, GROUPS, 4 * HEAD_DIM])
        masked = a("masked", [P, 2, BLOCKS, KEYS])
        neg_max = a("neg_max", [P, 2, BLOCKS])
        prob = a("prob", [P, 2, BLOCKS, KEYS])
        total = a("total", [P, 2, BLOCKS])
        inv_total = a("inv_total", [P, 2, BLOCKS])
        prob_t = a("prob_t", [P, 2, BLOCKS, P])
        o_hi = a("o_hi", [P, 2, ROWS], F32R)
        o_lo = a("o_lo", [P, 2, ROWS], F32R)

        scores_bank = bank[0:2]
        q_bank, k_bank = bank[2], bank[3]
        v_bank, o_bank, out_bank, misc_bank = bank[4], bank[5], bank[6], bank[7]

        taps_loaded = sem("taps_loaded")
        const_loaded = sem("const_loaded")
        minus_half_set = sem("minus_half_set")
        borders_zero = sem("borders_zero")
        band_part = sem("band_part")
        band_ready = sem("band_ready")
        raw_loaded = [sem(f"raw_loaded{i}") for i in range(RAW_SLOTS)]
        w_hi_ready = sem("w_hi_ready")
        w_lo_ready = sem("w_lo_ready")
        x_loaded = sem("x_loaded")
        gray_first = sem("gray_first")
        gray_second = sem("gray_second")
        gray_done = sem("gray_done")
        halo_loaded = sem("halo_loaded")
        conv_done = sem("conv_done")
        abs_done = sem("abs_done")
        h_done = sem("h_done")
        stats_done = sem("stats_done")
        moments_done = sem("moments_done")
        spread_done = sem("spread_done")
        rstd_done = sem("rstd_done")
        xn_done = sem("xn_done")
        xt_done = sem("xt_done")
        x_hi_done = sem("x_hi_done")
        x_lo_done = sem("x_lo_done")
        qk_done = sem("qk_done")
        rope_mul = sem("rope_mul")
        rope_add = sem("rope_add")
        moved = [sem(f"moved{g}") for g in range(GROUPS)]
        v_done = sem("v_done")
        v_evac = sem("v_evac")
        v_crossed = [sem(f"v_crossed{g}") for g in range(GROUPS)]
        s_done = sem("s_done")
        masked_done = sem("masked_done")
        max_done = sem("max_done")
        exp_done = sem("exp_done")
        recip_done = sem("recip_done")
        norm_done = sem("norm_done")
        t_done = sem("t_done")
        pt_evac = sem("pt_evac")
        o_done = sem("o_done")
        o_hi_done = sem("o_hi_done")
        o_lo_done = sem("o_lo_done")
        out_done = sem("out_done")
        resid_done = sem("resid_done")
        stored = sem("stored")

        TAPS, CONSTS = 5, 3

        CHUNKS = CT * GROUPS + PAIRS // 2
        qk_space = qk[:, :, :, :].rearrange("p a b c -> p (a b c)")
        raw_slot = [qk_space[:, i * GROUP_COLS:(i + 1) * GROUP_COLS] for i in range(RAW_SLOTS)]

        def raw_chunk(n):
            slot = raw_slot[n % RAW_SLOTS]
            if n < CT * GROUPS:
                g, ct = n // CT, n % CT
                return (w_qkv[ct * P:(ct + 1) * P, g, :], slot[:, 0:GROUP_COLS], w_hi[:, ct, g, :], w_lo[:, ct, g, :])
            pair = 2 * (n - CT * GROUPS)
            return (w_out[pair * P:(pair + 2) * P, :].rearrange("(a p) c -> p a c", p=P),
                    slot[:, 0:2 * COLS].rearrange("p (a c) -> p a c", a=2),
                    wo_hi[:, pair:pair + 2, :], wo_lo[:, pair:pair + 2, :])

        def tiles(image):
            return bass.ds(image * TT, TT)

        def bodies(eng, body):
            body(0, True, True)
            with eng.Fori(1, IMAGES - 2) as n:
                body(n, True, True)
            body(IMAGES - 2, True, False)
            body(IMAGES - 1, False, False)

        def bodies_a(eng, body):
            body(0, True, True, True)
            with eng.Fori(1, IMAGES - 3) as n:
                body(n, True, True, True)
            body(IMAGES - 3, True, True, False)
            body(IMAGES - 2, True, False, False)
            body(IMAGES - 1, False, False, False)

        block = ctx.enter_context(nc.Block())

        @block.sync
        def _(sp):
            def load_halo(f):
                sp.wait_ge(gray_done, f + 1)
                positive(sp, conv_done, 2 * f)
                for k, (p, t) in enumerate(((0, 1), (P - 1, 0))):
                    src = gray[p:p + 1, t, 0:COLS]
                    shifted = bass.AP(tensor=src.tensor, offset=src.offset, ap=[list(src.ap[0]), [1, 3], [1, COLS]])
                    sp.dma_start(halo[3 * k:3 * k + 3, k, :], shifted).then_inc(halo_loaded, 16)

            def move_rotated(m, g):
                sp.wait_ge(rope_add, 2 * (GROUPS * m + g) + 2)
                for j in range(4):
                    for half in range(2):
                        to = HEAD_DIM * (j % 2) + HALF * half
                        sp.dma_start(qk[to:to + HALF, 2 * g + j // 2, :, :],
                                     rotated[HALF * j:HALF * (j + 1), g % 2, :, half, :]).then_inc(moved[g], 16)

            def move_values(m, g):
                sp.wait_ge(v_evac, GROUPS * m + g + 1)
                sp.dma_start(v_cross[0:WINDOW, g, :], v[0:WINDOW, g, 1, :]).then_inc(v_crossed[g], 16)
                sp.dma_start(v_cross[WINDOW:P, g, :], v[WINDOW:P, g, 0, :]).then_inc(v_crossed[g], 16)

            def load_chunk(n):
                if n >= RAW_SLOTS:
                    sp.wait_ge(w_hi_ready, n - RAW_SLOTS + 1)
                    sp.wait_ge(w_lo_ready, n - RAW_SLOTS + 1)
                src, slot, _, _ = raw_chunk(n)
                sp.dma_start(slot, src).then_inc(raw_loaded[n % RAW_SLOTS], 16)

            sp.dma_start(taps[:, :, :, :].rearrange("p a b c -> p (a b c)"),
                         scharr.rearrange("a o b c -> (a o b c)").partition_broadcast(P)).then_inc(taps_loaded, 16)
            sp.dma_start(row_t[:, :, :], row).then_inc(taps_loaded, 16)
            sp.dma_start(edge_t[:, :], edge).then_inc(taps_loaded, 16)
            for k, dy in enumerate((2, 0)):
                sp.dma_start(edge_taps[3 * k:3 * k + 3, :],
                             scharr_last[dy, :, :]).then_inc(taps_loaded, 16)
            load_chunk(0)
            load_chunk(1)
            sp.dma_start(ident[:, :], identity).then_inc(const_loaded, 16)
            load_halo(0)
            load_chunk(2)
            load_chunk(3)
            sp.dma_start(rope_t[:, :, :, :], rope).then_inc(const_loaded, 16)
            sp.dma_start(mask_t[:, :, :], mask).then_inc(const_loaded, 16)
            for n in range(4, CHUNKS):
                load_chunk(n)
            load_halo(1)
            for g in range(GROUPS):
                move_rotated(0, g)
                move_values(0, g)

            def body(n, project, edges, load):
                for g in range(GROUPS):
                    if edges and g == 0:
                        load_halo(n + 2)
                    if project:
                        move_rotated(n + 1, g)
                        move_values(n + 1, g)
            bodies_a(sp, body)
            if stop_after_a:
                sp.wait_ge(resid_done, IMAGES)
                sp.dma_start(out.rearrange("b (t p) c -> p (b t) c", p=P), h_all[:, :, :]).then_inc(stored, 16)
                sp.wait_ge(stored, 16)

        @block.gpsimd
        def _(pool):
            nc.gpsimd.memset(minus_half[:, :], -0.5).then_inc(minus_half_set, 1)
            pool.wait_ge(minus_half_set, 1)

            def add_edges(f):
                pool.wait_ge(abs_done, 2 * f + 2)
                nc.gpsimd.tensor_tensor(h_all[:, tiles(f), :], abs_e[:, 0, :, :], abs_e[:, 1, :, :],
                                        ALU.add).then_inc(h_done, 1)

            def inverse_root(f):
                pool.wait_ge(spread_done, f + 1)
                nc.gpsimd.tensor_tensor(rstd[:, :], spread[:, :], minus_half[:, :], ALU.pow).then_inc(rstd_done, 1)

            def rotate(m, g, which):
                pool.wait_ge(rope_mul, 2 * (GROUPS * m + g) + which + 1)
                if which == 0:
                    if g >= 2:
                        pool.wait_ge(moved[g - 2], 16 * MOVES * (m + 1))
                    else:
                        positive(pool, moved[g + 2], 16 * MOVES * m)
                nc.gpsimd.tensor_tensor(rotated[:, g % 2, which, :, :], own_part[:, which, :, :],
                                        other_part[:, which, :, :], ALU.add).then_inc(rope_add, 1)

            def normalise(n, p):
                pool.wait_ge(recip_done, PAIRS * n + p + 1)
                nc.gpsimd.tensor_tensor(prob[:, p % 2, :, :], prob[:, p % 2, :, :],
                                        inv_total[:, p % 2, :].unsqueeze(2).to_broadcast([P, BLOCKS, KEYS]),
                                        ALU.mult).then_inc(norm_done, 1)

            add_edges(0)
            inverse_root(0)
            for g in range(GROUPS):
                if g == 2:
                    add_edges(1)
                rotate(0, g, 0)
                rotate(0, g, 1)
                if g == 2:
                    inverse_root(1)
            normalise(0, 0)

            def body(n, project, edges, load):
                for p in range(PAIRS):
                    if project:
                        rotate(n + 1, p // 2, p % 2)
                    if project or p < PAIRS - 1:
                        normalise(n, p + 1)
                    if edges and p == 2:
                        add_edges(n + 2)
                    if edges and p == 4:
                        inverse_root(n + 2)
            bodies_a(pool, body)

        @block.scalar
        def _(act):
            def load_image(f):
                positive(act, gray_done, f)
                act.dma_start(x_in[:, :, :, :], x[f].rearrange("c (t p) w -> p c t w", p=P)).then_inc(x_loaded, 16)

            def gray_red(f):
                act.wait_ge(x_loaded, 16 * (f + 1))
                positive(act, conv_done, 2 * f)
                positive(act, halo_loaded, 32 * f)
                nc.scalar.activation(gray[:, :, 1:COLS + 1], x_in[:, 0, :, :], ACT.Copy,
                                     scale=GRAY[0]).then_inc(gray_first, 1)

            def edge_size(f, which):
                act.wait_ge(conv_done, 2 * f + which + 1)
                if which == 0:
                    positive(act, h_done, f)
                src = (v_bank, misc_bank)[which]
                nc.scalar.activation(abs_e[:, which, :, :], src[:, :].rearrange("p (t c) -> p t c", t=TT),
                                     ACT.Abs, scale=0.5).then_inc(abs_done, 1)

            def split_x(f):
                act.wait_ge(xt_done, f + 1)
                positive(act, v_done, GROUPS * f)
                nc.scalar.activation(x_hi[:, :, :], misc_bank[:, :].rearrange("p (t c) -> p t c", t=CT),
                                     ACT.Copy).then_inc(x_hi_done, 1)

            def values(m, g):
                act.wait_ge(v_done, GROUPS * m + g + 1)
                positive(act, o_done, PAIRS * (m - 1) + 2 * g + 2)
                nc.scalar.activation(v[:, g, :, :], v_bank[:, :].rearrange("p (t c) -> p t c", t=TT),
                                     ACT.Copy).then_inc(v_evac, 1)

            def exponent(n, p, blocks):
                if blocks[0] == 0:
                    act.wait_ge(max_done, PAIRS * n + p + 1)
                    positive(act, t_done, PAIRS * n + p - 1)
                for b in blocks:
                    last = nc.scalar.activation(prob[:, p % 2, b, :], masked[:, p % 2, b, :], ACT.Exp,
                                                bias=neg_max[:, p % 2, b:b + 1],
                                                accum_out=total[:, p % 2, b:b + 1])
                if blocks[-1] == BLOCKS - 1:
                    last.then_inc(exp_done, 1)

            def transposed(n, p):
                act.wait_ge(t_done, PAIRS * n + p + 1)
                positive(act, o_done, PAIRS * n + p - 1)
                nc.scalar.activation(prob_t[:, p % 2, :, :],
                                     scores_bank[p % 2][:, :].rearrange("p (b c) -> p b c", b=BLOCKS),
                                     ACT.Copy).then_inc(pt_evac, 1)

            def split_o(n, p):
                act.wait_ge(o_done, PAIRS * n + p + 1)
                nc.scalar.activation(o_hi[:, p % 2, :], o_bank[:, (p % 2) * ROWS:(p % 2 + 1) * ROWS],
                                     ACT.Copy).then_inc(o_hi_done, 1)

            act.dma_start(x_in[:, :, :, :], x[0].rearrange("c (t p) w -> p c t w", p=P)).then_inc(x_loaded, 16)
            gray_red(0)
            load_image(1)
            for n in range(CHUNKS):
                act.wait_ge(raw_loaded[n % RAW_SLOTS], 16 * (n // RAW_SLOTS + 1))
                _, slot, hi, _ = raw_chunk(n)
                nc.scalar.activation(hi, slot, ACT.Copy).then_inc(w_hi_ready, 1)
                if n == 3:
                    edge_size(0, 0)
                    edge_size(0, 1)
                    gray_red(1)
                if n == 7:
                    load_image(2)
                    split_x(0)
            values(0, 0)
            values(0, 1)
            edge_size(1, 0)
            edge_size(1, 1)
            values(0, 2)
            values(0, 3)
            split_x(1)
            exponent(0, 0, range(BLOCKS))

            def body(n, project, edges, load):
                for p in range(PAIRS):
                    following = project or p < PAIRS - 1
                    if edges and p == 0:
                        gray_red(n + 2)
                    if edges and p == 2:
                        exponent(n, p + 1, range(BLOCKS))
                        edge_size(n + 2, 0)
                        edge_size(n + 2, 1)
                        transposed(n, p)
                    else:
                        if following:
                            exponent(n, p + 1, range(0, 2))
                        transposed(n, p)
                        if edges and p == PAIRS - 1:
                            split_x(n + 2)
                        if following:
                            exponent(n, p + 1, range(2, BLOCKS))
                    split_o(n, p)
                    if project and p % 2:
                        values(n + 1, p // 2)
                    if load and p == 2:
                        load_image(n + 3)
            bodies_a(act, body)

        @block.vector
        def _(dve):
            def gray_green(f):
                dve.wait_ge(gray_first, f + 1)
                nc.vector.scalar_tensor_tensor(out=gray[:, :, 1:COLS + 1], in0=x_in[:, 1, :, :], scalar=GRAY[1],
                                               in1=gray[:, :, 1:COLS + 1], op0=ALU.mult,
                                               op1=ALU.add).then_inc(gray_second, 1)

            def gray_blue(f):
                dve.wait_ge(gray_second, f + 1)
                nc.vector.scalar_tensor_tensor(out=gray[:, :, 1:COLS + 1], in0=x_in[:, 2, :, :], scalar=GRAY[2],
                                               in1=gray[:, :, 1:COLS + 1], op0=ALU.mult,
                                               op1=ALU.add).then_inc(gray_done, 1)

            def layer_stats(f):
                dve.wait_ge(h_done, f + 1)
                for t in range(TT):
                    last = nc.vector.bn_stats(stats[:, t, :], h_all[:, bass.ds(f * TT + t, 1), :])
                last.then_inc(stats_done, 1)

            def layer_moments(f):
                dve.wait_ge(stats_done, f + 1)
                nc.vector.memset(carrier[:, :], 0.0)
                for t in range(TT):
                    last = nc.vector.bn_aggr(moments[:, t, :], stats[:, t, :])
                last.then_inc(moments_done, 1)
                dve.wait_ge(moments_done, f + 1)
                nc.vector.tensor_scalar(spread[:, :], moments[:, :, 1], 1.0 + RMS_EPS, LN_EPS * RMS_EPS,
                                        ALU.mult, ALU.add).then_inc(spread_done, 1)

            def layer_norm(f):
                dve.wait_ge(rstd_done, f + 1)
                positive(dve, xt_done, f)
                for t in range(TT):
                    last = nc.vector.tensor_scalar(xn[:, t:t + 1, :], h_all[:, bass.ds(f * TT + t, 1), :],
                                                   moments[:, t, 0:1], rstd[:, t:t + 1],
                                                   ALU.subtract, ALU.mult)
                last.then_inc(xn_done, 1)

            def split_x(f):
                dve.wait_ge(x_hi_done, f + 1)
                nc.vector.tensor_tensor(x_lo[:, :, :], misc_bank[:, :].rearrange("p (t c) -> p t c", t=CT),
                                        x_hi[:, :, :].bitcast(F32), ALU.subtract).then_inc(x_lo_done, 1)

            def rotate(m, g, which):
                src = (q_bank, k_bank)[which][:, :].rearrange("p (a c) -> p a c", a=2)
                done = 2 * (GROUPS * m + g) + which
                dve.wait_ge(qk_done, done + 1)
                positive(dve, rope_add, done - 1)
                nc.vector.tensor_tensor(own_part[:, which, :, :], src,
                                        rope_t[:, which, 0:1, :].to_broadcast([P, 2, ROWS]), ALU.mult)
                nc.vector.tensor_tensor(other_part[:, which, :, :], reversed_halves(src),
                                        rope_t[:, which, 1:3, :], ALU.mult).then_inc(rope_mul, 1)

            def mask_scores(n, p):
                done = PAIRS * n + p
                dve.wait_ge(s_done, done + 1)
                positive(dve, exp_done, done - 1)
                nc.vector.tensor_tensor(masked[:, p % 2, :, :],
                                        scores_bank[p % 2][:, :].rearrange("p (b c) -> p b c", b=BLOCKS),
                                        mask_t[:, :, :], ALU.add).then_inc(masked_done, 1)

            def row_max(n, p):
                dve.wait_ge(masked_done, PAIRS * n + p + 1)
                nc.vector.tensor_reduce(neg_max[:, p % 2, :], masked[:, p % 2, :, :], AX_X, ALU.max,
                                        negate=True).then_inc(max_done, 1)

            def inverse_total(n, p):
                dve.wait_ge(exp_done, PAIRS * n + p + 1)
                positive(dve, norm_done, PAIRS * n + p - 1)
                nc.vector.reciprocal(inv_total[:, p % 2, :], total[:, p % 2, :]).then_inc(recip_done, 1)

            def split_o(n, p):
                dve.wait_ge(o_hi_done, PAIRS * n + p + 1)
                nc.vector.tensor_tensor(o_lo[:, p % 2, :], o_bank[:, (p % 2) * ROWS:(p % 2 + 1) * ROWS],
                                        o_hi[:, p % 2, :].bitcast(F32), ALU.subtract).then_inc(o_lo_done, 1)

            def residual(n):
                dve.wait_ge(out_done, n + 1)
                nc.vector.tensor_tensor(h_all[:, tiles(n), :], out_bank[:, :].rearrange("p (t c) -> p t c", t=TT),
                                        h_all[:, tiles(n), :], ALU.add).then_inc(resid_done, 1)

            nc.vector.memset(gray[:, :, 0:1], 0.0)
            nc.vector.memset(gray[:, :, COLS + 1:COLS + 2], 0.0)
            nc.vector.memset(halo[:, :, :], 0.0).then_inc(borders_zero, 1)
            dve.wait_ge(taps_loaded, 16 * TAPS)
            for f in range(2):
                nc.vector.tensor_scalar(edge_band[:, f, :], edge_t[:, :], edge_taps[:, f:f + 1], None, ALU.mult)
            for dy in range(3):
                if dy:
                    dve.wait_ge(band_part, dy)
                for f in range(2):
                    for dx in range(3):
                        tap = taps[:, f, dy, dx:dx + 1]
                        if dy == 0:
                            last = nc.vector.tensor_scalar(band[:, f, dx, :], row_t[:, 0, :], tap, None, ALU.mult)
                        else:
                            last = nc.vector.scalar_tensor_tensor(
                                out=band[:, f, dx, :], in0=row_t[:, dy, :], scalar=tap, in1=band[:, f, dx, :],
                                op0=ALU.mult, op1=ALU.add)
                last.then_inc(band_part if dy < 2 else band_ready, 1)
                if dy == 0:
                    gray_green(0)
                if dy == 1:
                    gray_blue(0)
            for n in range(CHUNKS):
                dve.wait_ge(w_hi_ready, n + 1)
                _, slot, hi, lo = raw_chunk(n)
                nc.vector.tensor_tensor(lo, slot, hi.bitcast(F32), ALU.subtract).then_inc(w_lo_ready, 1)
                if n == 3:
                    layer_stats(0)
                    layer_moments(0)
                    gray_green(1)
                    gray_blue(1)
                if n == 5:
                    layer_norm(0)
                if n == 7:
                    split_x(0)
            dve.wait_ge(const_loaded, 16 * CONSTS)
            for g in range(GROUPS):
                rotate(0, g, 0)
                if g == 2:
                    layer_stats(1)
                    layer_moments(1)
                rotate(0, g, 1)
                if g == 2:
                    layer_norm(1)
            split_x(1)
            for p in range(2):
                mask_scores(0, p)
                row_max(0, p)
            inverse_total(0, 0)

            def body(n, project, edges, load):
                for p in range(PAIRS):
                    following = project or p < PAIRS - 1
                    if p:
                        split_o(n, p - 1)
                        if following:
                            mask_scores(n, p + 1)
                            row_max(n, p + 1)
                    if project:
                        rotate(n + 1, p // 2, p % 2)
                    if edges and p == PAIRS - 1:
                        split_x(n + 2)
                    if following:
                        inverse_total(n, p + 1)
                    if edges and p == 0:
                        gray_green(n + 2)
                    if edges and p == 1:
                        gray_blue(n + 2)
                    if edges and p == 3:
                        layer_stats(n + 2)
                    if edges and p == 4:
                        layer_moments(n + 2)
                    if edges and p == 5:
                        layer_norm(n + 2)
                split_o(n, PAIRS - 1)
                if project:
                    mask_scores(n, PAIRS + 1)
                    row_max(n, PAIRS + 1)
                residual(n)
            bodies_a(dve, body)

        @block.tensor
        def _(pe):
            def convolve(f, values_before):
                pe.wait_ge(gray_done, f + 1)
                positive(pe, x_lo_done, f)
                for which in range(2):
                    dst = (v_bank, misc_bank)[which]
                    if which == 0:
                        positive(pe, v_evac, values_before)
                    for dx in range(3):
                        nc.tensor.matmul(dst[:, :], band[:, which, dx, :], gray[:, :, dx:dx + COLS],
                                         start=(dx == 0), stop=False)
                pe.wait_ge(halo_loaded, 32 * (f + 1))
                for which in range(2):
                    nc.tensor.matmul((v_bank, misc_bank)[which][:, :], edge_band[:, which, :], halo[:, :, :],
                                     start=False, stop=True).then_inc(conv_done, 1)

            def transpose_x(f):
                pe.wait_ge(xn_done, f + 1)
                for ct in range(CT):
                    for t in range(TT):
                        last = nc.tensor.transpose(misc_bank[:, ct * ROWS + t * P:ct * ROWS + (t + 1) * P],
                                                   xn[:, t, ct * P:(ct + 1) * P], ident[:, :])
                last.then_inc(xt_done, 1)

            def three_passes(dst, stationary, moving, terms, **flags):
                passes = [(s, m) for k in range(terms) for s, m in ((0, 0), (0, 1), (1, 0))]
                for i, (s, m) in enumerate(passes):
                    k = i // 3
                    last = nc.tensor.matmul(dst, stationary[s](k), moving[m](k),
                                            start=(i == 0), stop=(i == len(passes) - 1), **flags)
                return last

            def project_qk(m, g, which):
                if g == 0 and which == 0:
                    pe.wait_ge(x_lo_done, m + 1)
                dst = (q_bank, k_bank)[which]
                positive(pe, rope_mul, 2 * (GROUPS * m + g) + which - 1)
                for half in range(2):
                    at = (2 * which + half) * P
                    last = three_passes(
                        dst[:, half * ROWS:(half + 1) * ROWS],
                        [lambda k, w=w: w[:, k, g, at:at + P] for w in (w_hi, w_lo)],
                        [lambda k, t=t: t[:, k, :] for t in (x_hi, x_lo)], CT)
                last.then_inc(qk_done, 1)

            def project_v(m, g, t, edges):
                if t == 0:
                    positive(pe, v_evac, GROUPS * m + g)
                    if edges:
                        pe.wait_ge(abs_done, 2 * (m + 1) + 1)
                at = 4 * P
                last = three_passes(
                    v_bank[:, t * COLS:(t + 1) * COLS],
                    [lambda k, s=s: s[:, k, t * P:(t + 1) * P] for s in (x_hi, x_lo)],
                    [lambda k, w=w: w[:, k, g, at:at + 4 * HEAD_DIM] for w in (w_hi, w_lo)], CT)
                if t == TT - 1:
                    last.then_inc(v_done, 1)

            def scores(n, p):
                pair = p % PAIRS
                for b in range(BLOCKS):
                    for head in range(2):
                        rows = slice(HEAD_DIM * head, HEAD_DIM * (head + 1))
                        if b % 2 or b == 0:
                            first = key_of(b, 0)
                            keys = qk[rows, pair, 1, first:first + KEYS]
                        else:
                            own = qk[rows, pair, 1, WINDOW * b:WINDOW * (b + 1)]
                            keys = bass.AP(tensor=own.tensor, offset=own.offset,
                                           ap=[list(own.ap[0]), [-WINDOW, 2], [1, WINDOW]])
                        last = nc.tensor.matmul(scores_bank[p % 2][rows, b * KEYS:(b + 1) * KEYS],
                                                qk[rows, pair, 0, WINDOW * b:WINDOW * (b + 1)], keys,
                                                start=True, stop=True)
                last.then_inc(s_done, 1)

            def in_place(n, g):
                pe.wait_ge(moved[g], 16 * MOVES * (n + 1))

            def transpose_p(n, p):
                pe.wait_ge(norm_done, PAIRS * n + p + 1)
                for b in range(BLOCKS):
                    last = nc.tensor.transpose(scores_bank[p % 2][:, b * P:(b + 1) * P], prob[:, p % 2, b, :],
                                               ident[:, :])
                last.then_inc(t_done, 1)

            def attend(n, p):
                g = p // 2
                if p % 2 == 0:
                    pe.wait_ge(v_evac, GROUPS * n + g + 1)
                    pe.wait_ge(v_crossed[g], 32 * (n + 1))
                positive(pe, o_lo_done, PAIRS * n + p)
                pe.wait_ge(pt_evac, PAIRS * n + p + 1)
                for b in range(BLOCKS):
                    for head in range(2):
                        at = HEAD_DIM * (2 * (p % 2) + head)
                        vals = v_cross[:, g, at:at + HEAD_DIM] if b == 2 else v[:, g, b // 2, at:at + HEAD_DIM]
                        to = (p % 2) * ROWS + WINDOW * b
                        last = nc.tensor.matmul(
                            o_bank[HEAD_DIM * head:HEAD_DIM * (head + 1), to:to + WINDOW], vals,
                            prob_t[:, p % 2, b, HEAD_DIM * head:HEAD_DIM * (head + 1)], start=True, stop=True)
                last.then_inc(o_done, 1)

            def project_out(n, p):
                pe.wait_ge(o_lo_done, PAIRS * n + p + 1)
                if p == 0:
                    positive(pe, resid_done, n)
                for t in range(TT):
                    for s, w in ((o_hi, wo_hi), (o_hi, wo_lo), (o_lo, wo_hi)):
                        first = p == 0 and t == 0 and w is wo_hi and s is o_hi
                        last = nc.tensor.matmul(out_bank[:, t * COLS:(t + 1) * COLS],
                                                s[:, p % 2, t * P:(t + 1) * P], w[:, p, :],
                                                start=first, stop=(p == PAIRS - 1), skip_group_check=True)
                if p == PAIRS - 1:
                    last.then_inc(out_done, 1)

            pe.wait_ge(borders_zero, 1)
            pe.wait_ge(band_ready, 1)
            convolve(0, 0)
            pe.wait_ge(const_loaded, 16 * CONSTS)
            transpose_x(0)
            for g in range(GROUPS):
                pe.wait_ge(w_lo_ready, CT * (g + 1))
                project_qk(0, g, 0)
                project_qk(0, g, 1)
                if g == 0:
                    pe.wait_ge(abs_done, 1)
                for t in range(TT):
                    project_v(0, g, t, g == 2)
                if g == 1:
                    convolve(1, 2)
            pe.wait_ge(w_lo_ready, CHUNKS)
            in_place(0, 0)
            transpose_x(1)
            scores(0, 0)
            scores(0, 1)

            def body(n, project, edges, load):
                for p in range(PAIRS):
                    g, part = p // 2, p % 2
                    if p and (project or p < PAIRS - 1):
                        scores(n, p + 1)
                    if edges and p == 2:
                        convolve(n + 2, GROUPS * (n + 1) + g)
                    if project:
                        project_qk(n + 1, g, part)
                        if p == PAIRS - 1:
                            project_v(n + 1, g, part, False)
                    if part == 0 and (project or g < GROUPS - 1):
                        in_place(n + (g + 1) // GROUPS, (g + 1) % GROUPS)
                    transpose_p(n, p)
                    if project and p < PAIRS - 1:
                        project_v(n + 1, g, part, edges and p == 2)
                    if p:
                        project_out(n, p - 1)
                    if edges and p == PAIRS - 2:
                        transpose_x(n + 2)
                    attend(n, p)
                if project:
                    scores(n, PAIRS + 1)
                project_out(n, PAIRS - 1)
            bodies_a(pe, body)


        a_scope.close()
        b_ = lambda name, shape, dt=F32: sb(name, shape, dt)
        me_hi = b_("me_hi", [P, EXPERTS, CT, EXPERT_COLS], F32R)
        me_lo = b_("me_lo", [P, EXPERTS, CT, EXPERT_COLS], F32R)
        mo_hi = b_("mo_hi", [P, EXPERTS, COLS], F32R)
        mo_lo = b_("mo_lo", [P, EXPERTS, COLS], F32R)
        raw = b_("raw", [P, 2, 4 * COLS])
        sim_t = b_("sim_t", [P, CT, EXPERTS])
        sim_sq = b_("sim_sq", [P, CT, EXPERTS])
        ones = b_("ones", [P, P])
        expert_no = b_("expert_no", [P, EXPERTS])
        gate_t = b_("gate_t", [P, EXPERTS])
        m_stats = b_("m_stats", [P, TT, 6])
        m_moments = b_("m_moments", [P, TT, 2])
        m_spread = b_("m_spread", [P, TT])
        m_rstd = b_("m_rstd", [P, TT])
        m_square = b_("m_square", [P, TT])
        m_rnorm = b_("m_rnorm", [P, TT])
        m_xn = b_("m_xn", [P, TT, COLS])
        m_x = b_("m_x", [P, CT, ROWS])
        mx_hi = b_("mx_hi", [P, CT, ROWS], F32R)
        mx_lo = b_("mx_lo", [P, CT, ROWS], F32R)
        logit = b_("logit", [P, TT, EXPERTS])
        gated = b_("gated", [P, TT, EXPERTS])
        active = b_("active", [P, TT, EXPERTS])
        fallback = b_("fallback", [P, TT, EXPERTS])
        idle = b_("idle", [P, TT])
        top = b_("top", [P, TT, 8])
        top_at = b_("top_at", [P, TT, 8], U32)
        top_no = b_("top_no", [P, TT, 2])
        row_stat = b_("row_stat", [P, TT])
        share = b_("share", [P, 3, TT, EXPERTS])
        share_n = b_("share_n", [P, TT, EXPERTS])
        part = b_("part", [P, TT, EXPERT_COLS])
        qkv = b_("qkv", [P, TT, EXPERT_COLS])
        qkt = b_("qkt", [P, 2, ROWS])
        m_bias = b_("m_bias", [P, 2, TT])
        m_prob = b_("m_prob", [P, TT, ROWS])
        m_total = b_("m_total", [P, TT])
        m_inv = b_("m_inv", [P, TT])
        m_prob_t = b_("m_prob_t", [P, TT, ROWS])
        mo_t_hi = b_("mo_t_hi", [P, ROWS], F32R)
        mo_t_lo = b_("mo_t_lo", [P, ROWS], F32R)
        out_part = b_("out_part", [P, TT, COLS])
        result = b_("result", [P, TT, COLS])

        chunk_bank = bank[0:4]
        down_bank = bank[4:6]
        turn_bank, attn_bank = bank[6], bank[7]
        logit_ps = turn_bank[:, 0:TT * EXPERTS].rearrange("p (t e) -> p t e", t=TT)

        STEPS = EXPERTS * TT
        DOWNS = EXPERTS // 2 * TT
        M_CHUNKS = EXPERTS + EXPERTS // 4
        
        m_const_loaded = sem("m_const_loaded")
        m_raw_loaded = [sem(f"m_raw_loaded{i}") for i in range(2)]
        ones_set = sem("ones_set")
        m_hi_ready = sem("m_hi_ready")
        m_lo_ready = sem("m_lo_ready")
        gate_exp = sem("gate_exp")
        setup_step = sem("setup_step")
        sim_squared = sem("sim_squared")
        sim_summed_ps = sem("sim_summed_ps")
        sim_summed = sem("sim_summed")
        sim_root = sem("sim_root")
        sim_ready = sem("sim_ready")
        norm_step = sem("norm_step")
        m_spread_done = sem("m_spread_done")
        m_rstd_done = sem("m_rstd_done")
        m_square_done = sem("m_square_done")
        m_rnorm_done = sem("m_rnorm_done")
        m_xn_done = sem("m_xn_done")
        m_xt_done = sem("m_xt_done")
        m_x_done = sem("m_x_done")
        mx_hi_done = sem("mx_hi_done")
        mx_lo_done = sem("mx_lo_done")
        logits_done = sem("logits_done")
        logits_read = sem("logits_read")
        router_step = sem("router_step")
        share_step = sem("share_step")
        router_in = sem("router_in")
        router_exp = sem("router_exp")
        shifted = sem("shifted")
        step_done = sem("step_done")
        combined = sem("combined")
        qk_turned = sem("qk_turned")
        qkt_done = sem("qkt_done")
        m_scores = sem("m_scores")
        m_max = sem("m_max")
        m_bias_done = sem("m_bias_done")
        m_exp = sem("m_exp")
        m_inv_done = sem("m_inv_done")
        share_n_done = sem("share_n_done")
        m_turned = sem("m_turned")
        m_prob_t_done = sem("m_prob_t_done")
        mixed = sem("mixed")
        mo_hi_done = sem("mo_hi_done")
        mo_lo_done = sem("mo_lo_done")
        down_done = sem("down_done")
        down_step = sem("down_step")

        def m_chunk(n):
            slot = raw[:, n % 2, :]
            if n < EXPERTS:
                view = slot[:, 0:CT * EXPERT_COLS].rearrange("p (a c) -> p a c", a=CT)
                return w_moe[:, n, :, :], view, me_hi[:, n, :, :], me_lo[:, n, :, :]
            e = 4 * (n - EXPERTS)
            return (w_moe_out[:, e:e + 4, :], slot.rearrange("p (a c) -> p a c", a=4),
                    mo_hi[:, e:e + 4, :], mo_lo[:, e:e + 4, :])


        @block.sync
        def _(sp):
            sp.wait_ge(resid_done, IMAGES)
            sp.dma_start(sim_t[:, :, :], sim.rearrange("(a p) e -> p a e", p=P)).then_inc(m_const_loaded, 16)
            sp.dma_start(gate_t[:, :], gates.partition_broadcast(P)).then_inc(m_const_loaded, 16)
            sp.dma_start(expert_no[:, :], numbers).then_inc(m_const_loaded, 16)
            for n in range(M_CHUNKS):
                if n >= 2:
                    sp.wait_ge(m_hi_ready, n - 1)
                    sp.wait_ge(m_lo_ready, n - 1)
                src, slot, _, _ = m_chunk(n)
                sp.dma_start(slot, src).then_inc(m_raw_loaded[n % 2], 16)

        @block.gpsimd
        def _(pool):
            pool.wait_ge(resid_done, IMAGES)
            nc.gpsimd.memset(ones[:, :], 1.0).then_inc(ones_set, 1)

            def roots(f):
                pool.wait_ge(m_spread_done, f + 1)
                nc.gpsimd.tensor_tensor(m_rstd[:, :], m_spread[:, :], minus_half[:, :], ALU.pow).then_inc(m_rstd_done, 1)
                pool.wait_ge(m_square_done, f + 1)
                nc.gpsimd.tensor_tensor(m_rnorm[:, :], m_square[:, :], minus_half[:, :], ALU.pow).then_inc(m_rnorm_done, 1)

            roots(0)
            pool.wait_ge(sim_summed, 1)
            nc.gpsimd.tensor_tensor(sim_sq[:, 0, :], sim_sq[:, 1, :],
                                    minus_half[:, 0:1].to_broadcast([P, EXPERTS]), ALU.pow).then_inc(sim_root, 1)
            roots(1)

            def body(b, project, front):
                if front:
                    roots(b + 2)
                pool.wait_ge(down_step, 2 * DOWNS * (b + 1))
                pool.dma_start(out[b].rearrange("(t p) c -> p t c", p=P), result[:, :, :]).then_inc(stored, 16)
            bodies(pool, body)
            pool.wait_ge(stored, 16 * IMAGES)

        @block.scalar
        def _(act):
            def evacuate_x(f):
                act.wait_ge(m_xt_done, f + 1)
                positive(act, logits_done, f)
                positive(act, mx_lo_done, f)
                nc.scalar.activation(m_x[:, :, :], turn_bank[:, :].rearrange("p (a c) -> p a c", a=CT),
                                     ACT.Copy).then_inc(m_x_done, 1)

            def split_x(f):
                positive(act, step_done, STEPS * f)
                act.wait_ge(m_x_done, f + 1)
                nc.scalar.activation(mx_hi[:, :, :], m_x[:, :, :], ACT.Copy).then_inc(mx_hi_done, 1)

            def router_exponent(f):
                act.wait_ge(router_in, f + 1)
                nc.scalar.activation(active[:, :, :], gated[:, :, :], ACT.Exp).then_inc(router_exp, 1)

            act.wait_ge(resid_done, IMAGES)
            act.wait_ge(m_const_loaded, 48)
            nc.scalar.activation(gate_t[:, :], gate_t[:, :], ACT.Exp, scale=-1.0).then_inc(gate_exp, 1)
            for n in range(M_CHUNKS):
                act.wait_ge(m_raw_loaded[n % 2], 16 * (n // 2 + 1))
                _, slot, hi, _ = m_chunk(n)
                nc.scalar.activation(hi, slot, ACT.Copy).then_inc(m_hi_ready, 1)
                if n == 2:
                    evacuate_x(0)
                    split_x(0)
                if n == 4:
                    router_exponent(0)
            evacuate_x(1)
            router_exponent(1)
            split_x(1)

            def body(b, project, front):
                act.wait_ge(qk_turned, b + 1)
                positive(act, m_scores, b)
                nc.scalar.activation(qkt[:, :, :], turn_bank[:, :].rearrange("p (a c) -> p a c", a=2),
                                     ACT.Copy).then_inc(qkt_done, 1)
                act.wait_ge(m_bias_done, b + 1)
                positive(act, m_turned, b)
                for t in range(TT):
                    last = nc.scalar.activation(m_prob[:, t, :], attn_bank[:, t * ROWS:(t + 1) * ROWS], ACT.Exp,
                                                bias=m_bias[:, 1, t:t + 1], scale=SCORE_SCALE,
                                                accum_out=m_total[:, t:t + 1])
                last.then_inc(m_exp, 1)
                act.wait_ge(m_turned, b + 1)
                nc.scalar.activation(m_prob_t[:, :, :], attn_bank[:, :].rearrange("p (a c) -> p a c", a=TT),
                                     ACT.Copy).then_inc(m_prob_t_done, 1)
                act.wait_ge(mixed, b + 1)
                positive(act, down_done, DOWNS * b)
                nc.scalar.activation(mo_t_hi[:, :], attn_bank[:, 0:ROWS], ACT.Copy).then_inc(mo_hi_done, 1)
                if front:
                    evacuate_x(b + 2)
                    router_exponent(b + 2)
                    split_x(b + 2)
            bodies(act, body)

        @block.vector
        def _(dve):
            def statistics(f):
                for t in range(TT):
                    last = nc.vector.bn_stats(m_stats[:, t, :], h_all[:, bass.ds(f * TT + t, 1), :])
                last.then_inc(norm_step, 1)
                dve.wait_ge(norm_step, 4 * f + 1)
                positive(dve, m_rnorm_done, f)
                nc.vector.memset(carrier[:, :], 0.0)
                for t in range(TT):
                    last = nc.vector.bn_aggr(m_moments[:, t, :], m_stats[:, t, :])
                last.then_inc(norm_step, 1)
                dve.wait_ge(norm_step, 4 * f + 2)
                nc.vector.tensor_scalar(m_spread[:, :], m_moments[:, :, 1], LN_EPS, None, ALU.add)\
                    .then_inc(m_spread_done, 1)

            def layer_norm(f):
                dve.wait_ge(m_rstd_done, f + 1)
                nc.vector.tensor_tensor(m_square[:, :], m_rstd[:, :], m_rstd[:, :], ALU.mult).then_inc(norm_step, 1)
                positive(dve, m_xt_done, f)
                for t in range(TT):
                    last = nc.vector.tensor_scalar(m_xn[:, t:t + 1, :], h_all[:, bass.ds(f * TT + t, 1), :],
                                                   m_moments[:, t, 0:1], m_rstd[:, t:t + 1],
                                                   ALU.subtract, ALU.mult)
                last.then_inc(m_xn_done, 1)
                dve.wait_ge(norm_step, 4 * f + 3)
                nc.vector.tensor_tensor(m_square[:, :], m_square[:, :], m_moments[:, :, 1], ALU.mult)\
                    .then_inc(norm_step, 1)
                dve.wait_ge(norm_step, 4 * f + 4)
                nc.vector.tensor_scalar(m_square[:, :], m_square[:, :], float(COLS), 1e-24, ALU.mult, ALU.max)\
                    .then_inc(m_square_done, 1)

            def split_x(f):
                dve.wait_ge(mx_hi_done, f + 1)
                nc.vector.tensor_tensor(mx_lo[:, :, :], m_x[:, :, :], mx_hi[:, :, :].bitcast(F32), ALU.subtract)\
                    .then_inc(mx_lo_done, 1)

            ROUTER_STEPS = 12

            def router(f, section):
                base = ROUTER_STEPS * f

                def after(step):
                    dve.wait_ge(router_step, base + step)

                if section == 0:
                    dve.wait_ge(logits_done, f + 1)
                    dve.wait_ge(m_rnorm_done, f + 1)
                    for t in range(TT):
                        last = nc.vector.scalar_tensor_tensor(
                            out=logit[:, t, :], in0=logit_ps[:, t, :], scalar=m_rnorm[:, t:t + 1],
                            in1=gate_t[:, :], op0=ALU.mult, op1=ALU.subtract)
                    last.then_inc(logits_read, 1)
                    dve.wait_ge(logits_read, f + 1)
                    nc.vector.tensor_scalar(active[:, :, :], logit[:, :, :], 0.0, None, ALU.is_gt)\
                        .then_inc(router_step, 1)
                    for t in range(TT):
                        last = nc.vector.max(top[:, t, :], logit[:, t, :])
                    last.then_inc(router_step, 1)
                    after(2)
                    nc.vector.tensor_reduce(row_stat[:, :], active[:, :, :], AX_X, ALU.max)\
                        .then_inc(router_step, 1)
                    for t in range(TT):
                        last = nc.vector.max_index(top_at[:, t, :], top[:, t, :], logit[:, t, :])
                    last.then_inc(router_step, 1)
                    after(4)
                    nc.vector.tensor_copy(top_no[:, :, :], top_at[:, :, 0:2]).then_inc(router_step, 1)
                    nc.vector.tensor_scalar(idle[:, :], row_stat[:, :], 0.0, None, ALU.is_equal)\
                        .then_inc(router_step, 1)
                    after(5)
                    for t in range(TT):
                        last = nc.vector.tensor_scalar(fallback[:, t, :], expert_no[:, :], top_no[:, t, 0:1], None,
                                                       ALU.is_equal)
                    last.then_inc(router_step, 1)
                    after(7)
                    for t in range(TT):
                        last = nc.vector.scalar_tensor_tensor(
                            out=fallback[:, t, :], in0=expert_no[:, :], scalar=top_no[:, t, 1:2],
                            in1=fallback[:, t, :], op0=ALU.is_equal, op1=ALU.max)
                    last.then_inc(router_step, 1)
                    nc.vector.tensor_scalar(gated[:, :, :], logit[:, :, :], 0.0, None, ALU.max)
                    after(8)
                    for t in range(TT):
                        last = nc.vector.scalar_tensor_tensor(
                            out=active[:, t, :], in0=fallback[:, t, :], scalar=idle[:, t:t + 1],
                            in1=active[:, t, :], op0=ALU.mult, op1=ALU.max)
                    last.then_inc(router_step, 1)
                    after(9)
                    nc.vector.tensor_scalar(fallback[:, :, :], active[:, :, :], 1.0, EXCLUDED, ALU.subtract,
                                            ALU.mult).then_inc(router_step, 1)
                    after(10)
                    nc.vector.tensor_tensor(gated[:, :, :], gated[:, :, :], fallback[:, :, :], ALU.add)\
                        .then_inc(router_step, 1)
                    after(11)
                    nc.vector.tensor_reduce(row_stat[:, :], gated[:, :, :], AX_X, ALU.max)\
                        .then_inc(router_step, 1)
                    after(12)
                    nc.vector.tensor_tensor(gated[:, :, :], gated[:, :, :],
                                            row_stat[:, :].unsqueeze(2).to_broadcast([P, TT, EXPERTS]),
                                            ALU.subtract).then_inc(router_in, 1)
                else:
                    dve.wait_ge(router_exp, f + 1)
                    nc.vector.tensor_reduce(row_stat[:, :], active[:, :, :], AX_X, ALU.add).then_inc(share_step, 1)
                    dve.wait_ge(share_step, 3 * f + 1)
                    nc.vector.reciprocal(idle[:, :], row_stat[:, :]).then_inc(share_step, 1)
                    dve.wait_ge(share_step, 3 * f + 2)
                    nc.vector.tensor_tensor(share[:, 2, :, :], active[:, :, :],
                                            idle[:, :].unsqueeze(2).to_broadcast([P, TT, EXPERTS]),
                                            ALU.mult).then_inc(share_step, 1)

            def shift_shares(f):
                dve.wait_ge(share_step, 3 * f + 3)
                positive(dve, combined, STEPS * f)
                if not (isinstance(f, int) and f == 0):
                    nc.vector.tensor_copy(share[:, 0, :, :], share[:, 1, :, :]).then_inc(shifted, 1)
                    dve.wait_ge(shifted, 2 * f)
                    nc.vector.tensor_copy(share[:, 1, :, :], share[:, 2, :, :]).then_inc(shifted, 1)
                else:
                    nc.vector.tensor_copy(share[:, 1, :, :], share[:, 2, :, :]).then_inc(shifted, 1)
                dve.wait_ge(shifted, 2 * f + 1)

            def combine(m, k):
                e, t = k // TT, k % TT
                done = STEPS * m + k
                dve.wait_ge(step_done, done + 1)
                src = chunk_bank[k % 4][:, 0:EXPERT_COLS]
                by = share[:, 1, t, e:e + 1]
                if e == 0:
                    nc.vector.tensor_scalar(part[:, t, :], src, by, None, ALU.mult).then_inc(combined, 1)
                    return
                dve.wait_ge(combined, done - 1)
                if e == EXPERTS - 1:
                    positive(dve, mixed, m)
                nc.vector.scalar_tensor_tensor(out=(qkv if e == EXPERTS - 1 else part)[:, t, :], in0=src, scalar=by,
                                               in1=part[:, t, :], op0=ALU.mult, op1=ALU.add).then_inc(combined, 1)

            def attention_max(b):
                dve.wait_ge(m_scores, b + 1)
                nc.vector.tensor_reduce(m_bias[:, 0, :], attn_bank[:, :].rearrange("p (t c) -> p t c", t=TT), AX_X,
                                        ALU.max, negate=True).then_inc(m_max, 1)
                dve.wait_ge(m_max, b + 1)
                nc.vector.tensor_scalar(m_bias[:, 1, :], m_bias[:, 0, :], SCORE_SCALE, None, ALU.mult)\
                    .then_inc(m_bias_done, 1)

            def normalise_shares(b):
                dve.wait_ge(m_exp, b + 1)
                nc.vector.reciprocal(m_inv[:, :], m_total[:, :]).then_inc(m_inv_done, 1)
                dve.wait_ge(m_inv_done, b + 1)
                nc.vector.tensor_tensor(share_n[:, :, :], share[:, 0, :, :],
                                        m_inv[:, :].unsqueeze(2).to_broadcast([P, TT, EXPERTS]),
                                        ALU.mult).then_inc(share_n_done, 1)

            def split_mixed(b):
                dve.wait_ge(mo_hi_done, b + 1)
                nc.vector.tensor_tensor(mo_t_lo[:, :], attn_bank[:, 0:ROWS], mo_t_hi[:, :].bitcast(F32),
                                        ALU.subtract).then_inc(mo_lo_done, 1)

            def add_down(b, j):
                t = j % TT
                dve.wait_ge(down_done, DOWNS * b + j + 1)
                if j == 0:
                    dve.wait_ge(share_n_done, b + 1)
                for i in range(2):
                    e = 2 * (j // TT) + i
                    at = 2 * DOWNS * b + 2 * j + i
                    if e == 0:
                        before = h_all[:, bass.ds(b * TT + t, 1), :]
                    else:
                        before = out_part[:, t:t + 1, :]
                        dve.wait_ge(down_step, at if i else at - 2)
                    last_e = e == EXPERTS - 1
                    if last_e and t == 0:
                        positive(dve, stored, 16 * b)
                    ins = nc.vector.scalar_tensor_tensor(
                        out=(result if last_e else out_part)[:, t:t + 1, :],
                        in0=down_bank[j % 2][:, i * COLS:(i + 1) * COLS].unsqueeze(1),
                        scalar=share_n[:, t, e:e + 1], in1=before, op0=ALU.mult, op1=ALU.add)
                    ins.then_inc(down_step, 1)

            statistics(0)
            layer_norm(0)
            dve.wait_ge(gate_exp, 1)
            nc.vector.tensor_scalar(gate_t[:, :], gate_t[:, :], 1.0, None, ALU.add).then_inc(setup_step, 1)
            dve.wait_ge(setup_step, 1)
            nc.vector.reciprocal(gate_t[:, :], gate_t[:, :]).then_inc(setup_step, 1)
            nc.vector.tensor_tensor(sim_sq[:, :, :], sim_t[:, :, :], sim_t[:, :, :], ALU.mult).then_inc(sim_squared, 1)
            dve.wait_ge(sim_summed_ps, 1)
            nc.vector.tensor_scalar(sim_sq[:, 1, :], attn_bank[:, 0:EXPERTS], 1e-24, None, ALU.max)\
                .then_inc(sim_summed, 1)
            dve.wait_ge(sim_root, 1)
            nc.vector.tensor_tensor(sim_t[:, :, :], sim_t[:, :, :],
                                    sim_sq[:, 0:1, :].to_broadcast([P, CT, EXPERTS]), ALU.mult).then_inc(sim_ready, 1)
            dve.wait_ge(setup_step, 2)
            for n in range(EXPERTS):
                dve.wait_ge(m_hi_ready, n + 1)
                _, slot, hi, lo = m_chunk(n)
                nc.vector.tensor_tensor(lo, slot, hi.bitcast(F32), ALU.subtract).then_inc(m_lo_ready, 1)
                if n == 2:
                    split_x(0)
                    router(0, 0)
                if n == 4:
                    router(0, 1)
                    shift_shares(0)
                if n >= 5:
                    for k in range(TT * (n - 5), TT * (n - 4)):
                        combine(0, k)
            for k in range(TT * (EXPERTS - 5), STEPS):
                combine(0, k)
            for n in range(EXPERTS, M_CHUNKS):
                dve.wait_ge(m_hi_ready, n + 1)
                _, slot, hi, lo = m_chunk(n)
                nc.vector.tensor_tensor(lo, slot, hi.bitcast(F32), ALU.subtract).then_inc(m_lo_ready, 1)
            statistics(1)
            layer_norm(1)
            router(1, 0)
            router(1, 1)
            shift_shares(1)
            split_x(1)

            def body(b, project, front):
                for k in range(STEPS):
                    if project:
                        combine(b + 1, k)
                    if k == 3:
                        attention_max(b)
                    if k == 6:
                        normalise_shares(b)
                    if k == 11:
                        split_mixed(b)
                    if front and k == 8:
                        statistics(b + 2)
                    if front and k == 12:
                        layer_norm(b + 2)
                    if front and k == 21:
                        router(b + 2, 0)
                    if front and k == 26:
                        router(b + 2, 1)
                    if 13 <= k < 27:
                        add_down(b, k - 13)
                if front:
                    shift_shares(b + 2)
                    split_x(b + 2)
                elif project:
                    nc.vector.tensor_copy(share[:, 0, :, :], share[:, 1, :, :]).then_inc(shifted, 1)
                    dve.wait_ge(shifted, 2 * (b + 2))
                for j in range(DOWNS - 2, DOWNS):
                    add_down(b, j)
            bodies(dve, body)

        @block.tensor
        def _(pe):
            def transpose_x(f):
                pe.wait_ge(m_xn_done, f + 1)
                positive(pe, qkt_done, f - 1)
                for ct in range(CT):
                    for t in range(TT):
                        last = nc.tensor.transpose(turn_bank[:, ct * ROWS + t * P:ct * ROWS + (t + 1) * P],
                                                   m_xn[:, t, ct * P:(ct + 1) * P], ident[:, :])
                last.then_inc(m_xt_done, 1)

            def logits(f):
                pe.wait_ge(m_x_done, f + 1)
                if isinstance(f, int) and f == 0:
                    pe.wait_ge(sim_ready, 1)
                for t in range(TT):
                    for ct in range(CT):
                        last = nc.tensor.matmul(logit_ps[:, t, :], m_x[:, ct, t * P:(t + 1) * P], sim_t[:, ct, :],
                                                start=(ct == 0), stop=(ct == CT - 1))
                last.then_inc(logits_done, 1)

            def expert_step(m, k):
                e, t = k // TT, k % TT
                if k == 0:
                    pe.wait_ge(mx_lo_done, m + 1)
                positive(pe, combined, STEPS * m + k - 3)
                if isinstance(m, int) and m == 0 and t == 0:
                    pe.wait_ge(m_lo_ready, e + 1)
                dst = chunk_bank[k % 4][:, 0:EXPERT_COLS]
                n = 0
                for ct in range(CT):
                    for s, w in ((mx_hi, me_hi), (mx_hi, me_lo), (mx_lo, me_hi)):
                        last = nc.tensor.matmul(dst, s[:, ct, t * P:(t + 1) * P], w[:, e, ct, :],
                                                start=(n == 0), stop=(n == 3 * CT - 1))
                        n += 1
                last.then_inc(step_done, 1)

            def transpose_qk(b):
                pe.wait_ge(combined, STEPS * (b + 1))
                positive(pe, logits_read, b + 2 if not isinstance(b, int) else min(b + 2, IMAGES))
                for which in range(2):
                    for t in range(TT):
                        last = nc.tensor.transpose(turn_bank[:, which * ROWS + t * P:which * ROWS + (t + 1) * P],
                                                   qkv[:, t, which * P:(which + 1) * P], ident[:, :])
                last.then_inc(qk_turned, 1)

            def token_scores(b):
                pe.wait_ge(qkt_done, b + 1)
                positive(pe, mo_lo_done, b)
                for t in range(TT):
                    last = nc.tensor.matmul(attn_bank[:, t * ROWS:(t + 1) * ROWS], qkt[:, 0, t * P:(t + 1) * P],
                                            qkt[:, 1, :], start=True, stop=True)
                last.then_inc(m_scores, 1)

            def transpose_prob(b):
                pe.wait_ge(m_exp, b + 1)
                for kt in range(TT):
                    for t in range(TT):
                        last = nc.tensor.transpose(attn_bank[:, kt * ROWS + t * P:kt * ROWS + (t + 1) * P],
                                                   m_prob[:, t, kt * P:(kt + 1) * P], ident[:, :])
                last.then_inc(m_turned, 1)

            def mix_values(b):
                pe.wait_ge(m_prob_t_done, b + 1)
                for kt in range(TT):
                    last = nc.tensor.matmul(attn_bank[:, 0:ROWS], qkv[:, kt, 2 * EXPERT_DIM:EXPERT_COLS],
                                            m_prob_t[:, kt, :], start=(kt == 0), stop=(kt == TT - 1))
                last.then_inc(mixed, 1)

            def down_step_pair(b, j):
                e, t = 2 * (j // TT), j % TT
                if j == 0:
                    pe.wait_ge(mo_lo_done, b + 1)
                    if isinstance(b, int) and b == 0:
                        pe.wait_ge(m_lo_ready, M_CHUNKS)
                positive(pe, down_step, 2 * DOWNS * b + 2 * j - 2)
                for i, (s, w) in enumerate(((mo_t_hi, mo_hi), (mo_t_hi, mo_lo), (mo_t_lo, mo_hi))):
                    last = nc.tensor.matmul(down_bank[j % 2][:, :], s[:, t * P:(t + 1) * P], w[:, e:e + 2, :],
                                            start=(i == 0), stop=(i == 2))
                last.then_inc(down_done, 1)

            pe.wait_ge(sim_squared, 1)
            pe.wait_ge(ones_set, 1)
            for ct in range(CT):
                last = nc.tensor.matmul(attn_bank[:, 0:EXPERTS], ones[:, :], sim_sq[:, ct, :],
                                        start=(ct == 0), stop=(ct == CT - 1))
            last.then_inc(sim_summed_ps, 1)
            transpose_x(0)
            logits(0)
            for k in range(STEPS):
                expert_step(0, k)
            transpose_x(1)
            logits(1)

            def body(b, project, front):
                for k in range(STEPS):
                    if project:
                        expert_step(b + 1, k)
                    if k == 1:
                        transpose_qk(b)
                    if k == 3:
                        token_scores(b)
                    if k == 7:
                        transpose_prob(b)
                    if k == 10:
                        mix_values(b)
                    if front and k == 14:
                        transpose_x(b + 2)
                    if front and k == 19:
                        logits(b + 2)
                    if 12 <= k < 26:
                        down_step_pair(b, k - 12)
                for j in range(DOWNS - 2, DOWNS):
                    down_step_pair(b, j)
            bodies(pe, body)


def layouts(x, scharr, w_qkv, w_out, sim, gates, q_proj, k_proj, v_proj, o_proj):
    inner = HEADS * HEAD_DIM
    halves = [w_qkv[k * inner:(k + 1) * inner].reshape(GROUPS, 4, 2, HALF, COLS).transpose(4, 0, 2, 1, 3)
              .reshape(COLS, GROUPS, 4 * HEAD_DIM) for k in range(2)]
    values = w_qkv[2 * inner:].reshape(GROUPS, 4 * HEAD_DIM, COLS).transpose(2, 0, 1)
    experts = np.concatenate([q_proj, k_proj, v_proj], axis=2)
    return {
        "x": x,
        "scharr": scharr,
        "scharr_last": np.ascontiguousarray(scharr[:, 0].transpose(1, 2, 0)),
        "w_qkv": np.ascontiguousarray(np.concatenate(halves + [values], axis=2)),
        "w_out": np.ascontiguousarray(w_out.T),
        "sim": sim,
        "gates": gates,
        "w_moe": np.ascontiguousarray(experts.reshape(EXPERTS, CT, P, EXPERT_COLS).transpose(2, 0, 1, 3)),
        "w_moe_out": np.ascontiguousarray(o_proj.transpose(1, 0, 2)),
    }


def kernel(x, L0_tok_scharr, L0_attn_w_qkv, L0_attn_w_out, L0_ffn_sim_matrix, L0_ffn_gates, L0_ffn_q_proj,
           L0_ffn_k_proj, L0_ffn_v_proj, L0_ffn_o_proj):
    import concourse.bacc as bacc
    from concourse.bass_utils import run_bass_kernel_spmd

    given = [np.asarray(a) for a in (x, L0_tok_scharr, L0_attn_w_qkv, L0_attn_w_out, L0_ffn_sim_matrix, L0_ffn_gates,
                                     L0_ffn_q_proj, L0_ffn_k_proj, L0_ffn_v_proj, L0_ffn_o_proj)]
    arrays = {**layouts(*given), **shape_constants()}
    nc = bacc.Bacc("TRN2", target_bir_lowering=False, num_devices=1)
    args = {name: nc.dram_tensor(f"in_{name}", a.shape, mybir.dt.from_np(a.dtype), kind="ExternalInput").ap()
            for name, a in arrays.items()}
    out = nc.dram_tensor("out", (IMAGES, ROWS, COLS), F32, kind="ExternalOutput").ap()
    build(nc, **args, out=out)
    ran = run_bass_kernel_spmd(nc, [{f"in_{name}": np.ascontiguousarray(a) for name, a in arrays.items()}],
                               core_ids=[0])
    return ran.results[0]["out"]
```

```python
from contextlib import ExitStack

import numpy as np

import concourse.bass as bass
from concourse import mybir

F32 = mybir.dt.float32
F32R = mybir.dt.float32r
U32 = mybir.dt.uint32
ALU = mybir.AluOpType
ACT = mybir.ActivationFunctionType
AX_X = mybir.AxisListType.X

P = 128
IMAGES, CHANNELS, ROWS, COLS = 16, 3, 256, 256
TT = ROWS // P
CT = COLS // P
HEADS, HEAD_DIM, WINDOW = 16, 64, 64
HALF = HEAD_DIM // 2
PAIRS = HEADS // 2
GROUPS = HEADS // 4
BLOCKS = ROWS // WINDOW
KEYS = 2 * WINDOW
GROUP_COLS = 3 * 4 * HEAD_DIM
HALO_AT = (0, 32, 64)
HALO_ROWS = HALO_AT[-1] + 6
RAW_SLOTS = 5
MOVES = 8
GRAY = (0.2989, 0.587, 0.114)
LN_EPS, RMS_EPS = 1e-5, 1e-6
MASKED = -1e9
EXCLUDED = 1e29
EXPERTS, EXPERT_DIM = 16, 128
EXPERT_COLS = 3 * EXPERT_DIM
SCORE_SCALE = float(EXPERT_DIM) ** -0.5


def positive(eng, sem, count):
    if isinstance(count, int) and count <= 0:
        return
    eng.wait_ge(sem, count)


def shape_constants():
    freq = 1.0 / np.float32(10000.0) ** (np.arange(0, HEAD_DIM, 2, dtype=np.float32) / np.float32(HEAD_DIM))
    angle = np.outer(np.arange(ROWS, dtype=np.float32), freq.astype(np.float32)).astype(np.float32)
    cos, sin = np.cos(angle).T, np.sin(angle).T
    cos, sin = np.tile(cos, (4, 1)), np.tile(sin, (4, 1))
    rope_k = np.stack([cos, -sin, sin], 1).astype(np.float32)
    rope_q = (rope_k * np.float32(HEAD_DIM ** -0.5)).astype(np.float32)
    mask = np.full((P, BLOCKS, KEYS), MASKED, np.float32)
    for b in range(BLOCKS):
        for c in range(KEYS):
            key = key_of(b, c)
            for r in range(WINDOW):
                q = WINDOW * b + r
                if q >= key and q - key <= WINDOW:
                    mask[r, b, c] = mask[WINDOW + r, b, c] = 0.0
    row = np.zeros((P, 3, P), np.float32)
    for dy in range(3):
        for m in range(P):
            k = m + dy - 1
            if 0 <= k < P:
                row[k, dy, m] = 1.0
    edge = np.zeros((HALO_ROWS, P), np.float32)
    for at in HALO_AT:
        edge[at:at + 3, P - 1] = 1.0
        edge[at + 3:at + 6, 0] = 1.0
    return {"rope": np.stack([rope_q, rope_k], 1).reshape(P, 2, 3, ROWS), "mask": mask, "row": row,
            "edge": edge, "identity": np.eye(P, dtype=np.float32),
            "numbers": np.tile(np.arange(EXPERTS, dtype=np.float32), (P, 1))}


def key_of(block, column):
    if block == 0:
        return column
    if block % 2:
        return WINDOW * (block - 1) + column
    return WINDOW * block + column if column < WINDOW else WINDOW * (block - 1) + column - WINDOW


def reversed_halves(ap):
    (part, (step, two), inner) = ap.ap
    return bass.AP(tensor=ap.tensor, offset=ap.offset + step, ap=[list(part), [-step, two], list(inner)])


def build(nc, x, scharr, scharr_last, w_qkv, w_out, sim, gates, w_moe, w_moe_out, rope, mask, row, edge, identity, numbers, out):
    with ExitStack() as ctx:
        def sem(name):
            return ctx.enter_context(nc.semaphore(name))

        def sb(name, shape, dt=F32, scope=ctx):
            return scope.enter_context(nc.sbuf_tensor(name, shape, dt))

        bank = [ctx.enter_context(nc.psum_tensor(f"bank{i}", [P, 512], F32)) for i in range(8)]

        h_all = sb("h_all", [P, IMAGES * TT, COLS])
        ident = sb("ident", [P, P])
        minus_half = sb("minus_half", [P, TT])
        carrier = sb("carrier", [P, 1])

        a_scope = ctx.enter_context(ExitStack())
        a = lambda name, shape, dt=F32: sb(name, shape, dt, a_scope)
        w_hi = a("w_hi", [P, CT, GROUPS, GROUP_COLS], F32R)
        w_lo = a("w_lo", [P, CT, GROUPS, GROUP_COLS], F32R)
        rope_t = a("rope_t", [P, 2, 3, ROWS])
        row_t = a("row_t", [P, 3, P])
        edge_t = a("edge_t", [HALO_ROWS, P])
        taps = a("taps", [P, 2, 3, 3])
        edge_taps = a("edge_taps", [HALO_ROWS, 2])
        band_hi = a("band_hi", [P, 2, 3, P], F32R)
        band_lo = a("band_lo", [P, 2, 3, P], F32R)
        edge_band = a("edge_band", [HALO_ROWS, 2, P])
        edge_high = a("edge_high", [HALO_ROWS, 2, P], F32R)
        edge_stack = a("edge_stack", [HALO_ROWS, 2, P], F32R)
        x_in = a("x_in", [P, CHANNELS, TT, COLS])
        gray = a("gray", [P, TT, COLS + 2])
        gray_hi = a("gray_hi", [P, TT, COLS + 2], F32R)
        gray_lo = a("gray_lo", [P, TT, COLS + 2], F32R)
        halo = a("halo", [HALO_ROWS, TT, COLS], F32R)
        abs_e = a("abs_e", [P, 2, TT, COLS])
        stats = a("stats", [P, TT, 6])
        moments = a("moments", [P, TT, 2])
        spread = a("spread", [P, TT])
        rstd = a("rstd", [P, TT])
        xn = a("xn", [P, TT, COLS])
        x_hi = a("x_hi", [P, CT, ROWS], F32R)
        x_lo = a("x_lo", [P, CT, ROWS], F32R)
        own_part = a("own_part", [P, 2, 2, ROWS])
        other_part = a("other_part", [P, 2, 2, ROWS])
        rotated = a("rotated", [P, 2, 2, 2, ROWS])
        wo_hi = a("wo_hi", [P, PAIRS, COLS], F32R)
        wo_lo = a("wo_lo", [P, PAIRS, COLS], F32R)
        mask_t = a("mask_t", [P, BLOCKS, KEYS])
        qk = a("qk", [P, PAIRS, 2, ROWS])
        v = a("v", [P, GROUPS, TT, 4 * HEAD_DIM])
        v_cross = a("v_cross", [P, GROUPS, 4 * HEAD_DIM])
        masked = a("masked", [P, 2, BLOCKS, KEYS])
        band = masked[:, :, :, :].rearrange("p a b c -> p (a b c)")[:, 0:6 * P]\
            .rearrange("p (f d m) -> p f d m", f=2, d=3)
        neg_max = a("neg_max", [P, 2, BLOCKS])
        prob = a("prob", [P, 2, BLOCKS, KEYS])
        total = a("total", [P, 2, BLOCKS])
        inv_total = a("inv_total", [P, 2, BLOCKS])
        prob_t = a("prob_t", [P, 2, BLOCKS, P])
        o_hi = a("o_hi", [P, 2, ROWS], F32R)
        o_lo = a("o_lo", [P, 2, ROWS], F32R)

        scores_bank = bank[0:2]
        q_bank, k_bank = bank[2], bank[3]
        v_bank, o_bank, out_bank, misc_bank = bank[4], bank[5], bank[6], bank[7]

        row_loaded = sem("row_loaded")
        taps_loaded = sem("taps_loaded")
        band_lo_done = sem("band_lo_done")
        ident_loaded = sem("ident_loaded")
        const_loaded = sem("const_loaded")
        minus_half_set = sem("minus_half_set")
        borders_zero = sem("borders_zero")
        band_part = sem("band_part")
        band_ready = sem("band_ready")
        raw_loaded = [sem(f"raw_loaded{i}") for i in range(RAW_SLOTS)]
        w_hi_ready = sem("w_hi_ready")
        w_lo_ready = sem("w_lo_ready")
        x_loaded = sem("x_loaded")
        gray_first = sem("gray_first")
        gray_second = sem("gray_second")
        gray_done = sem("gray_done")
        gray_hi_done = sem("gray_hi_done")
        gray_lo_done = sem("gray_lo_done")
        band_hi_done = sem("band_hi_done")
        edge_part = sem("edge_part")
        halo_loaded = sem("halo_loaded")
        conv_done = sem("conv_done")
        abs_done = sem("abs_done")
        h_done = sem("h_done")
        stats_done = sem("stats_done")
        moments_done = sem("moments_done")
        spread_done = sem("spread_done")
        rstd_done = sem("rstd_done")
        xn_done = sem("xn_done")
        xt_done = sem("xt_done")
        x_hi_done = sem("x_hi_done")
        x_lo_done = sem("x_lo_done")
        qk_done = sem("qk_done")
        rope_mul = sem("rope_mul")
        rope_add = sem("rope_add")
        moved = [sem(f"moved{g}") for g in range(GROUPS)]
        v_done = sem("v_done")
        v_evac = sem("v_evac")
        v_crossed = [sem(f"v_crossed{g}") for g in range(GROUPS)]
        s_done = sem("s_done")
        masked_done = sem("masked_done")
        max_done = sem("max_done")
        exp_done = sem("exp_done")
        recip_done = sem("recip_done")
        norm_done = sem("norm_done")
        t_done = sem("t_done")
        pt_evac = sem("pt_evac")
        o_done = sem("o_done")
        o_hi_done = sem("o_hi_done")
        o_lo_done = sem("o_lo_done")
        out_done = sem("out_done")
        resid_done = sem("resid_done")
        stored = sem("stored")

        TAPS, CONSTS = 7, 2

        CHUNKS = CT * GROUPS + PAIRS // 2
        qk_space = qk[:, :, :, :].rearrange("p a b c -> p (a b c)")
        HALO_DMAS = 2 * len(HALO_AT)
        raw_slot = [qk_space[:, i * GROUP_COLS:(i + 1) * GROUP_COLS] for i in range(RAW_SLOTS)]

        def raw_chunk(n):
            slot = raw_slot[n % RAW_SLOTS]
            if n < CT * GROUPS:
                g, ct = n // CT, n % CT
                return (w_qkv[ct * P:(ct + 1) * P, g, :], slot[:, 0:GROUP_COLS], w_hi[:, ct, g, :], w_lo[:, ct, g, :])
            pair = 2 * (n - CT * GROUPS)
            return (w_out[pair * P:(pair + 2) * P, :].rearrange("(a p) c -> p a c", p=P),
                    slot[:, 0:2 * COLS].rearrange("p (a c) -> p a c", a=2),
                    wo_hi[:, pair:pair + 2, :], wo_lo[:, pair:pair + 2, :])

        a_scope.close()
        b_ = lambda name, shape, dt=F32: sb(name, shape, dt)
        work = b_("work", [P, 5, TT * ROWS])
        qkt, m_prob, m_prob_t, result = (work[:, i, :].rearrange("p (t c) -> p t c", t=TT) for i in range(4))
        raw = b_("raw", [P, 2, 4 * COLS])
        sim_t = b_("sim_t", [P, CT, EXPERTS])
        sim_sq = b_("sim_sq", [P, CT, EXPERTS])
        ones = b_("ones", [P, P])
        expert_no = b_("expert_no", [P, EXPERTS])
        gate_t = b_("gate_t", [P, EXPERTS])
        m_stats = b_("m_stats", [P, TT, 6])
        m_moments = b_("m_moments", [P, TT, 2])
        m_spread = b_("m_spread", [P, TT])
        m_rstd = b_("m_rstd", [P, TT])
        m_square = b_("m_square", [P, TT])
        m_rnorm = b_("m_rnorm", [P, TT])
        m_xn = b_("m_xn", [P, TT, COLS])
        m_x = b_("m_x", [P, CT, ROWS])
        mx_hi = b_("mx_hi", [P, CT, ROWS], F32R)
        mx_lo = b_("mx_lo", [P, CT, ROWS], F32R)
        logit = b_("logit", [P, TT, EXPERTS])
        gated = b_("gated", [P, TT, EXPERTS])
        active = b_("active", [P, TT, EXPERTS])
        fallback = b_("fallback", [P, TT, EXPERTS])
        idle = b_("idle", [P, TT])
        top = b_("top", [P, TT, 8])
        top_at = b_("top_at", [P, TT, 8], U32)
        top_no = b_("top_no", [P, TT, 2])
        row_stat = b_("row_stat", [P, TT])
        share = b_("share", [P, 3, TT, EXPERTS])
        share_n = b_("share_n", [P, TT, EXPERTS])
        m_bias = b_("m_bias", [P, 2, TT])
        m_total = b_("m_total", [P, TT])
        m_inv = b_("m_inv", [P, TT])
        mo_t_hi = b_("mo_t_hi", [P, ROWS], F32R)
        mo_t_lo = b_("mo_t_lo", [P, ROWS], F32R)
        me = b_("me", [P, EXPERTS, 2, CT, EXPERT_COLS], F32R)
        me_hi, me_lo = me[:, :, 0, :, :], me[:, :, 1, :, :]
        mo_hi = b_("mo_hi", [P, EXPERTS, COLS], F32R)
        mo_lo = b_("mo_lo", [P, EXPERTS, COLS], F32R)
        part = b_("part", [P, TT, EXPERT_COLS])
        qkv = b_("qkv", [P, TT, EXPERT_COLS])
        out_part = b_("out_part", [P, 2, TT, COLS])

        chunk_bank = bank[0:4]
        down_bank = bank[4:6]
        turn_bank, attn_bank = bank[7], bank[6]
        logit_ps = turn_bank[:, 0:TT * EXPERTS].rearrange("p (t e) -> p t e", t=TT)

        STEPS = EXPERTS * TT
        DOWNS = EXPERTS // 2 * TT
        M_CHUNKS = EXPERTS + EXPERTS // 4
        M_SLOTS = 5

        m_const_loaded = sem("m_const_loaded")
        m_raw_loaded = [sem(f"m_raw_loaded{i}") for i in range(M_SLOTS)]
        ones_set = sem("ones_set")
        m_hi_ready = sem("m_hi_ready")
        m_lo_ready = sem("m_lo_ready")
        gate_exp = sem("gate_exp")
        setup_step = sem("setup_step")
        sim_squared = sem("sim_squared")
        sim_summed_ps = sem("sim_summed_ps")
        sim_summed = sem("sim_summed")
        sim_root = sem("sim_root")
        sim_ready = sem("sim_ready")
        norm_step = sem("norm_step")
        m_spread_done = sem("m_spread_done")
        m_rstd_done = sem("m_rstd_done")
        m_square_done = sem("m_square_done")
        m_rnorm_done = sem("m_rnorm_done")
        m_xn_done = sem("m_xn_done")
        m_xt_done = sem("m_xt_done")
        m_x_done = sem("m_x_done")
        mx_hi_done = sem("mx_hi_done")
        mx_lo_done = sem("mx_lo_done")
        logits_done = sem("logits_done")
        logits_read = sem("logits_read")
        router_step = sem("router_step")
        share_step = sem("share_step")
        router_in = sem("router_in")
        router_exp = sem("router_exp")
        shifted = sem("shifted")
        step_done = sem("step_done")
        combined = sem("combined")
        qk_turned = sem("qk_turned")
        qkt_done = sem("qkt_done")
        m_scores = sem("m_scores")
        m_max = sem("m_max")
        m_bias_done = sem("m_bias_done")
        m_exp = sem("m_exp")
        m_inv_done = sem("m_inv_done")
        share_n_done = sem("share_n_done")
        m_turned = sem("m_turned")
        m_prob_t_done = sem("m_prob_t_done")
        mixed = sem("mixed")
        mo_hi_done = sem("mo_hi_done")
        mo_lo_done = sem("mo_lo_done")
        down_done = sem("down_done")
        down_step = sem("down_step")
        summed = sem("summed")

        work_space = work[:, :, :].rearrange("p a b -> p (a b)")
        m_slots = [raw[:, i, :] for i in range(2)] + [work_space[:, i * CT * EXPERT_COLS:(i + 1) * CT * EXPERT_COLS]
                                                      for i in range(3)]
        EARLY = 10
        m_slot_of = [n % M_SLOTS for n in range(EXPERTS)] + [(n + 1) % 2 for n in range(M_CHUNKS - EXPERTS)]

        def m_loads(n):
            return sum(1 for k in range(n + 1) if m_slot_of[k] == m_slot_of[n])

        def m_split_before(n):
            return max([k + 1 for k in range(n) if m_slot_of[k] == m_slot_of[n]], default=0)

        def m_chunk(n):
            slot = m_slots[m_slot_of[n]]
            if n < EXPERTS:
                view = slot[:, 0:CT * EXPERT_COLS].rearrange("p (a c) -> p a c", a=CT)
                return w_moe[:, n, :, :], view, me_hi[:, n, :, :], me_lo[:, n, :, :]
            e = 4 * (n - EXPERTS)
            return (w_moe_out[:, e:e + 4, :], slot.rearrange("p (a c) -> p a c", a=4),
                    mo_hi[:, e:e + 4, :], mo_lo[:, e:e + 4, :])

        def load_m_chunk(sp, n):
            positive(sp, m_hi_ready, m_split_before(n))
            positive(sp, m_lo_ready, m_split_before(n))
            src, slot, _, _ = m_chunk(n)
            sp.dma_start(slot, src).then_inc(m_raw_loaded[m_slot_of[n]], 16)

        def m_rstd_root(pool, f):
            pool.wait_ge(m_spread_done, f + 1)
            nc.gpsimd.tensor_tensor(m_rstd[:, :], m_spread[:, :], minus_half[:, :], ALU.pow).then_inc(m_rstd_done, 1)

        def m_norm_root(pool, f):
            pool.wait_ge(m_square_done, f + 1)
            nc.gpsimd.tensor_tensor(m_rnorm[:, :], m_square[:, :], minus_half[:, :], ALU.pow).then_inc(m_rnorm_done, 1)

        def high_part(act, n):
            act.wait_ge(m_raw_loaded[m_slot_of[n]], 16 * m_loads(n))
            _, slot, hi, _ = m_chunk(n)
            nc.scalar.activation(hi, slot, ACT.Copy).then_inc(m_hi_ready, 1)

        def low_part(dve, n):
            dve.wait_ge(m_hi_ready, n + 1)
            _, slot, hi, lo = m_chunk(n)
            nc.vector.tensor_tensor(lo, slot, hi.bitcast(F32), ALU.subtract).then_inc(m_lo_ready, 1)

        def m_statistics(dve, f, step):
            if step == 0:
                for t in range(TT):
                    last = nc.vector.bn_stats(m_stats[:, t, :], h_all[:, bass.ds(f * TT + t, 1), :])
                last.then_inc(norm_step, 1)
            if step == 1:
                dve.wait_ge(norm_step, 4 * f + 1)
                positive(dve, m_rnorm_done, f)
                nc.vector.memset(carrier[:, :], 0.0)
                for t in range(TT):
                    last = nc.vector.bn_aggr(m_moments[:, t, :], m_stats[:, t, :])
                last.then_inc(norm_step, 1)
            if step == 2:
                dve.wait_ge(norm_step, 4 * f + 2)
                nc.vector.tensor_scalar(m_spread[:, :], m_moments[:, :, 1], LN_EPS, None, ALU.add)\
                    .then_inc(m_spread_done, 1)

        def m_layer_norm(dve, f, step):
            if step == 0:
                dve.wait_ge(m_rstd_done, f + 1)
                nc.vector.tensor_tensor(m_square[:, :], m_rstd[:, :], m_rstd[:, :], ALU.mult).then_inc(norm_step, 1)
                positive(dve, m_xt_done, f)
                for t in range(TT):
                    last = nc.vector.tensor_scalar(m_xn[:, t:t + 1, :], h_all[:, bass.ds(f * TT + t, 1), :],
                                                   m_moments[:, t, 0:1], m_rstd[:, t:t + 1],
                                                   ALU.subtract, ALU.mult)
                last.then_inc(m_xn_done, 1)
            if step == 1:
                dve.wait_ge(norm_step, 4 * f + 3)
                nc.vector.tensor_tensor(m_square[:, :], m_square[:, :], m_moments[:, :, 1], ALU.mult)\
                    .then_inc(norm_step, 1)
            if step == 2:
                dve.wait_ge(norm_step, 4 * f + 4)
                nc.vector.tensor_scalar(m_square[:, :], m_square[:, :], float(COLS), 1e-24, ALU.mult, ALU.max)\
                    .then_inc(m_square_done, 1)

        def evacuate_x(act, f):
            act.wait_ge(m_xt_done, f + 1)
            positive(act, logits_done, f)
            positive(act, mx_lo_done, TT * f)
            nc.scalar.activation(m_x[:, :, :], turn_bank[:, :].rearrange("p (a c) -> p a c", a=CT),
                                 ACT.Copy).then_inc(m_x_done, 1)

        def m_split_x_high(act, f, t):
            positive(act, step_done, STEPS * f - TT + 1 + t)
            if t == 0:
                act.wait_ge(m_x_done, f + 1)
            nc.scalar.activation(mx_hi[:, :, t * P:(t + 1) * P], m_x[:, :, t * P:(t + 1) * P],
                                 ACT.Copy).then_inc(mx_hi_done, 1)

        def m_split_x_low(dve, f, t):
            dve.wait_ge(mx_hi_done, TT * f + t + 1)
            nc.vector.tensor_tensor(mx_lo[:, :, t * P:(t + 1) * P], m_x[:, :, t * P:(t + 1) * P],
                                    mx_hi[:, :, t * P:(t + 1) * P].bitcast(F32), ALU.subtract)\
                .then_inc(mx_lo_done, 1)

        def m_transpose_x(pe, f):
            pe.wait_ge(m_xn_done, f + 1)
            positive(pe, qkt_done, f - 1)
            for ct in range(CT):
                for t in range(TT):
                    last = nc.tensor.transpose(turn_bank[:, ct * ROWS + t * P:ct * ROWS + (t + 1) * P],
                                               m_xn[:, t, ct * P:(ct + 1) * P], ident[:, :])
            last.then_inc(m_xt_done, 1)

        def logits(pe, f):
            pe.wait_ge(m_x_done, f + 1)
            if isinstance(f, int) and f == 0:
                pe.wait_ge(sim_ready, 1)
            for t in range(TT):
                for ct in range(CT):
                    last = nc.tensor.matmul(logit_ps[:, t, :], m_x[:, ct, t * P:(t + 1) * P], sim_t[:, ct, :],
                                            start=(ct == 0), stop=(ct == CT - 1))
            last.then_inc(logits_done, 1)

        ROUTER_STEPS, ROUTER_PIECES = 12, 14

        def router(dve, f, piece):
            base = ROUTER_STEPS * f

            def after(step):
                dve.wait_ge(router_step, base + step)

            if piece == 0:
                dve.wait_ge(logits_done, f + 1)
                dve.wait_ge(m_rnorm_done, f + 1)
                for t in range(TT):
                    last = nc.vector.scalar_tensor_tensor(
                        out=logit[:, t, :], in0=logit_ps[:, t, :], scalar=m_rnorm[:, t:t + 1],
                        in1=gate_t[:, :], op0=ALU.mult, op1=ALU.subtract)
                last.then_inc(logits_read, 1)
            if piece == 1:
                dve.wait_ge(logits_read, f + 1)
                nc.vector.tensor_scalar(active[:, :, :], logit[:, :, :], 0.0, None, ALU.is_gt)\
                    .then_inc(router_step, 1)
                for t in range(TT):
                    last = nc.vector.max(top[:, t, :], logit[:, t, :])
                last.then_inc(router_step, 1)
            if piece == 2:
                after(2)
                nc.vector.tensor_reduce(row_stat[:, :], active[:, :, :], AX_X, ALU.max)\
                    .then_inc(router_step, 1)
                for t in range(TT):
                    last = nc.vector.max_index(top_at[:, t, :], top[:, t, :], logit[:, t, :])
                last.then_inc(router_step, 1)
            if piece == 3:
                after(4)
                nc.vector.tensor_copy(top_no[:, :, :], top_at[:, :, 0:2]).then_inc(router_step, 1)
                nc.vector.tensor_scalar(idle[:, :], row_stat[:, :], 0.0, None, ALU.is_equal)\
                    .then_inc(router_step, 1)
            if piece == 4:
                after(5)
                for t in range(TT):
                    last = nc.vector.tensor_scalar(fallback[:, t, :], expert_no[:, :], top_no[:, t, 0:1], None,
                                                   ALU.is_equal)
                last.then_inc(router_step, 1)
            if piece == 5:
                after(7)
                for t in range(TT):
                    last = nc.vector.scalar_tensor_tensor(
                        out=fallback[:, t, :], in0=expert_no[:, :], scalar=top_no[:, t, 1:2],
                        in1=fallback[:, t, :], op0=ALU.is_equal, op1=ALU.max)
                last.then_inc(router_step, 1)
                nc.vector.tensor_scalar(gated[:, :, :], logit[:, :, :], 0.0, None, ALU.max)
            if piece == 6:
                after(8)
                for t in range(TT):
                    last = nc.vector.scalar_tensor_tensor(
                        out=active[:, t, :], in0=fallback[:, t, :], scalar=idle[:, t:t + 1],
                        in1=active[:, t, :], op0=ALU.mult, op1=ALU.max)
                last.then_inc(router_step, 1)
            if piece == 7:
                after(9)
                nc.vector.tensor_scalar(fallback[:, :, :], active[:, :, :], 1.0, EXCLUDED, ALU.subtract,
                                        ALU.mult).then_inc(router_step, 1)
            if piece == 8:
                after(10)
                nc.vector.tensor_tensor(gated[:, :, :], gated[:, :, :], fallback[:, :, :], ALU.add)\
                    .then_inc(router_step, 1)
            if piece == 9:
                after(11)
                nc.vector.tensor_reduce(row_stat[:, :], gated[:, :, :], AX_X, ALU.max)\
                    .then_inc(router_step, 1)
            if piece == 10:
                after(12)
                nc.vector.tensor_tensor(gated[:, :, :], gated[:, :, :],
                                        row_stat[:, :].unsqueeze(2).to_broadcast([P, TT, EXPERTS]),
                                        ALU.subtract).then_inc(router_in, 1)
            if piece == 11:
                dve.wait_ge(router_exp, f + 1)
                nc.vector.tensor_reduce(row_stat[:, :], active[:, :, :], AX_X, ALU.add).then_inc(share_step, 1)
            if piece == 12:
                dve.wait_ge(share_step, 3 * f + 1)
                nc.vector.reciprocal(idle[:, :], row_stat[:, :]).then_inc(share_step, 1)
            if piece == 13:
                dve.wait_ge(share_step, 3 * f + 2)
                nc.vector.tensor_tensor(share[:, 2, :, :], active[:, :, :],
                                        idle[:, :].unsqueeze(2).to_broadcast([P, TT, EXPERTS]),
                                        ALU.mult).then_inc(share_step, 1)

        def scores_bank_of(n, p):
            return bank[p % 4] if isinstance(n, int) and n == IMAGES - 1 else scores_bank[p % 2]

        def tiles(image):
            return bass.ds(image * TT, TT)

        def bodies(eng, body):
            body(0, True, True)
            with eng.Fori(1, IMAGES - 2) as n:
                body(n, True, True)
            body(IMAGES - 2, True, False)
            body(IMAGES - 1, False, False)

        def bodies_a(eng, body, last_body):
            body(0, True, True)
            with eng.Fori(1, IMAGES - 3) as n:
                body(n, True, True)
            body(IMAGES - 3, True, False)
            body(IMAGES - 2, False, False)
            last_body(IMAGES - 1)

        def load_halo(eng, f):
            eng.wait_ge(gray_lo_done, f + 1)
            positive(eng, conv_done, 2 * f)
            for at, gray_part in zip(HALO_AT, (gray_hi, gray_lo, gray_hi)):
                for k, (p, t) in enumerate(((0, 1), (P - 1, 0))):
                    src = gray_part[p:p + 1, t, 0:COLS].bitcast(F32)
                    shifted = bass.AP(tensor=src.tensor, offset=src.offset,
                                      ap=[list(src.ap[0]), [1, 3], [1, COLS]])
                    eng.dma_start(halo[at + 3 * k:at + 3 * k + 3, k, :].bitcast(F32), shifted)\
                        .then_inc(halo_loaded, 16)

        block = ctx.enter_context(nc.Block())

        @block.sync
        def _(sp):
            def move_rotated(m, g):
                sp.wait_ge(rope_add, 2 * (GROUPS * m + g) + 2)
                for j in range(4):
                    for half in range(2):
                        to = HEAD_DIM * (j % 2) + HALF * half
                        sp.dma_start(qk[to:to + HALF, 2 * g + j // 2, :, :],
                                     rotated[HALF * j:HALF * (j + 1), g % 2, :, half, :]).then_inc(moved[g], 16)

            def move_values(m, g):
                sp.wait_ge(v_evac, GROUPS * m + g + 1)
                sp.dma_start(v_cross[0:WINDOW, g, :], v[0:WINDOW, g, 1, :]).then_inc(v_crossed[g], 16)
                sp.dma_start(v_cross[WINDOW:P, g, :], v[WINDOW:P, g, 0, :]).then_inc(v_crossed[g], 16)

            def load_chunk(n):
                if n >= RAW_SLOTS:
                    sp.wait_ge(w_hi_ready, n - RAW_SLOTS + 1)
                    sp.wait_ge(w_lo_ready, n - RAW_SLOTS + 1)
                src, slot, _, _ = raw_chunk(n)
                sp.dma_start(slot, src).then_inc(raw_loaded[n % RAW_SLOTS], 16)

            sp.dma_start(taps[:, :, :, :].rearrange("p a b c -> p (a b c)"),
                         scharr.rearrange("a o b c -> (a o b c)").partition_broadcast(P)).then_inc(row_loaded, 16)
            sp.dma_start(row_t[:, :, :], row).then_inc(row_loaded, 16)
            sp.dma_start(edge_t[:, :], edge).then_inc(taps_loaded, 16)
            sp.wait_ge(borders_zero, 1)
            for at in HALO_AT:
                for k, dy in enumerate((2, 0)):
                    sp.dma_start(edge_taps[at + 3 * k:at + 3 * k + 3, :],
                                 scharr_last[dy, :, :]).then_inc(taps_loaded, 16)
            load_chunk(0)
            load_chunk(1)
            sp.dma_start(ident[:, :], identity).then_inc(ident_loaded, 16)
            for n in range(2, RAW_SLOTS):
                load_chunk(n)
            load_halo(sp, 0)
            load_chunk(RAW_SLOTS)
            sp.dma_start(rope_t[:, :, :, :], rope).then_inc(const_loaded, 16)
            sp.dma_start(mask_t[:, :, :], mask).then_inc(const_loaded, 16)
            for n in range(RAW_SLOTS + 1, CHUNKS):
                load_chunk(n)
            load_halo(sp, 1)
            sp.wait_ge(w_hi_ready, CHUNKS)
            sp.wait_ge(w_lo_ready, CHUNKS)
            for g in range(GROUPS):
                move_rotated(0, g)
                move_values(0, g)

            def body(n, edges, load):
                for g in range(GROUPS):
                    if edges and g == 0:
                        load_halo(sp, n + 2)
                    move_rotated(n + 1, g)
                    move_values(n + 1, g)
            bodies_a(sp, body, lambda n: None)

            sp.wait_ge(v_done, GROUPS * IMAGES)
            sp.wait_ge(rope_add, 2 * GROUPS * IMAGES)
            for g in range(GROUPS):
                sp.wait_ge(moved[g], 16 * MOVES * IMAGES)
            sp.dma_start(sim_t[:, :, :], sim.rearrange("(a p) e -> p a e", p=P)).then_inc(m_const_loaded, 16)
            sp.dma_start(gate_t[:, :], gates.partition_broadcast(P)).then_inc(m_const_loaded, 16)
            sp.dma_start(expert_no[:, :], numbers).then_inc(m_const_loaded, 16)
            for n in range(M_CHUNKS):
                load_m_chunk(sp, n)

        @block.gpsimd
        def _(pool):
            nc.gpsimd.memset(minus_half[:, :], -0.5).then_inc(minus_half_set, 1)
            pool.wait_ge(minus_half_set, 1)

            def add_edges(f):
                pool.wait_ge(abs_done, 2 * f + 2)
                nc.gpsimd.tensor_tensor(h_all[:, tiles(f), :], abs_e[:, 0, :, :], abs_e[:, 1, :, :],
                                        ALU.add).then_inc(h_done, 1)

            def inverse_root(f):
                pool.wait_ge(spread_done, f + 1)
                nc.gpsimd.tensor_tensor(rstd[:, :], spread[:, :], minus_half[:, :], ALU.pow).then_inc(rstd_done, 1)

            def rotate(m, g, which):
                pool.wait_ge(rope_mul, 2 * (GROUPS * m + g) + which + 1)
                if which == 0:
                    if g >= 2:
                        pool.wait_ge(moved[g - 2], 16 * MOVES * (m + 1))
                    else:
                        positive(pool, moved[g + 2], 16 * MOVES * m)
                nc.gpsimd.tensor_tensor(rotated[:, g % 2, which, :, :], own_part[:, which, :, :],
                                        other_part[:, which, :, :], ALU.add).then_inc(rope_add, 1)

            def normalise(n, p):
                pool.wait_ge(recip_done, PAIRS * n + p + 1)
                nc.gpsimd.tensor_tensor(prob[:, p % 2, :, :], prob[:, p % 2, :, :],
                                        inv_total[:, p % 2, :].unsqueeze(2).to_broadcast([P, BLOCKS, KEYS]),
                                        ALU.mult).then_inc(norm_done, 1)

            add_edges(0)
            inverse_root(0)
            for g in range(GROUPS):
                if g == 2:
                    add_edges(1)
                rotate(0, g, 0)
                if g == 2:
                    inverse_root(1)
                rotate(0, g, 1)
            normalise(0, 0)

            def body(n, edges, load):
                for p in range(PAIRS):
                    rotate(n + 1, p // 2, p % 2)
                    normalise(n, p + 1)
                    if edges and p == 2:
                        add_edges(n + 2)
                    if edges and p == 4:
                        inverse_root(n + 2)

            def last_body(n):
                for p in range(PAIRS):
                    if p < PAIRS - 1:
                        normalise(n, p + 1)
                    if p == 3:
                        pool.wait_ge(m_const_loaded, 48)
                        nc.gpsimd.memset(ones[:, :], 1.0).then_inc(ones_set, 1)
                        m_rstd_root(pool, 0)
                    if p == 4:
                        m_norm_root(pool, 0)
                    if p == 6:
                        pool.wait_ge(sim_summed, 1)
                        nc.gpsimd.tensor_tensor(sim_sq[:, 0, :], sim_sq[:, 1, :],
                                                minus_half[:, 0:1].to_broadcast([P, EXPERTS]),
                                                ALU.pow).then_inc(sim_root, 1)
            bodies_a(pool, body, last_body)

        @block.scalar
        def _(act):
            def load_image(f):
                positive(act, gray_done, f)
                act.dma_start(x_in[:, :, :, :], x[f].rearrange("c (t p) w -> p c t w", p=P)).then_inc(x_loaded, 16)

            def gray_red(f):
                act.wait_ge(x_loaded, 16 * (f + 1))
                positive(act, gray_lo_done, f)
                nc.scalar.activation(gray[:, :, 1:COLS + 1], x_in[:, 0, :, :], ACT.Copy,
                                     scale=GRAY[0]).then_inc(gray_first, 1)

            def gray_high(f):
                act.wait_ge(gray_done, f + 1)
                positive(act, conv_done, 2 * f)
                positive(act, halo_loaded, 16 * HALO_DMAS * f)
                nc.scalar.activation(gray_hi[:, :, :], gray[:, :, :], ACT.Copy).then_inc(gray_hi_done, 1)

            def edge_size(f, which):
                act.wait_ge(conv_done, 2 * f + which + 1)
                if which == 0:
                    positive(act, h_done, f)
                src = (v_bank, misc_bank)[which]
                nc.scalar.activation(abs_e[:, which, :, :], src[:, :].rearrange("p (t c) -> p t c", t=TT),
                                     ACT.Abs, scale=0.5).then_inc(abs_done, 1)

            def split_x(f):
                act.wait_ge(xt_done, f + 1)
                positive(act, v_done, GROUPS * f)
                nc.scalar.activation(x_hi[:, :, :], misc_bank[:, :].rearrange("p (t c) -> p t c", t=CT),
                                     ACT.Copy).then_inc(x_hi_done, 1)

            def values(m, g):
                act.wait_ge(v_done, GROUPS * m + g + 1)
                positive(act, o_done, PAIRS * (m - 1) + 2 * g + 2)
                nc.scalar.activation(v[:, g, :, :], v_bank[:, :].rearrange("p (t c) -> p t c", t=TT),
                                     ACT.Copy).then_inc(v_evac, 1)

            def exponent(n, p, blocks):
                if blocks[0] == 0:
                    act.wait_ge(max_done, PAIRS * n + p + 1)
                    positive(act, t_done, PAIRS * n + p - 1)
                for b in blocks:
                    last = nc.scalar.activation(prob[:, p % 2, b, :], masked[:, p % 2, b, :], ACT.Exp,
                                                bias=neg_max[:, p % 2, b:b + 1],
                                                accum_out=total[:, p % 2, b:b + 1])
                if blocks[-1] == BLOCKS - 1:
                    last.then_inc(exp_done, 1)

            def transposed(n, p):
                act.wait_ge(t_done, PAIRS * n + p + 1)
                positive(act, o_done, PAIRS * n + p - 1)
                nc.scalar.activation(prob_t[:, p % 2, :, :],
                                     scores_bank_of(n, p)[:, :].rearrange("p (b c) -> p b c", b=BLOCKS),
                                     ACT.Copy).then_inc(pt_evac, 1)

            def split_o(n, p):
                act.wait_ge(o_done, PAIRS * n + p + 1)
                nc.scalar.activation(o_hi[:, p % 2, :], o_bank[:, (p % 2) * ROWS:(p % 2 + 1) * ROWS],
                                     ACT.Copy).then_inc(o_hi_done, 1)

            act.dma_start(x_in[:, :, :, :], x[0].rearrange("c (t p) w -> p c t w", p=P)).then_inc(x_loaded, 16)
            gray_red(0)
            load_image(1)
            act.wait_ge(band_ready, 1)
            nc.scalar.activation(band_hi[:, 0, :, :], band[:, 0, :, :], ACT.Copy).then_inc(band_hi_done, 1)
            gray_high(0)
            act.wait_ge(band_ready, 2)
            nc.scalar.activation(band_hi[:, 1, :, :], band[:, 1, :, :], ACT.Copy).then_inc(band_hi_done, 1)
            for n in range(CHUNKS):
                act.wait_ge(raw_loaded[n % RAW_SLOTS], 16 * (n // RAW_SLOTS + 1))
                _, slot, hi, _ = raw_chunk(n)
                nc.scalar.activation(hi, slot, ACT.Copy).then_inc(w_hi_ready, 1)
                if n == 2:
                    edge_size(0, 0)
                    edge_size(0, 1)
                    gray_red(1)
                if n == 4:
                    split_x(0)
                if n == 5:
                    gray_high(1)
                if n == 7:
                    load_image(2)
            values(0, 0)
            values(0, 1)
            edge_size(1, 0)
            edge_size(1, 1)
            values(0, 2)
            gray_red(2)
            split_x(1)
            values(0, 3)
            exponent(0, 0, range(BLOCKS))

            def last_body(n):
                transposed(n, 0)
                for p in range(PAIRS):
                    if p < PAIRS - 1:
                        exponent(n, p + 1, range(BLOCKS))
                    if p:
                        transposed(n, p)
                    if p == 2:
                        act.wait_ge(m_const_loaded, 48)
                        nc.scalar.activation(gate_t[:, :], gate_t[:, :], ACT.Exp, scale=-1.0).then_inc(gate_exp, 1)
                    if p == PAIRS - 1:
                        m_split_x_high(act, 0, 0)
                        m_split_x_high(act, 0, 1)
                    split_o(n, p)
                    if p == 5:
                        evacuate_x(act, 0)
                    if 2 <= p < PAIRS - 1:
                        high_part(act, 2 * (p - 2))
                        high_part(act, 2 * (p - 2) + 1)

            def body(n, edges, load):
                for p in range(PAIRS):
                    if edges and p == 0:
                        gray_high(n + 2)
                    if edges and p == 2:
                        exponent(n, p + 1, range(BLOCKS))
                        edge_size(n + 2, 0)
                        edge_size(n + 2, 1)
                        transposed(n, p)
                    elif p == PAIRS - 1:
                        exponent(n, p + 1, range(0, 2))
                        transposed(n, p)
                        if edges:
                            split_x(n + 2)
                        exponent(n, p + 1, range(2, BLOCKS))
                    else:
                        transposed(n, p)
                        exponent(n, p + 1, range(BLOCKS))
                    if p == 1:
                        values(n + 1, 0)
                    split_o(n, p)
                    if p % 2 and p > 1:
                        values(n + 1, p // 2)
                    if load and p == 2:
                        load_image(n + 3)
                    if load and p == 4:
                        gray_red(n + 3)
            bodies_a(act, body, last_body)

        @block.vector
        def _(dve):
            def gray_green(f):
                dve.wait_ge(gray_first, f + 1)
                nc.vector.scalar_tensor_tensor(out=gray[:, :, 1:COLS + 1], in0=x_in[:, 1, :, :], scalar=GRAY[1],
                                               in1=gray[:, :, 1:COLS + 1], op0=ALU.mult,
                                               op1=ALU.add).then_inc(gray_second, 1)

            def gray_blue(f):
                dve.wait_ge(gray_second, f + 1)
                nc.vector.scalar_tensor_tensor(out=gray[:, :, 1:COLS + 1], in0=x_in[:, 2, :, :], scalar=GRAY[2],
                                               in1=gray[:, :, 1:COLS + 1], op0=ALU.mult,
                                               op1=ALU.add).then_inc(gray_done, 1)

            def gray_low(f):
                dve.wait_ge(gray_hi_done, f + 1)
                nc.vector.tensor_tensor(gray_lo[:, :, :], gray[:, :, :], gray_hi[:, :, :].bitcast(F32),
                                        ALU.subtract).then_inc(gray_lo_done, 1)

            def layer_stats(f):
                dve.wait_ge(h_done, f + 1)
                for t in range(TT):
                    last = nc.vector.bn_stats(stats[:, t, :], h_all[:, bass.ds(f * TT + t, 1), :])
                last.then_inc(stats_done, 1)

            def layer_moments(f):
                dve.wait_ge(stats_done, f + 1)
                nc.vector.memset(carrier[:, :], 0.0)
                for t in range(TT):
                    last = nc.vector.bn_aggr(moments[:, t, :], stats[:, t, :])
                last.then_inc(moments_done, 1)
                dve.wait_ge(moments_done, f + 1)
                nc.vector.tensor_scalar(spread[:, :], moments[:, :, 1], 1.0 + RMS_EPS, LN_EPS * RMS_EPS,
                                        ALU.mult, ALU.add).then_inc(spread_done, 1)

            def layer_norm(f):
                dve.wait_ge(rstd_done, f + 1)
                positive(dve, xt_done, f)
                for t in range(TT):
                    last = nc.vector.tensor_scalar(xn[:, t:t + 1, :], h_all[:, bass.ds(f * TT + t, 1), :],
                                                   moments[:, t, 0:1], rstd[:, t:t + 1],
                                                   ALU.subtract, ALU.mult)
                last.then_inc(xn_done, 1)

            def split_x(f):
                dve.wait_ge(x_hi_done, f + 1)
                nc.vector.tensor_tensor(x_lo[:, :, :], misc_bank[:, :].rearrange("p (t c) -> p t c", t=CT),
                                        x_hi[:, :, :].bitcast(F32), ALU.subtract).then_inc(x_lo_done, 1)

            def rotate(m, g, which):
                src = (q_bank, k_bank)[which][:, :].rearrange("p (a c) -> p a c", a=2)
                done = 2 * (GROUPS * m + g) + which
                dve.wait_ge(qk_done, done + 1)
                positive(dve, rope_add, done - 1)
                nc.vector.tensor_tensor(own_part[:, which, :, :], src,
                                        rope_t[:, which, 0:1, :].to_broadcast([P, 2, ROWS]), ALU.mult)
                nc.vector.tensor_tensor(other_part[:, which, :, :], reversed_halves(src),
                                        rope_t[:, which, 1:3, :], ALU.mult).then_inc(rope_mul, 1)

            def mask_scores(n, p):
                done = PAIRS * n + p
                dve.wait_ge(s_done, done + 1)
                positive(dve, exp_done, done - 1)
                nc.vector.tensor_tensor(masked[:, p % 2, :, :],
                                        scores_bank_of(n, p)[:, :].rearrange("p (b c) -> p b c", b=BLOCKS),
                                        mask_t[:, :, :], ALU.add).then_inc(masked_done, 1)

            def row_max(n, p):
                dve.wait_ge(masked_done, PAIRS * n + p + 1)
                nc.vector.tensor_reduce(neg_max[:, p % 2, :], masked[:, p % 2, :, :], AX_X, ALU.max,
                                        negate=True).then_inc(max_done, 1)

            def inverse_total(n, p):
                dve.wait_ge(exp_done, PAIRS * n + p + 1)
                positive(dve, norm_done, PAIRS * n + p - 1)
                nc.vector.reciprocal(inv_total[:, p % 2, :], total[:, p % 2, :]).then_inc(recip_done, 1)

            def split_o(n, p):
                dve.wait_ge(o_hi_done, PAIRS * n + p + 1)
                nc.vector.tensor_tensor(o_lo[:, p % 2, :], o_bank[:, (p % 2) * ROWS:(p % 2 + 1) * ROWS],
                                        o_hi[:, p % 2, :].bitcast(F32), ALU.subtract).then_inc(o_lo_done, 1)

            def residual(n):
                dve.wait_ge(out_done, n + 1)
                nc.vector.tensor_tensor(h_all[:, tiles(n), :], out_bank[:, :].rearrange("p (t c) -> p t c", t=TT),
                                        h_all[:, tiles(n), :], ALU.add).then_inc(resid_done, 1)

            def last_body(n):
                for p in range(PAIRS):
                    if p:
                        split_o(n, p - 1)
                    if p < PAIRS - 2:
                        mask_scores(n, p + 2)
                        row_max(n, p + 2)
                    if p < PAIRS - 1:
                        inverse_total(n, p + 1)
                    if p == 0:
                        residual(n - 1)
                    if 3 <= p:
                        low_part(dve, 2 * (p - 3))
                        low_part(dve, 2 * (p - 3) + 1)
                    if p == 3:
                        nc.vector.tensor_tensor(sim_sq[:, :, :], sim_t[:, :, :], sim_t[:, :, :], ALU.mult)\
                            .then_inc(sim_squared, 1)
                        for step in range(3):
                            m_statistics(dve, 0, step)
                    if p == 4:
                        dve.wait_ge(gate_exp, 1)
                        nc.vector.tensor_scalar(gate_t[:, :], gate_t[:, :], 1.0, None, ALU.add)\
                            .then_inc(setup_step, 1)
                        for step in range(3):
                            m_layer_norm(dve, 0, step)
                    if p == 5:
                        dve.wait_ge(setup_step, 1)
                        nc.vector.reciprocal(gate_t[:, :], gate_t[:, :]).then_inc(setup_step, 1)
                        dve.wait_ge(sim_summed_ps, 1)
                        nc.vector.tensor_scalar(sim_sq[:, 1, :], down_bank[0][:, 0:EXPERTS], 1e-24, None, ALU.max)\
                            .then_inc(sim_summed, 1)
                dve.wait_ge(sim_root, 1)
                nc.vector.tensor_tensor(sim_t[:, :, :], sim_t[:, :, :],
                                        sim_sq[:, 0:1, :].to_broadcast([P, CT, EXPERTS]),
                                        ALU.mult).then_inc(sim_ready, 1)
                m_split_x_low(dve, 0, 0)
                m_split_x_low(dve, 0, 1)
                split_o(n, PAIRS - 1)
                dve.wait_ge(setup_step, 2)
                for piece in range(6):
                    router(dve, 0, piece)
                residual(n)

            nc.vector.memset(gray[:, :, 0:1], 0.0)
            nc.vector.memset(gray[:, :, COLS + 1:COLS + 2], 0.0)
            nc.vector.memset(edge_taps[:, :], 0.0)
            nc.vector.memset(halo[:, :, :].bitcast(F32), 0.0).then_inc(borders_zero, 1)
            dve.wait_ge(row_loaded, 32)
            for f in range(2):
                for dy in range(3):
                    if dy:
                        dve.wait_ge(band_part, 2 * f + dy)
                    for dx in range(3):
                        tap = taps[:, f, dy, dx:dx + 1]
                        if dy == 0:
                            last = nc.vector.tensor_scalar(band[:, f, dx, :], row_t[:, 0, :], tap, None, ALU.mult)
                        else:
                            last = nc.vector.scalar_tensor_tensor(
                                out=band[:, f, dx, :], in0=row_t[:, dy, :], scalar=tap, in1=band[:, f, dx, :],
                                op0=ALU.mult, op1=ALU.add)
                    last.then_inc(band_part if dy < 2 else band_ready, 1)
                    if f == 1 and dy == 0:
                        gray_green(0)
                    if f == 1 and dy == 1:
                        gray_blue(0)
            for f in range(2):
                dve.wait_ge(band_hi_done, f + 1)
                nc.vector.tensor_tensor(band_lo[:, f, :, :], band[:, f, :, :], band_hi[:, f, :, :].bitcast(F32),
                                        ALU.subtract).then_inc(band_lo_done, 1)
                if f == 0:
                    gray_low(0)
            dve.wait_ge(taps_loaded, 16 * TAPS)
            for f in range(2):
                last = nc.vector.tensor_scalar(edge_band[:, f, :], edge_t[:, :], edge_taps[:, f:f + 1], None, ALU.mult)
            last.then_inc(edge_part, 1)
            dve.wait_ge(edge_part, 1)
            nc.vector.tensor_copy(edge_high[:, :, :], edge_band[:, :, :]).then_inc(edge_part, 1)
            dve.wait_ge(edge_part, 2)
            low = HALO_AT[2]
            nc.vector.tensor_copy(edge_stack[0:low, :, :], edge_high[0:low, :, :].bitcast(F32))
            nc.vector.tensor_tensor(edge_stack[low:, :, :], edge_band[low:, :, :],
                                    edge_high[low:, :, :].bitcast(F32), ALU.subtract).then_inc(edge_part, 1)
            for n in range(CHUNKS):
                dve.wait_ge(w_hi_ready, n + 1)
                _, slot, hi, lo = raw_chunk(n)
                nc.vector.tensor_tensor(lo, slot, hi.bitcast(F32), ALU.subtract).then_inc(w_lo_ready, 1)
                if n == 2:
                    layer_stats(0)
                    layer_moments(0)
                    gray_green(1)
                    layer_norm(0)
                    gray_blue(1)
                if n == 4:
                    split_x(0)
                if n == 5:
                    gray_low(1)
                if n == 8:
                    dve.wait_ge(const_loaded, 16 * CONSTS)
                    rotate(0, 0, 0)
                if n == 9:
                    rotate(0, 0, 1)
            for g in range(1, GROUPS):
                rotate(0, g, 0)
                if g == 2:
                    layer_stats(1)
                    layer_moments(1)
                rotate(0, g, 1)
                if g == 2:
                    layer_norm(1)
            mask_scores(0, 0)
            row_max(0, 0)
            split_x(1)
            mask_scores(0, 1)
            row_max(0, 1)
            gray_green(2)
            inverse_total(0, 0)
            gray_blue(2)

            def body(n, edges, load):
                for p in range(PAIRS):
                    if p:
                        split_o(n, p - 1)
                        mask_scores(n, p + 1)
                        row_max(n, p + 1)
                    if p == 1 and not (isinstance(n, int) and n == 0):
                        residual(n - 1)
                    rotate(n + 1, p // 2, p % 2)
                    if edges and p == PAIRS - 1:
                        split_x(n + 2)
                    if edges and p == 0:
                        gray_low(n + 2)
                    if load and p == PAIRS - 1:
                        gray_blue(n + 3)
                    inverse_total(n, p + 1)
                    if load and p == 6:
                        gray_green(n + 3)
                    if edges and p == 3:
                        layer_stats(n + 2)
                    if edges and p == 4:
                        layer_moments(n + 2)
                    if edges and p == 5:
                        layer_norm(n + 2)
                mask_scores(n, PAIRS + 1)
                split_o(n, PAIRS - 1)
                row_max(n, PAIRS + 1)
            bodies_a(dve, body, last_body)

        @block.tensor
        def _(pe):
            def convolve(f, values_before):
                pe.wait_ge(gray_lo_done, f + 1)
                positive(pe, x_lo_done, f)
                for which in range(2):
                    dst = (v_bank, misc_bank)[which]
                    if which == 0:
                        positive(pe, v_evac, values_before)
                    if isinstance(f, int) and f == 0:
                        pe.wait_ge(band_lo_done, which + 1)
                    for dx in range(3):
                        for w, g in ((band_hi, gray_hi), (band_hi, gray_lo), (band_lo, gray_hi)):
                            nc.tensor.matmul(dst[:, :], w[:, which, dx, :], g[:, :, dx:dx + COLS],
                                             start=(dx == 0 and w is band_hi and g is gray_hi), stop=False)
                if isinstance(f, int) and f == 0:
                    pe.wait_ge(edge_part, 3)
                pe.wait_ge(halo_loaded, 16 * HALO_DMAS * (f + 1))
                for which in range(2):
                    nc.tensor.matmul((v_bank, misc_bank)[which][:, :], edge_stack[:, which, :], halo[:, :, :],
                                     start=False, stop=True).then_inc(conv_done, 1)

            def transpose_x(f):
                pe.wait_ge(xn_done, f + 1)
                for ct in range(CT):
                    for t in range(TT):
                        last = nc.tensor.transpose(misc_bank[:, ct * ROWS + t * P:ct * ROWS + (t + 1) * P],
                                                   xn[:, t, ct * P:(ct + 1) * P], ident[:, :])
                last.then_inc(xt_done, 1)

            def three_passes(dst, stationary, moving, terms, **flags):
                passes = [(s, m) for k in range(terms) for s, m in ((0, 0), (0, 1), (1, 0))]
                for i, (s, m) in enumerate(passes):
                    k = i // 3
                    last = nc.tensor.matmul(dst, stationary[s](k), moving[m](k),
                                            start=(i == 0), stop=(i == len(passes) - 1), **flags)
                return last

            def project_qk(m, g, which):
                if g == 0 and which == 0:
                    pe.wait_ge(x_lo_done, m + 1)
                dst = (q_bank, k_bank)[which]
                positive(pe, rope_mul, 2 * (GROUPS * m + g) + which - 1)
                for half in range(2):
                    at = (2 * which + half) * P
                    last = three_passes(
                        dst[:, half * ROWS:(half + 1) * ROWS],
                        [lambda k, w=w: w[:, k, g, at:at + P] for w in (w_hi, w_lo)],
                        [lambda k, t=t: t[:, k, :] for t in (x_hi, x_lo)], CT)
                last.then_inc(qk_done, 1)

            def project_v(m, g, t, edges):
                if t == 0:
                    positive(pe, v_evac, GROUPS * m + g)
                    if edges:
                        pe.wait_ge(abs_done, 2 * (m + 1) + 1)
                at = 4 * P
                last = three_passes(
                    v_bank[:, t * COLS:(t + 1) * COLS],
                    [lambda k, s=s: s[:, k, t * P:(t + 1) * P] for s in (x_hi, x_lo)],
                    [lambda k, w=w: w[:, k, g, at:at + 4 * HEAD_DIM] for w in (w_hi, w_lo)], CT)
                if t == TT - 1:
                    last.then_inc(v_done, 1)

            def scores(n, p):
                pair = p % PAIRS
                for b in range(BLOCKS):
                    for head in range(2):
                        rows = slice(HEAD_DIM * head, HEAD_DIM * (head + 1))
                        if b % 2 or b == 0:
                            first = key_of(b, 0)
                            keys = qk[rows, pair, 1, first:first + KEYS]
                        else:
                            own = qk[rows, pair, 1, WINDOW * b:WINDOW * (b + 1)]
                            keys = bass.AP(tensor=own.tensor, offset=own.offset,
                                           ap=[list(own.ap[0]), [-WINDOW, 2], [1, WINDOW]])
                        last = nc.tensor.matmul(scores_bank_of(n, p)[rows, b * KEYS:(b + 1) * KEYS],
                                                qk[rows, pair, 0, WINDOW * b:WINDOW * (b + 1)], keys,
                                                start=True, stop=True)
                last.then_inc(s_done, 1)

            def in_place(n, g):
                pe.wait_ge(moved[g], 16 * MOVES * (n + 1))

            def transpose_p(n, p):
                pe.wait_ge(norm_done, PAIRS * n + p + 1)
                for b in range(BLOCKS):
                    last = nc.tensor.transpose(scores_bank_of(n, p)[:, b * P:(b + 1) * P], prob[:, p % 2, b, :],
                                               ident[:, :])
                last.then_inc(t_done, 1)

            def attend(n, p):
                g = p // 2
                if p % 2 == 0:
                    pe.wait_ge(v_evac, GROUPS * n + g + 1)
                    pe.wait_ge(v_crossed[g], 32 * (n + 1))
                positive(pe, o_lo_done, PAIRS * n + p)
                pe.wait_ge(pt_evac, PAIRS * n + p + 1)
                for b in range(BLOCKS):
                    for head in range(2):
                        at = HEAD_DIM * (2 * (p % 2) + head)
                        vals = v_cross[:, g, at:at + HEAD_DIM] if b == 2 else v[:, g, b // 2, at:at + HEAD_DIM]
                        to = (p % 2) * ROWS + WINDOW * b
                        last = nc.tensor.matmul(
                            o_bank[HEAD_DIM * head:HEAD_DIM * (head + 1), to:to + WINDOW], vals,
                            prob_t[:, p % 2, b, HEAD_DIM * head:HEAD_DIM * (head + 1)], start=True, stop=True)
                last.then_inc(o_done, 1)

            def project_out(n, p):
                pe.wait_ge(o_lo_done, PAIRS * n + p + 1)
                if p == 0:
                    positive(pe, resid_done, n)
                for t in range(TT):
                    for s, w in ((o_hi, wo_hi), (o_hi, wo_lo), (o_lo, wo_hi)):
                        first = p == 0 and t == 0 and w is wo_hi and s is o_hi
                        last = nc.tensor.matmul(out_bank[:, t * COLS:(t + 1) * COLS],
                                                s[:, p % 2, t * P:(t + 1) * P], w[:, p, :],
                                                start=first, stop=(p == PAIRS - 1), skip_group_check=True)
                if p == PAIRS - 1:
                    last.then_inc(out_done, 1)

            convolve(0, 0)
            pe.wait_ge(ident_loaded, 16)
            transpose_x(0)
            for g in range(GROUPS):
                pe.wait_ge(w_lo_ready, CT * (g + 1))
                if g == GROUPS - 1:
                    in_place(0, 0)
                project_qk(0, g, 0)
                project_qk(0, g, 1)
                if g == GROUPS - 1:
                    scores(0, 0)
                if g == 0:
                    pe.wait_ge(abs_done, 1)
                for t in range(TT):
                    project_v(0, g, t, g == 2)
                if g == 1:
                    convolve(1, 2)
            pe.wait_ge(w_lo_ready, CHUNKS)
            transpose_x(1)
            scores(0, 1)

            def finish_out(n):
                if not (isinstance(n, int) and n == 0):
                    project_out(n - 1, PAIRS - 1)

            def last_body(n):
                pe.wait_ge(rope_mul, 2 * GROUPS * IMAGES)
                for p in range(PAIRS):
                    if p < PAIRS - 2:
                        scores(n, p + 2)
                    if p % 2 and (p + 3) // 2 < GROUPS:
                        in_place(n, (p + 3) // 2)
                    transpose_p(n, p)
                    if p:
                        project_out(n, p - 1)
                    else:
                        finish_out(n)
                    if p == 5:
                        m_transpose_x(pe, 0)
                    if p == 4:
                        pe.wait_ge(sim_squared, 1)
                        pe.wait_ge(ones_set, 1)
                        pe.wait_ge(v_evac, GROUPS * IMAGES)
                        for ct in range(CT):
                            last = nc.tensor.matmul(down_bank[0][:, 0:EXPERTS], ones[:, :], sim_sq[:, ct, :],
                                                    start=(ct == 0), stop=(ct == CT - 1))
                        last.then_inc(sim_summed_ps, 1)
                    attend(n, p)
                logits(pe, 0)
                project_out(n, PAIRS - 1)

            def body(n, edges, load):
                for p in range(PAIRS):
                    g, part = p // 2, p % 2
                    if p:
                        scores(n, p + 1)
                    if edges and p == 2:
                        convolve(n + 2, GROUPS * (n + 1) + g)
                    project_qk(n + 1, g, part)
                    if part == 0:
                        in_place(n + (g + 1) // GROUPS, (g + 1) % GROUPS)
                        if g == GROUPS - 1 and not edges:
                            in_place(n + 1, 1)
                    transpose_p(n, p)
                    project_v(n + 1, g, part, edges and p == 2)
                    if p:
                        project_out(n, p - 1)
                    else:
                        finish_out(n)
                    if edges and p == PAIRS - 2:
                        transpose_x(n + 2)
                    attend(n, p)
                scores(n, PAIRS + 1)
            bodies_a(pe, body, last_body)



        @block.gpsimd
        def _(pool):
            m_rstd_root(pool, 1)
            m_norm_root(pool, 1)

            def body(b, project, front):
                if front:
                    m_rstd_root(pool, b + 2)
                    m_norm_root(pool, b + 2)
                positive(pool, stored, 16 * b)
                pool.wait_ge(down_step, 2 * DOWNS * (b + 1))
                nc.gpsimd.tensor_tensor(result[:, :, :], out_part[:, 0, :, :], out_part[:, 1, :, :],
                                        ALU.add).then_inc(summed, 1)
                pool.wait_ge(summed, b + 1)
                pool.dma_start(out[b].rearrange("(t p) c -> p t c", p=P), result[:, :, :]).then_inc(stored, 16)
            bodies(pool, body)
            pool.wait_ge(stored, 16 * IMAGES)

        @block.scalar
        def _(act):
            def router_exponent(f):
                act.wait_ge(router_in, f + 1)
                nc.scalar.activation(active[:, :, :], gated[:, :, :], ACT.Exp).then_inc(router_exp, 1)

            act.wait_ge(resid_done, IMAGES)
            router_exponent(0)
            for n in range(EARLY, EXPERTS):
                high_part(act, n)
            evacuate_x(act, 1)
            router_exponent(1)
            m_split_x_high(act, 1, 0)
            m_split_x_high(act, 1, 1)
            for n in range(EXPERTS, M_CHUNKS - 2):
                high_part(act, n)
            act.wait_ge(m_lo_ready, EXPERTS)

            def body(b, project, front):
                act.wait_ge(qk_turned, b + 1)
                positive(act, m_scores, b)
                nc.scalar.activation(qkt[:, :, :], turn_bank[:, :].rearrange("p (a c) -> p a c", a=2),
                                     ACT.Copy).then_inc(qkt_done, 1)
                act.wait_ge(m_bias_done, b + 1)
                positive(act, m_turned, b)
                for t in range(TT):
                    last = nc.scalar.activation(m_prob[:, t, :], attn_bank[:, t * ROWS:(t + 1) * ROWS], ACT.Exp,
                                                bias=m_bias[:, 1, t:t + 1], scale=SCORE_SCALE,
                                                accum_out=m_total[:, t:t + 1])
                last.then_inc(m_exp, 1)
                if isinstance(b, int) and b == 0:
                    for n in range(M_CHUNKS - 2, M_CHUNKS):
                        high_part(act, n)
                act.wait_ge(m_turned, b + 1)
                nc.scalar.activation(m_prob_t[:, :, :], attn_bank[:, :].rearrange("p (a c) -> p a c", a=TT),
                                     ACT.Copy).then_inc(m_prob_t_done, 1)
                if front:
                    evacuate_x(act, b + 2)
                act.wait_ge(mixed, b + 1)
                positive(act, down_done, DOWNS * b)
                nc.scalar.activation(mo_t_hi[:, :], attn_bank[:, 0:ROWS], ACT.Copy).then_inc(mo_hi_done, 1)
                if front:
                    router_exponent(b + 2)
                    m_split_x_high(act, b + 2, 0)
                    m_split_x_high(act, b + 2, 1)
            bodies(act, body)

        @block.vector
        def _(dve):
            def shift_shares(f):
                dve.wait_ge(share_step, 3 * f + 3)
                positive(dve, combined, STEPS * f)
                if not (isinstance(f, int) and f == 0):
                    nc.vector.tensor_copy(share[:, 0, :, :], share[:, 1, :, :]).then_inc(shifted, 1)
                    dve.wait_ge(shifted, 2 * f)
                nc.vector.tensor_copy(share[:, 1, :, :], share[:, 2, :, :]).then_inc(shifted, 1)
                dve.wait_ge(shifted, 2 * f + 1)

            def combine(m, k):
                e, t = k // TT, k % TT
                done = STEPS * m + k
                dve.wait_ge(step_done, done + 1)
                src = chunk_bank[k % 4][:, 0:EXPERT_COLS]
                by = share[:, 1, t, e:e + 1]
                if e == 0:
                    nc.vector.tensor_scalar(part[:, t, :], src, by, None, ALU.mult).then_inc(combined, 1)
                    return
                dve.wait_ge(combined, done - 1)
                if e == EXPERTS - 1:
                    positive(dve, mixed, m)
                nc.vector.scalar_tensor_tensor(out=(qkv if e == EXPERTS - 1 else part)[:, t, :], in0=src, scalar=by,
                                               in1=part[:, t, :], op0=ALU.mult, op1=ALU.add).then_inc(combined, 1)

            def attention_max(b):
                dve.wait_ge(m_scores, b + 1)
                nc.vector.tensor_reduce(m_bias[:, 0, :], attn_bank[:, :].rearrange("p (t c) -> p t c", t=TT), AX_X,
                                        ALU.max, negate=True).then_inc(m_max, 1)
                dve.wait_ge(m_max, b + 1)
                nc.vector.tensor_scalar(m_bias[:, 1, :], m_bias[:, 0, :], SCORE_SCALE, None, ALU.mult)\
                    .then_inc(m_bias_done, 1)

            def normalise_shares(b):
                dve.wait_ge(m_exp, b + 1)
                nc.vector.reciprocal(m_inv[:, :], m_total[:, :]).then_inc(m_inv_done, 1)
                dve.wait_ge(m_inv_done, b + 1)
                nc.vector.tensor_tensor(share_n[:, :, :], share[:, 0, :, :],
                                        m_inv[:, :].unsqueeze(2).to_broadcast([P, TT, EXPERTS]),
                                        ALU.mult).then_inc(share_n_done, 1)

            def split_mixed(b):
                dve.wait_ge(mo_hi_done, b + 1)
                nc.vector.tensor_tensor(mo_t_lo[:, :], attn_bank[:, 0:ROWS], mo_t_hi[:, :].bitcast(F32),
                                        ALU.subtract).then_inc(mo_lo_done, 1)

            def add_down(b, j):
                t = j % TT
                dve.wait_ge(down_done, DOWNS * b + j + 1)
                if j == 0:
                    dve.wait_ge(share_n_done, b + 1)
                if j < TT:
                    positive(dve, summed, b)
                else:
                    dve.wait_ge(down_step, 2 * DOWNS * b + 2 * (j - TT + 1))
                for i in range(2):
                    e = 2 * (j // TT) + i
                    src = down_bank[j % 2][:, i * COLS:(i + 1) * COLS].unsqueeze(1)
                    if e == 1:
                        ins = nc.vector.tensor_scalar(out_part[:, 1, t:t + 1, :], src, share_n[:, t, e:e + 1], None,
                                                      ALU.mult)
                    else:
                        before = h_all[:, bass.ds(b * TT + t, 1), :] if e == 0 else out_part[:, i, t:t + 1, :]
                        ins = nc.vector.scalar_tensor_tensor(out=out_part[:, i, t:t + 1, :], in0=src,
                                                             scalar=share_n[:, t, e:e + 1], in1=before,
                                                             op0=ALU.mult, op1=ALU.add)
                    ins.then_inc(down_step, 1)

            for piece in range(6, ROUTER_PIECES):
                router(dve, 0, piece)
            shift_shares(0)
            for k in range(STEPS):
                combine(0, k)
                if k % 2 == 0 and k < 2 * (EXPERTS - EARLY):
                    low_part(dve, EARLY + k // 2)
                if k in (1, 3, 5):
                    m_statistics(dve, 1, k // 2)
                if k in (7, 9, 11):
                    m_layer_norm(dve, 1, k // 2 - 3)
                if 15 <= k < 26:
                    router(dve, 1, k - 15)
                if 27 <= k < 30:
                    router(dve, 1, k - 16)
                if k == STEPS - 2:
                    m_split_x_low(dve, 1, 0)
            m_split_x_low(dve, 1, 1)
            shift_shares(1)

            def body(b, project, front):
                for k in range(STEPS):
                    if front and k == STEPS - 1:
                        m_split_x_low(dve, b + 2, 0)
                    if 13 <= k < 27:
                        add_down(b, k - 13)
                    if project:
                        combine(b + 1, k)
                    if isinstance(b, int) and b == 0 and k in (1, 2, 8, 9):
                        low_part(dve, EXPERTS + (1, 2, 8, 9).index(k))
                    if k == 4:
                        attention_max(b)
                    if k == 7:
                        normalise_shares(b)
                    if k == 10:
                        split_mixed(b)
                    if front:
                        if k < 3:
                            m_statistics(dve, b + 2, k)
                        if k in (5, 6, 8):
                            m_layer_norm(dve, b + 2, (5, 6, 8).index(k))
                        if 13 <= k < 24:
                            router(dve, b + 2, k - 13)
                        if 26 <= k < 29:
                            router(dve, b + 2, k - 15)
                if front:
                    m_split_x_low(dve, b + 2, 1)
                    shift_shares(b + 2)
                elif project:
                    nc.vector.tensor_copy(share[:, 0, :, :], share[:, 1, :, :]).then_inc(shifted, 1)
                    dve.wait_ge(shifted, 2 * (b + 2))
                for j in range(DOWNS - 2, DOWNS):
                    add_down(b, j)
            bodies(dve, body)

        @block.tensor
        def _(pe):
            def expert_step(m, k):
                e, t = k // TT, k % TT
                if k < TT:
                    pe.wait_ge(mx_lo_done, TT * m + k + 1)
                positive(pe, combined, STEPS * m + k - 3)
                if isinstance(m, int) and m == 0 and t == 0:
                    pe.wait_ge(m_lo_ready, e + 1)
                dst = chunk_bank[k % 4][:, 0:EXPERT_COLS]
                n = 0
                for ct in range(CT):
                    for s, w in ((mx_hi, me_hi), (mx_hi, me_lo), (mx_lo, me_hi)):
                        last = nc.tensor.matmul(dst, s[:, ct, t * P:(t + 1) * P], w[:, e, ct, :],
                                                start=(n == 0), stop=(n == 3 * CT - 1))
                        n += 1
                last.then_inc(step_done, 1)

            def transpose_qk(b):
                pe.wait_ge(combined, STEPS * (b + 1))
                positive(pe, logits_read, b + 2 if not isinstance(b, int) else min(b + 2, IMAGES))
                for which in range(2):
                    for t in range(TT):
                        last = nc.tensor.transpose(turn_bank[:, which * ROWS + t * P:which * ROWS + (t + 1) * P],
                                                   qkv[:, t, which * P:(which + 1) * P], ident[:, :])
                last.then_inc(qk_turned, 1)

            def token_scores(b):
                pe.wait_ge(qkt_done, b + 1)
                positive(pe, mo_lo_done, b)
                for t in range(TT):
                    last = nc.tensor.matmul(attn_bank[:, t * ROWS:(t + 1) * ROWS], qkt[:, 0, t * P:(t + 1) * P],
                                            qkt[:, 1, :], start=True, stop=True)
                last.then_inc(m_scores, 1)

            def transpose_prob(b):
                pe.wait_ge(m_exp, b + 1)
                for kt in range(TT):
                    for t in range(TT):
                        last = nc.tensor.transpose(attn_bank[:, kt * ROWS + t * P:kt * ROWS + (t + 1) * P],
                                                   m_prob[:, t, kt * P:(kt + 1) * P], ident[:, :])
                last.then_inc(m_turned, 1)

            def mix_values(b):
                pe.wait_ge(m_prob_t_done, b + 1)
                for kt in range(TT):
                    last = nc.tensor.matmul(attn_bank[:, 0:ROWS], qkv[:, kt, 2 * EXPERT_DIM:EXPERT_COLS],
                                            m_prob_t[:, kt, :], start=(kt == 0), stop=(kt == TT - 1))
                last.then_inc(mixed, 1)

            def down_step_pair(b, j):
                e, t = 2 * (j // TT), j % TT
                if j == 0:
                    pe.wait_ge(mo_lo_done, b + 1)
                    if isinstance(b, int) and b == 0:
                        pe.wait_ge(m_lo_ready, M_CHUNKS)
                positive(pe, down_step, 2 * DOWNS * b + 2 * j - 2)
                for i, (s, w) in enumerate(((mo_t_hi, mo_hi), (mo_t_hi, mo_lo), (mo_t_lo, mo_hi))):
                    last = nc.tensor.matmul(down_bank[j % 2][:, :], s[:, t * P:(t + 1) * P], w[:, e:e + 2, :],
                                            start=(i == 0), stop=(i == 2))
                last.then_inc(down_done, 1)

            for k in range(STEPS):
                expert_step(0, k)
                if k == 10:
                    m_transpose_x(pe, 1)
                if k == 13:
                    logits(pe, 1)

            def body(b, project, front):
                for k in range(STEPS):
                    if project:
                        expert_step(b + 1, k)
                    if k == 1:
                        transpose_qk(b)
                    if k == 3:
                        token_scores(b)
                    if k == 7:
                        transpose_prob(b)
                    if k == 9:
                        mix_values(b)
                    if front and k == 8:
                        m_transpose_x(pe, b + 2)
                    if front and k == 11:
                        logits(pe, b + 2)
                    if 12 <= k < 26:
                        down_step_pair(b, k - 12)
                for j in range(DOWNS - 2, DOWNS):
                    down_step_pair(b, j)
            bodies(pe, body)


def layouts(x, scharr, w_qkv, w_out, sim, gates, q_proj, k_proj, v_proj, o_proj):
    inner = HEADS * HEAD_DIM
    halves = [w_qkv[k * inner:(k + 1) * inner].reshape(GROUPS, 4, 2, HALF, COLS).transpose(4, 0, 2, 1, 3)
              .reshape(COLS, GROUPS, 4 * HEAD_DIM) for k in range(2)]
    values = w_qkv[2 * inner:].reshape(GROUPS, 4 * HEAD_DIM, COLS).transpose(2, 0, 1)
    experts = np.concatenate([q_proj, k_proj, v_proj], axis=2)
    return {
        "x": x,
        "scharr": scharr,
        "scharr_last": np.ascontiguousarray(scharr[:, 0].transpose(1, 2, 0)),
        "w_qkv": np.ascontiguousarray(np.concatenate(halves + [values], axis=2)),
        "w_out": np.ascontiguousarray(w_out.T),
        "sim": sim,
        "gates": gates,
        "w_moe": np.ascontiguousarray(experts.reshape(EXPERTS, CT, P, EXPERT_COLS).transpose(2, 0, 1, 3)),
        "w_moe_out": np.ascontiguousarray(o_proj.transpose(1, 0, 2)),
    }


def kernel(x, L0_tok_scharr, L0_attn_w_qkv, L0_attn_w_out, L0_ffn_sim_matrix, L0_ffn_gates, L0_ffn_q_proj,
           L0_ffn_k_proj, L0_ffn_v_proj, L0_ffn_o_proj):
    import concourse.bacc as bacc
    from concourse.bass_utils import run_bass_kernel_spmd

    given = [np.asarray(a) for a in (x, L0_tok_scharr, L0_attn_w_qkv, L0_attn_w_out, L0_ffn_sim_matrix, L0_ffn_gates,
                                     L0_ffn_q_proj, L0_ffn_k_proj, L0_ffn_v_proj, L0_ffn_o_proj)]
    arrays = {**layouts(*given), **shape_constants()}
    nc = bacc.Bacc("TRN2", target_bir_lowering=False, num_devices=1)
    args = {name: nc.dram_tensor(f"in_{name}", a.shape, mybir.dt.from_np(a.dtype), kind="ExternalInput").ap()
            for name, a in arrays.items()}
    out = nc.dram_tensor("out", (IMAGES, ROWS, COLS), F32, kind="ExternalOutput").ap()
    build(nc, **args, out=out)
    ran = run_bass_kernel_spmd(nc, [{f"in_{name}": np.ascontiguousarray(a) for name, a in arrays.items()}],
                               core_ids=[0])
    return ran.results[0]["out"]
```
